# Optimizing a Trainium2 kernel written in Bass

```python
import numpy as np
import jax
import jax.numpy as jnp

def _softmax(x, axis=-1):
    return jax.nn.softmax(x, axis=axis)

def _gelu(x):
    return jax.nn.gelu(x, approximate=True)

def _silu(x):
    return jax.nn.silu(x)

def _sigmoid(x):
    return jax.nn.sigmoid(x)

def _layernorm(x, axis=-1, eps=1e-05):
    m = jnp.mean(x, axis=axis, keepdims=True)
    v = jnp.var(x, axis=axis, keepdims=True)
    return (x - m) / jnp.sqrt(v + eps)

def _scatter_add(tgt, idx, src, axis=0):
    return tgt.at[idx].add(src)

def _segment_sum(src, seg, n):
    return jax.ops.segment_sum(src, seg, n)
kernel_name = 'mk_flamingo_gated_d2_seqx_r4_3aef64'

def setup_inputs(seed: int=0):
    np.random.seed(seed)
    _w = jnp.asarray

    def _rec_inputs():
        import jax
        import jax.numpy as jnp
        _rk = jax.random.key(seed)
        x = -0.0002928 + 1 * jax.random.normal(jax.random.fold_in(_rk, 1), (32, 256, 256), jnp.float32)
        _lenS = 256 - jax.random.randint(jax.random.fold_in(_rk, 7), (32,), 0, max(1, 256 // 4) + 1, jnp.int32)
        _lenS2 = 120 - jax.random.randint(jax.random.fold_in(_rk, 8), (32,), 0, max(1, 120 // 4) + 1, jnp.int32)
        _ctx_1024P = jax.random.normal(jax.random.fold_in(_rk, 11), (32, 16, 256), jnp.float32)
        _ctx_1024c = jax.random.dirichlet(jax.random.fold_in(_rk, 511), 0.3 * jnp.ones((16,), jnp.float32), (32, 120))
        _ctx_1024t = jnp.einsum('bsk,bkd->bsd', _ctx_1024c, _ctx_1024P)
        _ctx_1024t = _ctx_1024t * jax.lax.rsqrt(jnp.mean(jnp.square(_ctx_1024t)) + 1e-12) * 0.953939
        ctx_1024 = -1.39393e-06 + 0.999914 * (_ctx_1024t + 0.3 * jax.random.normal(jax.random.fold_in(_rk, 611), (32, 120, 256), jnp.float32))
        fside_BxSxS2_0 = jax.random.uniform(jax.random.fold_in(_rk, 13), (32, 256, 120), jnp.float32, 0.0, 1)
        _validS = jnp.arange(256)[None, :] < _lenS[:, None]
        _validS2 = jnp.arange(120)[None, :] < _lenS2[:, None]
        _causal = jnp.tril(jnp.ones((256, 256), dtype=bool))
        mask_Bx1xSxS2_ik1 = jnp.where(jnp.broadcast_to(_validS2[:, None, None, :], (32, 1, 256, 120)), 1, 0).astype(jnp.int32)
        mask_BxSxS2_ik1 = jnp.where(jnp.broadcast_to(_validS2[:, None, :], (32, 256, 120)), 1, 0).astype(jnp.int32)
        _g = jax.random.normal(jax.random.fold_in(_rk, 9001), (2, 2), jnp.float32)
        _g = jnp.sign(_g) * jnp.maximum(jnp.abs(_g), 1.0) + (_g == 0) * 1.0
        g_xattn = _g[0]
        g_ffn = _g[1]
        return (x, ctx_1024, fside_BxSxS2_0, mask_Bx1xSxS2_ik1, mask_BxSxS2_ik1, g_xattn, g_ffn)
    x, ctx_1024, fside_BxSxS2_0, mask_Bx1xSxS2_ik1, mask_BxSxS2_ik1, g_xattn, g_ffn = _rec_inputs()

    def _L0_xattn_setup():
        import jax, jax.numpy as jnp
        import numpy as np
        DIM = 256
        HEADS = 16
        HEAD_DIM = DIM // HEADS
        key = jax.random.key(seed)
        ks = jax.random.split(key, 12)
        B, Tq, Tk = (2, 512, 512)
        inp = {'query': jax.random.normal(ks[0], (B, Tq, DIM), jnp.float32), 'key': jax.random.normal(ks[1], (B, Tk, DIM), jnp.float32), 'value': jax.random.normal(ks[2], (B, Tk, DIM), jnp.float32), 'mask': jax.random.randint(ks[3], (B, 1, Tq, Tk), 0, 2, jnp.int32), 'wq': jax.random.uniform(ks[4], (DIM, DIM), jnp.float32, -1.0, 1.0) * np.sqrt(6.0 / (2 * DIM)), 'wk': jax.random.uniform(ks[5], (DIM, DIM), jnp.float32, -1.0, 1.0) * np.sqrt(6.0 / (2 * DIM)), 'wv': jax.random.uniform(ks[6], (DIM, DIM), jnp.float32, -1.0, 1.0) * np.sqrt(6.0 / (2 * DIM)), 'wo': jax.random.uniform(ks[7], (DIM, DIM), jnp.float32, -1.0, 1.0) * np.sqrt(6.0 / (2 * DIM)), 'bq': jnp.zeros((DIM,), jnp.float32), 'bk': jnp.zeros((DIM,), jnp.float32), 'bv': jnp.zeros((DIM,), jnp.float32), 'bo': jnp.zeros((DIM,), jnp.float32)}
        return inp
    _L0_xattn_all = _L0_xattn_setup()
    _L0_xattn_in = {k: v for k, v in _L0_xattn_all.items() if k in ('wq', 'wk', 'wv', 'wo', 'bq', 'bk', 'bv', 'bo')}
    del _L0_xattn_all

    def _L0_ffn_setup():
        import jax, jax.numpy as jnp
        import numpy as np
        from jax import lax
        T, B, I, M, O = (64, 64, 256, 256, 256)

        def _xavier(key, shape):
            fan_out, fan_in = shape
            limit = float(np.sqrt(6.0 / (fan_in + fan_out)))
            return jax.random.uniform(key, shape, jnp.float32, -limit, limit)
        key = jax.random.key(seed)
        ks = jax.random.split(key, 9)
        x = jax.random.normal(ks[0], (T, B, I), jnp.float32)
        return {'x': x, 'wf': _xavier(ks[1], (M, I)), 'uf': _xavier(ks[2], (M, M)), 'bf': jnp.zeros((M,), jnp.float32), 'wi': _xavier(ks[3], (M, I)), 'ui': _xavier(ks[4], (M, M)), 'bi': jnp.zeros((M,), jnp.float32), 'wc': _xavier(ks[5], (M, I)), 'uc': _xavier(ks[6], (M, M)), 'bc': jnp.zeros((M,), jnp.float32), 'wo': _xavier(ks[7], (O, I)), 'uo': _xavier(ks[8], (O, M)), 'bo': jnp.zeros((O,), jnp.float32), 'in_c': jnp.zeros((M,), jnp.float32)}
    _L0_ffn_all = _L0_ffn_setup()
    _L0_ffn_in = {k: v for k, v in _L0_ffn_all.items() if k in ('wf', 'uf', 'bf', 'wi', 'ui', 'bi', 'wc', 'uc', 'bc', 'wo', 'uo', 'bo', 'in_c')}
    del _L0_ffn_all

    def _L1_xattn_setup():
        import jax, jax.numpy as jnp
        import numpy as np
        NUM_HEADS = 16
        HIDDEN = 256
        B, S = (2, 512)

        def _split_heads(x, H):
            b, s, d = x.shape
            return x.reshape(b, s, H, d // H).transpose(0, 2, 1, 3)
        key = jax.random.key(seed)
        ks = jax.random.split(key, 14)
        D = HIDDEN
        scale = 1.0 / np.sqrt(D)
        inp = {'query': jax.random.normal(ks[0], (B, S, D), jnp.float32), 'key_in': jax.random.normal(ks[1], (B, S, D), jnp.float32), 'value': jax.random.normal(ks[2], (B, S, D), jnp.float32), 'group_prob': jax.random.uniform(ks[3], (B, S, S), jnp.float32), 'mask': jax.random.randint(ks[4], (B, S, S), 0, 2, jnp.int32), 'wq_k': jax.random.normal(ks[5], (D, D), jnp.float32) * scale, 'wq_b': jnp.zeros((D,), jnp.float32), 'wk_k': jax.random.normal(ks[6], (D, D), jnp.float32) * scale, 'wk_b': jnp.zeros((D,), jnp.float32), 'wv_k': jax.random.normal(ks[7], (D, D), jnp.float32) * scale, 'wv_b': jnp.zeros((D,), jnp.float32), 'wo_k': jax.random.normal(ks[8], (D, D), jnp.float32) * scale, 'wo_b': jnp.zeros((D,), jnp.float32)}
        return inp
    _L1_xattn_all = _L1_xattn_setup()
    _L1_xattn_in = {k: v for k, v in _L1_xattn_all.items() if k in ('wq_k', 'wq_b', 'wk_k', 'wk_b', 'wv_k', 'wv_b', 'wo_k', 'wo_b')}
    del _L1_xattn_all

    def _L1_ffn_setup():
        import jax, jax.numpy as jnp
        import numpy as np
        NUM_HEADS = 16
        TOP_K = 2
        key = jax.random.key(seed)
        ks = jax.random.split(key, 5)
        B, S, D, E = (4, 512, 256, 8)
        scale = 0.02
        return {'x': jax.random.normal(ks[0], (B, S, D), dtype=jnp.float32), 'W_qkv': jax.random.normal(ks[1], (D, 3 * D), dtype=jnp.float32) * scale, 'b_qkv': jnp.zeros((3 * D,), dtype=jnp.float32), 'W_gate': jax.random.normal(ks[2], (D, E), dtype=jnp.float32) * scale, 'b_gate': jnp.zeros((E,), dtype=jnp.float32), 'W_experts': jax.random.normal(ks[3], (E, D, D), dtype=jnp.float32) * scale, 'b_experts': jnp.zeros((E, D), dtype=jnp.float32)}
    _L1_ffn_all = _L1_ffn_setup()
    _L1_ffn_in = {k: v for k, v in _L1_ffn_all.items() if k in ('W_qkv', 'b_qkv', 'W_gate', 'b_gate', 'W_experts', 'b_experts')}
    del _L1_ffn_all
    return {'x': x, 'ctx_1024': ctx_1024, 'fside_BxSxS2_0': fside_BxSxS2_0, 'mask_Bx1xSxS2_ik1': mask_Bx1xSxS2_ik1, 'mask_BxSxS2_ik1': mask_BxSxS2_ik1, 'g_xattn': g_xattn, 'g_ffn': g_ffn, 'L0_xattn_wq': _L0_xattn_in['wq'], 'L0_xattn_wk': _L0_xattn_in['wk'], 'L0_xattn_wv': _L0_xattn_in['wv'], 'L0_xattn_wo': _L0_xattn_in['wo'], 'L0_xattn_bq': _L0_xattn_in['bq'], 'L0_xattn_bk': _L0_xattn_in['bk'], 'L0_xattn_bv': _L0_xattn_in['bv'], 'L0_xattn_bo': _L0_xattn_in['bo'], 'L0_ffn_wf': _L0_ffn_in['wf'], 'L0_ffn_uf': _L0_ffn_in['uf'], 'L0_ffn_bf': _L0_ffn_in['bf'], 'L0_ffn_wi': _L0_ffn_in['wi'], 'L0_ffn_ui': _L0_ffn_in['ui'], 'L0_ffn_bi': _L0_ffn_in['bi'], 'L0_ffn_wc': _L0_ffn_in['wc'], 'L0_ffn_uc': _L0_ffn_in['uc'], 'L0_ffn_bc': _L0_ffn_in['bc'], 'L0_ffn_wo': _L0_ffn_in['wo'], 'L0_ffn_uo': _L0_ffn_in['uo'], 'L0_ffn_bo': _L0_ffn_in['bo'], 'L0_ffn_in_c': _L0_ffn_in['in_c'], 'L1_xattn_wq_k': _L1_xattn_in['wq_k'], 'L1_xattn_wq_b': _L1_xattn_in['wq_b'], 'L1_xattn_wk_k': _L1_xattn_in['wk_k'], 'L1_xattn_wk_b': _L1_xattn_in['wk_b'], 'L1_xattn_wv_k': _L1_xattn_in['wv_k'], 'L1_xattn_wv_b': _L1_xattn_in['wv_b'], 'L1_xattn_wo_k': _L1_xattn_in['wo_k'], 'L1_xattn_wo_b': _L1_xattn_in['wo_b'], 'L1_ffn_W_qkv': _L1_ffn_in['W_qkv'], 'L1_ffn_b_qkv': _L1_ffn_in['b_qkv'], 'L1_ffn_W_gate': _L1_ffn_in['W_gate'], 'L1_ffn_b_gate': _L1_ffn_in['b_gate'], 'L1_ffn_W_experts': _L1_ffn_in['W_experts'], 'L1_ffn_b_experts': _L1_ffn_in['b_experts']}

def reference(x, ctx_1024, fside_BxSxS2_0, mask_Bx1xSxS2_ik1, mask_BxSxS2_ik1, g_xattn, g_ffn, L0_xattn_wq, L0_xattn_wk, L0_xattn_wv, L0_xattn_wo, L0_xattn_bq, L0_xattn_bk, L0_xattn_bv, L0_xattn_bo, L0_ffn_wf, L0_ffn_uf, L0_ffn_bf, L0_ffn_wi, L0_ffn_ui, L0_ffn_bi, L0_ffn_wc, L0_ffn_uc, L0_ffn_bc, L0_ffn_wo, L0_ffn_uo, L0_ffn_bo, L0_ffn_in_c, L1_xattn_wq_k, L1_xattn_wq_b, L1_xattn_wk_k, L1_xattn_wk_b, L1_xattn_wv_k, L1_xattn_wv_b, L1_xattn_wo_k, L1_xattn_wo_b, L1_ffn_W_qkv, L1_ffn_b_qkv, L1_ffn_W_gate, L1_ffn_b_gate, L1_ffn_W_experts, L1_ffn_b_experts):
    import jax
    import jax.numpy as jnp

    def _L0_xattn_ref(query, key, value, mask, wq, wk, wv, wo, bq, bk, bv, bo):
        import jax, jax.numpy as jnp
        import numpy as np
        DIM = 256
        HEADS = 16
        HEAD_DIM = DIM // HEADS
        B, Tq, C = query.shape
        Tk = key.shape[1]
        scale = 1.0 / np.sqrt(HEAD_DIM)
        q = (query @ wq.T + bq).reshape(B, Tq, HEADS, HEAD_DIM).transpose(0, 2, 1, 3)
        k = (key @ wk.T + bk).reshape(B, Tk, HEADS, HEAD_DIM).transpose(0, 2, 1, 3)
        v = (value @ wv.T + bv).reshape(B, Tk, HEADS, HEAD_DIM).transpose(0, 2, 1, 3)
        scores = jnp.einsum('bhqd,bhkd->bhqk', q, k) * scale
        scores = jnp.clip(scores, -100.0, 100.0)
        scores = jnp.where(mask == 0, -jnp.inf, scores)
        attn = jax.nn.softmax(scores, axis=-1)
        out = jnp.einsum('bhqk,bhkd->bhqd', attn, v)
        out = out.transpose(0, 2, 1, 3).reshape(B, Tq, HEADS * HEAD_DIM)
        return out @ wo.T + bo

    def _L0_ffn_ref(x, wf, uf, bf, wi, ui, bi, wc, uc, bc, wo, uo, bo, in_c):
        import jax, jax.numpy as jnp
        import numpy as np
        from jax import lax
        T, B, I, M, O = (64, 64, 256, 256, 256)

        def _xavier(key, shape):
            fan_out, fan_in = shape
            limit = float(np.sqrt(6.0 / (fan_in + fan_out)))
            return jax.random.uniform(key, shape, jnp.float32, -limit, limit)
        batch = x.shape[1]
        c0 = jnp.broadcast_to(in_c, (batch, in_c.shape[0]))

        def step(c, xt):
            ft = jax.nn.sigmoid(xt @ wf.T + c @ uf.T + bf)
            it = jax.nn.sigmoid(xt @ wi.T + c @ ui.T + bi)
            gt = jnp.tanh(xt @ wc.T + c @ uc.T + bc)
            c = ft * c + it * gt
            return (c, None)
        c_final, _ = lax.scan(step, c0, x)
        h = jnp.tanh(jnp.einsum('tbi,oi->tbo', x, wo) + c_final @ uo.T + bo)
        return h

    def _L1_xattn_ref(query, key_in, value, group_prob, mask, wq_k, wq_b, wk_k, wk_b, wv_k, wv_b, wo_k, wo_b):
        import jax, jax.numpy as jnp
        import numpy as np
        NUM_HEADS = 16
        HIDDEN = 256
        B, S = (2, 512)

        def _split_heads(x, H):
            b, s, d = x.shape
            return x.reshape(b, s, H, d // H).transpose(0, 2, 1, 3)
        H = NUM_HEADS
        dh = query.shape[-1] // H
        q = _split_heads(query @ wq_k + wq_b, H)
        k = _split_heads(key_in @ wk_k + wk_b, H)
        v = _split_heads(value @ wv_k + wv_b, H)
        logits = jnp.einsum('bhqd,bhkd->bhqk', q, k) / jnp.sqrt(jnp.asarray(dh, q.dtype))
        neg = (1.0 - mask.astype(q.dtype)) * -1000000000.0
        logits = logits + neg[:, None, :, :]
        attn = jax.nn.softmax(logits, axis=-1)
        attn = attn * group_prob[:, None, :, :]
        out = jnp.einsum('bhqk,bhkd->bhqd', attn, v)
        out = out.transpose(0, 2, 1, 3).reshape(query.shape[0], -1, H * dh)
        return out @ wo_k + wo_b

    def _L1_ffn_ref(x, W_qkv, b_qkv, W_gate, b_gate, W_experts, b_experts):
        import jax, jax.numpy as jnp
        import numpy as np
        NUM_HEADS = 16
        TOP_K = 2
        B, S, D = x.shape
        H = NUM_HEADS
        hd = D // H
        E = W_gate.shape[-1]
        qkv = (x @ W_qkv + b_qkv).reshape(B, S, 3, H, hd)
        q, k, v = (qkv[:, :, 0], qkv[:, :, 1], qkv[:, :, 2])
        attn = jnp.einsum('bqhd,bkhd->bhqk', q, k) / jnp.sqrt(jnp.asarray(hd, x.dtype))
        attn = jax.nn.softmax(attn, axis=-1)
        attn_out = jnp.einsum('bhqk,bkhd->bqhd', attn, v).reshape(B, S, D)
        gate = jax.nn.softmax(x @ W_gate + b_gate, axis=-1)
        top_g, top_i = jax.lax.top_k(gate, TOP_K)
        combine = jnp.sum(jax.nn.one_hot(top_i, E, dtype=x.dtype) * top_g[..., None], axis=2)
        expert_out = jnp.einsum('bsd,edf->bsef', x, W_experts) + b_experts
        moe_out = jnp.einsum('bsef,bse->bsf', expert_out, combine)
        return attn_out + moe_out
    x = x + jnp.tanh(g_xattn[0]) * _L0_xattn_ref(_layernorm(x, axis=-1), ctx_1024, ctx_1024, mask_Bx1xSxS2_ik1, L0_xattn_wq, L0_xattn_wk, L0_xattn_wv, L0_xattn_wo, L0_xattn_bq, L0_xattn_bk, L0_xattn_bv, L0_xattn_bo)
    x = x + jnp.tanh(g_ffn[0]) * _L0_ffn_ref(_layernorm(x, axis=-1), L0_ffn_wf, L0_ffn_uf, L0_ffn_bf, L0_ffn_wi, L0_ffn_ui, L0_ffn_bi, L0_ffn_wc, L0_ffn_uc, L0_ffn_bc, L0_ffn_wo, L0_ffn_uo, L0_ffn_bo, L0_ffn_in_c)
    x = x + jnp.tanh(g_xattn[1]) * _L1_xattn_ref(_layernorm(x, axis=-1), ctx_1024, ctx_1024, fside_BxSxS2_0, mask_BxSxS2_ik1, L1_xattn_wq_k, L1_xattn_wq_b, L1_xattn_wk_k, L1_xattn_wk_b, L1_xattn_wv_k, L1_xattn_wv_b, L1_xattn_wo_k, L1_xattn_wo_b)
    x = x + jnp.tanh(g_ffn[1]) * _L1_ffn_ref(_layernorm(x, axis=-1), L1_ffn_W_qkv, L1_ffn_b_qkv, L1_ffn_W_gate, L1_ffn_b_gate, L1_ffn_W_experts, L1_ffn_b_experts)
    return x

_drawn_inputs = setup_inputs


def setup_inputs(seed=0):
    import zlib

    import numpy as np

    out = dict(_drawn_inputs(seed))
    spreads = {'g_ffn': (-1.0, 0.6),
     'L0_xattn_bq': (0.0, 0.432),
     'L0_xattn_bk': (0.0, 2.0),
     'L0_xattn_bv': (0.0, 0.1),
     'L0_xattn_bo': (0.0, 0.1),
     'L0_ffn_bf': (0.0, 0.8),
     'L0_ffn_bi': (0.0, 0.8),
     'L0_ffn_bc': (0.0, 0.1),
     'L0_ffn_bo': (0.0, 0.1),
     'L0_ffn_in_c': (0.0, 2.0),
     'L1_xattn_wq_b': (0.0, 0.651),
     'L1_xattn_wk_b': (0.0, 2.0),
     'L1_xattn_wv_b': (0.0, 0.1),
     'L1_xattn_wo_b': (0.0, 0.1),
     'L1_ffn_b_qkv': (0.0, 0.1),
     'L1_ffn_b_gate': (0.0, 0.286),
     'L1_ffn_b_experts': (0.0, 0.465)}
    factors = {}
    for name, (base, spread) in spreads.items():
        noise = np.random.default_rng([zlib.crc32(name.encode()), seed]).standard_normal(out[name].shape)
        drawn = base * np.exp(spread * noise) if base else spread * noise
        out[name] = jnp.asarray(drawn.astype(out[name].dtype))
    for name, factor in factors.items():
        out[name] = (out[name] * factor).astype(out[name].dtype)
    return out
```

```python
from contextlib import ExitStack

import numpy as np

import concourse.bass as bass
from concourse import mybir

F32 = mybir.dt.float32
F32R = mybir.dt.float32r
BF16 = mybir.dt.bfloat16
I32 = mybir.dt.int32
ALU = mybir.AluOpType
ACT = mybir.ActivationFunctionType
AX = mybir.AxisListType

P = 128
D = 256
KT = D // P
S = 256
QT = S // P
S2 = 120
H = 16
HD = D // H
PAIRS = H // 2
VW = 32
E = 8
SCALE = HD ** -0.5
CLIP = 100.0 / SCALE
MASKED = 998244352.0 / SCALE
EPS = 1e-5
LINKS = 160


class Signal:

    def __init__(self, sem, per, steps):
        self.sem, self.per, self.start, at = sem, per, [], 0
        for p in per:
            self.start.append(at)
            at += steps * p

    def at(self, L, n, k=None):
        if isinstance(n, int) and n < 0:
            return self.start[L]
        return self.start[L] + n * self.per[L] + (self.per[L] if k is None else k)


class Chain:

    def __init__(self, eng, sem):
        self.eng, self.sem, self.base, self.k = eng, sem, 0, 0

    def step(self, base):
        self.base, self.k = base, 0

    def link(self, ins):
        ins.then_inc(self.sem, 1)
        self.k += 1
        return self.k

    def at(self, k=None):
        return self.base * LINKS + (self.k if k is None else k)

    def close(self):
        assert self.k < LINKS
        self.eng.sem_inc(self.sem, LINKS - self.k)


def flamingo_block(nc, io, out, B):
    ctx = ExitStack()
    with ctx:
        def sb(name, shape, dt=F32):
            return ctx.enter_context(nc.sbuf_tensor(name, shape, dt))

        def sem(name):
            return ctx.enter_context(nc.semaphore(name))

        def signal(name, *per):
            return Signal(sem(name), per, B)

        x1_d = nc.dram_tensor("x1_d", [B, S, D], F32, kind="Internal").ap()
        hx_d = nc.dram_tensor("hx_d", [B, S, D], F32, kind="Internal").ap()
        x2_d = nc.dram_tensor("x2_d", [B, S, D], F32, kind="Internal").ap()
        x3_d = nc.dram_tensor("x3_d", [B, S, D], F32, kind="Internal").ap()
        q_d = [nc.dram_tensor(f"q_d{L}", [B, 2, D, S], F32, kind="Internal").ap() for L in range(3)]
        k_d = [nc.dram_tensor(f"k_d{L}", [B, 2, D, S2 if L < 2 else S], F32, kind="Internal").ap() for L in range(3)]

        ident = sb("ident", [P, P])
        identb = sb("identb", [P, P], BF16)
        sel_f = sb("sel_f", [P, H * P])
        sel = sb("sel", [P, H, P], F32R)
        earlier = sb("earlier", [P, E, E])
        ones_col = sb("ones_col", [P, VW])
        zeros = sb("zeros", [P, S])
        neg_half = sb("neg_half", [P, QT])
        gates_in = sb("gates_in", [P, 4])
        tg = sb("tg", [P, 4])
        wname = ["wq0", "wk0", "wv0", "wo0", "wf", "uf", "wi", "ui", "wc", "uc", "wo_f", "uo_f",
                 "wq1", "wk1", "wv1", "wo1", "wq2", "wk2", "wv2"]
        w = {n: sb("w_" + n, [P, KT, D]) for n in wname}
        w_gate = sb("w_gate", [P, KT, E])
        w_exp = sb("w_exp", [P, KT, E, D])
        colname = ["bq0", "bk0", "bq1", "bk1", "bq2", "bk2", "bf", "bi", "bc", "in_c"]
        col = {n: sb("col_" + n, [P, KT]) for n in colname}
        rowname = ["bv0", "bo0", "bv1", "bo1", "bv2", "bo_f"]
        row = {n: sb("row_" + n, [P, D]) for n in rowname}
        b_gate = sb("b_gate", [P, E])
        b_exp = sb("b_exp", [E, D])

        x_in = sb("x_in", [P, QT, D])
        hx_in = sb("hx_in", [P, QT, D])
        x2 = sb("x2", [P, QT, D])
        x_res = sb("x_res", [P, QT, D])
        ctx_t = sb("ctx_t", [P, KT, S2])
        stats = sb("stats", [P, QT, 6])
        mv = sb("mv", [P, QT, 2])
        var_eps = sb("var_eps", [P, QT])
        rstd = sb("rstd", [P, QT])
        xn = sb("xn", [P, QT, D])
        xt = sb("xt", [P, KT, S])
        qhl = sb("qhl", [P, 2, KT, S], F32R)
        khl = sb("khl", [P, 2, KT, S], F32R)
        q_stack = sb("q_stack", [P, PAIRS, S], F32R)
        k_stack = sb("k_stack", [P, PAIRS, 2, S], F32R)
        vx = sb("vx", [P, 2, H, VW])
        mask_i = sb("mask_i", [P, QT, S2], I32)
        mask_ti = sb("mask_ti", [P, S], I32)
        mask_q = sb("mask_q", [P, QT, S2], BF16)
        mask_k = sb("mask_k", [P, S], BF16)
        prob_k = sb("prob_k", [P, S])
        top = sb("top", [P, QT, H])
        top2 = sb("top2", [P, QT, H])
        shift_hl = sb("shift_hl", [P, QT, 2 * H], F32R)
        shift_t = sb("shift_t", [P, S], F32R)
        NPR = 4
        probs = sb("probs", [P, NPR, 2 * S])
        probs_g = sb("probs_g", [P, NPR, 2 * S])
        att_t = sb("att_t", [P, 4, S])
        rec = sb("rec", [P, QT, H])
        att = sb("att", [P, QT, D])
        att_n = sb("att_n", [P, KT, S])
        y = sb("y", [P, QT, D])
        y2 = sb("y2", [P, QT, D])
        xn1 = sb("xn1", [P, QT, D])
        xt1 = sb("xt1", [P, KT, S])
        cell = sb("cell", [P, KT, S])
        gf = sb("gf", [P, KT, S])
        gi = sb("gi", [P, KT, S])
        gc = sb("gc", [P, KT, S])
        ca = sb("ca", [P, KT, S])
        cb = sb("cb", [P, KT, S])
        hx = sb("hx", [P, QT, D])
        cu = sb("cu", [P, QT, D])
        xtm = sb("xtm", [P, KT, S])
        lg = sb("lg", [P, QT, E])
        nmx = sb("nmx", [P, QT])
        ge = sb("ge", [P, QT, E])
        gsum = sb("gsum", [P, QT])
        grec = sb("grec", [P, QT])
        cmp1 = sb("cmp1", [P, QT, E, E])
        cmp2 = sb("cmp2", [P, QT, E, E])
        rank = sb("rank", [P, QT, E])
        comb = sb("comb", [P, QT, E])
        comb_t = sb("comb_t", [E, S])
        acc = [sb("acc0", [P, QT, D]), sb("acc1", [P, QT, D])]

        def bank(name, n=1):
            return ctx.enter_context(nc.psum_tensor(name, [P, n, 512], F32))
        work = bank("work", 2)
        score = bank("score", 2)
        o_ps = bank("o_ps", 2)
        dense = bank("dense", 2)

        NU = [PAIRS, PAIRS, 2 * PAIRS]
        const_in = sem("const_in")
        const_ready = sem("const_ready")
        gates_ready = sem("gates_ready")
        layer_done = sem("layer_done")
        vx_set = sem("vx_set")
        ones_cleared = sem("ones_cleared")
        cell_final = sem("cell_final")
        cu_ready = sem("cu_ready")
        dve_chain = sem("dve_chain")
        passed = sem("passed")
        x_loaded = signal("x_loaded", 16, 32, 16)
        ctx_loaded = signal("ctx_loaded", 16, 16, 0)
        mask_loaded = signal("mask_loaded", 32, 32, 0)
        prob_loaded = signal("prob_loaded", 0, 16, 0)
        res_loaded = signal("res_loaded", 16, 16, 16)
        parts_stored = signal("parts_stored", 64, 64, 64)
        stack_loaded = signal("stack_loaded", 192, 192, 192)
        y_stored = signal("y_stored", 16, 16, 16)
        hx_stored = signal("hx_stored", 16, 0, 0)
        x2_stored = signal("x2_stored", 0, 16, 0)
        pre_h = signal("pre_h", 0, 1, 0)
        tanh_h = signal("tanh_h", 0, 1, 0)
        x2_ready = signal("x2_ready", 0, 1, 0)
        var_ready = signal("var_ready", 1, 1, 1)
        rstd_ready = signal("rstd_ready", 1, 1, 1)
        xn_ready = signal("xn_ready", 1, 1, 1)
        mask_q_ready = signal("mask_q_ready", 1, 1, 0)
        mask_k_ready = signal("mask_k_ready", 1, 1, 0)
        xt_made = signal("xt_made", 1, 1, 1)
        xt_ready = signal("xt_ready", 1, 1, 1)
        q_made = signal("q_made", 1, 1, 1)
        k_made = signal("k_made", 1, 1, 1)
        v_made = signal("v_made", 1, 1, 1)
        qh_ready = signal("qh_ready", 2, 2, 2)
        kh_ready = signal("kh_ready", 2, 2, 2)
        ql_ready = signal("ql_ready", 2, 2, 2)
        kl_ready = signal("kl_ready", 2, 2, 2)
        v_ready = signal("v_ready", 1, 1, 1)
        tops_made = signal("tops_made", 8, 8, 16)
        tops_read = signal("tops_read", 8, 8, 16)
        shift_ready = signal("shift_ready", 1, 1, 1)
        shift_t_made = signal("shift_t_made", 1, 1, 1)
        shift_t_ready = signal("shift_t_ready", 1, 1, 1)
        raw_made = signal("raw_made", 8, 0, 0)
        clipped = signal("clipped", 8, 0, 0)
        scores_made = signal("scores_made", *NU)
        probs_ready = signal("probs_ready", *NU)
        probs_g_ready = signal("probs_g_ready", 0, NU[1], 0)
        pv_made = signal("pv_made", *NU)
        att_t_ready = signal("att_t_ready", 2, 2, 2)
        att_made = signal("att_made", 2, 2, 2)
        att_ready = signal("att_ready", 2, 2, 2)
        att_n_made = signal("att_n_made", 1, 1, 0)
        att_n_ready = signal("att_n_ready", 1, 1, 0)
        y_made = signal("y_made", 1, 1, 0)
        y_ready = signal("y_ready", 1, 1, 1)
        var1_ready = signal("var1_ready", 1, 0, 0)
        rstd1_ready = signal("rstd1_ready", 1, 0, 0)
        xn1_ready = signal("xn1_ready", 1, 0, 0)
        xt1_made = signal("xt1_made", 1, 0, 0)
        xt1_ready = signal("xt1_ready", 1, 0, 0)
        gate_made = signal("gate_made", 3, 0, 0)
        gate_ready = signal("gate_ready", 3, 0, 0)
        cell_ready = signal("cell_ready", 1, 0, 0)
        hx_made = signal("hx_made", 1, 0, 0)
        hx_ready = signal("hx_ready", 1, 0, 0)
        xtm_ready = signal("xtm_ready", 0, 0, 1)
        logits_made = signal("logits_made", 0, 0, 1)
        logits_ready = signal("logits_ready", 0, 0, 1)
        gexp_ready = signal("gexp_ready", 0, 0, 2)
        comb_ready = signal("comb_ready", 0, 0, 1)
        comb_t_made = signal("comb_t_made", 0, 0, 1)
        comb_t_ready = signal("comb_t_ready", 0, 0, 1)
        ebias_made = signal("ebias_made", 0, 0, 1)
        ebias_read = signal("ebias_read", 0, 0, 1)
        exp_made = signal("exp_made", 0, 0, 8)
        exp_read = signal("exp_read", 0, 0, 8)

        KQ = [S2, S2, P]
        KN = [S2, S2, S]

        FIRST = [2, 1, 1]

        def tokens(ap):
            return ap.rearrange("(t p) d -> p t d", p=P)

        def steps(eng, L, body):
            body(None, 0, None)
            body(0, 1, None)
            if L == 0:
                body(1, 2, 0)
            with eng.Fori(FIRST[L], B - 1) as t:
                body(t, t + 1, t - 1 if L == 0 else None)
            body(B - 1, None, B - 2 if L == 0 else None)
            if L == 0:
                body(None, None, B - 1)

        def layer_end(eng, L):
            eng.drain().then_inc(layer_done, 1)
            eng.wait_ge(layer_done, 5 * (L + 1))

        consts = []
        for n in wname:
            consts.append((w[n][:], io[n].rearrange("(k p) o -> p k o", p=P)))
        consts.append((w_gate[:], io["w_gate"].rearrange("(k p) o -> p k o", p=P)))
        for k in range(KT):
            consts.append((w_exp[:, k], io["w_exp"][:, k * P:(k + 1) * P, :].rearrange("e p o -> p e o")))
        for n in colname:
            consts.append((col[n][:], io[n]))
        for n in rowname:
            consts.append((row[n][:], io[n].partition_broadcast(P)))
        consts.append((b_gate[:], io["b_gate"].partition_broadcast(P)))
        consts.append((b_exp[:], io["b_exp"]))
        consts.append((ident[:], io["ident"]))
        consts.append((sel_f[:], io["sel"]))
        consts.append((earlier[:].rearrange("p a b -> p (a b)"), io["earlier"].partition_broadcast(P)))
        consts.append((gates_in[:, 0:2], io["g_xattn"].partition_broadcast(P)))
        consts.append((gates_in[:, 2:4], io["g_ffn"].partition_broadcast(P)))
        NCONST = 16 * len(consts)
        NREADY = 5

        block = ctx.enter_context(nc.Block())

        @block.sync
        def _(sp):
            for dst, src in consts:
                sp.dma_start(dst, src).then_inc(const_in, 16)

            def body(L, m, n):
                if n is not None:
                    for part, ready in ((0, qh_ready), (1, ql_ready)):
                        sp.wait_ge(ready.sem, ready.at(L, n))
                        sp.dma_start(q_d[L][n, part].rearrange("(m p) t -> p m t", p=P),
                                     qhl[:, part].bitcast(F32)).then_inc(parts_stored.sem, 16)
                    for part, ready in ((0, kh_ready), (1, kl_ready)):
                        sp.wait_ge(ready.sem, ready.at(L, n))
                        sp.dma_start(k_d[L][n, part].rearrange("(m p) t -> p m t", p=P),
                                     khl[:, part, :, 0:KN[L]].bitcast(F32)).then_inc(parts_stored.sem, 16)
                    sp.wait_ge(parts_stored.sem, parts_stored.at(L, n))
                    if m is not None:
                        sp.wait_ge(scores_made.sem, scores_made.at(L, m))
                    for stack, src, order in ((q_stack, q_d[L], (0, 0, 1)), (k_stack, k_d[L], (0, 1, 0))):
                        for par in range(2):
                            for r, part in enumerate(order):
                                rows = slice(64 * par + HD * r, 64 * par + HD * r + HD)
                                dst = stack[rows, :, :] if stack is q_stack else stack[rows, :, par, 0:KN[L]]
                                sp.dma_start(dst.bitcast(F32),
                                             src[n, part].rearrange("(j a d) t -> a d j t", a=2, d=HD)[par])\
                                  .then_inc(stack_loaded.sem, 16)
                if m is not None:
                    sp.wait_ge(y_ready.sem, y_ready.at(L, m))
                    dst = [x1_d, x3_d, out][L]
                    sp.dma_start(tokens(dst[m]), y[:]).then_inc(y_stored.sem, 16)

            def body0(m, n, r):
                body(0, m, n)
                if r is not None:
                    sp.wait_ge(hx_ready.sem, hx_ready.at(0, r))
                    sp.dma_start(tokens(hx_d[r]), hx[:]).then_inc(hx_stored.sem, 16)

            def body1(m, n, r):
                if n is not None:
                    sp.wait_ge(x2_ready.sem, x2_ready.at(1, n))
                    sp.dma_start(tokens(x2_d[n]), x2[:]).then_inc(x2_stored.sem, 16)
                body(1, m, n)

            steps(sp, 0, body0)
            sp.wait_ge(y_stored.sem, y_stored.at(0, B - 1))
            sp.wait_ge(hx_stored.sem, hx_stored.at(0, B - 1))
            layer_end(sp, 0)
            steps(sp, 1, body1)
            sp.wait_ge(y_stored.sem, y_stored.at(1, B - 1))
            sp.wait_ge(x2_stored.sem, x2_stored.at(1, B - 1))
            layer_end(sp, 1)
            steps(sp, 2, lambda m, n, r: body(2, m, n))
            sp.wait_ge(y_stored.sem, y_stored.at(2, B - 1))

        @block.gpsimd
        def _(pool):
            pool.memset(neg_half[:], -0.5).then_inc(const_ready, 1)
            pool.memset(ones_col[:], 0.0).then_inc(ones_cleared, 1)
            pool.wait_ge(ones_cleared, 1)
            pool.memset(ones_col[:, HD:HD + 1], 1.0).then_inc(const_ready, 1)

            def load_prep(L, n):
                if L == 1:
                    pool.wait_ge(x2_ready.sem, x2_ready.at(1, n - 1))
                    pool.sem_inc(passed, 1)
                    pool.dma_start(hx_in[:], tokens(hx_d[n])).then_inc(x_loaded.sem, 16)
                else:
                    pool.wait_ge(xn_ready.sem, xn_ready.at(L, n - 1))
                pool.sem_inc(passed, 1)
                pool.dma_start(x_in[:], tokens([io["x"], x1_d, x3_d][L][n])).then_inc(x_loaded.sem, 16)

            def load_ctx(L, n):
                pool.wait_ge(v_made.sem, v_made.at(L, n - 1))
                pool.sem_inc(passed, 1)
                pool.dma_start(ctx_t[:], io["ctx_t"][n].rearrange("(k p) t -> p k t", p=P)).then_inc(ctx_loaded.sem, 16)

            def load_mask(L, n):
                pool.wait_ge(mask_q_ready.sem, mask_q_ready.at(L, n - 1))
                pool.wait_ge(mask_k_ready.sem, mask_k_ready.at(L, n - 1))
                pool.sem_inc(passed, 1)
                pool.dma_start(mask_i[:], io[f"mask{L}"][n].rearrange("(t p) k -> p t k", p=P))\
                    .then_inc(mask_loaded.sem, 16)
                pool.sem_inc(passed, 1)
                pool.dma_start(mask_ti[0:S2, :], io[f"mask{L}_t"][n]).then_inc(mask_loaded.sem, 16)

            def load_res(L, m):
                pool.wait_ge(y_ready.sem, y_ready.at(L, m - 1))
                pool.sem_inc(passed, 1)
                pool.dma_start(x_res[:], tokens([io["x"], x2_d, x3_d][L][m])).then_inc(res_loaded.sem, 16)

            def body(L, m, n, ahead):
                if n is not None:
                    pool.wait_ge(var_ready.sem, var_ready.at(L, n))
                    pool.tensor_tensor(rstd[:], var_eps[:], neg_half[:], ALU.pow).then_inc(rstd_ready.sem, 1)
                if m is not None:
                    if L == 1:
                        pool.wait_ge(x2_stored.sem, x2_stored.at(1, m))
                    load_res(L, m)
                if ahead is not None:
                    load_prep(L, ahead)
                if L < 2 and n is not None:
                    pool.wait_ge(mask_loaded.sem, mask_loaded.at(L, n))
                    if m is not None:
                        pool.wait_ge(tops_made.sem, tops_made.at(L, m))
                    pool.sem_inc(passed, 1)
                    pool.tensor_scalar(mask_q[:], mask_i[:], MASKED, -MASKED, ALU.mult, ALU.add)\
                        .then_inc(mask_q_ready.sem, 1)
                    if m is not None:
                        pool.wait_ge(scores_made.sem, scores_made.at(L, m))
                    pool.sem_inc(passed, 1)
                    pool.tensor_scalar(mask_k[0:S2, :], mask_ti[0:S2, :], MASKED, -MASKED, ALU.mult, ALU.add)\
                        .then_inc(mask_k_ready.sem, 1)
                    if ahead is not None:
                        load_mask(L, ahead)
                        load_ctx(L, ahead)
                if L == 1 and n is not None:
                    if m is not None:
                        pool.wait_ge(probs_g_ready.sem, probs_g_ready.at(1, m))
                    pool.sem_inc(passed, 1)
                    pool.dma_start(prob_k[0:S2, :], io["prob_t"][n]).then_inc(prob_loaded.sem, 16)
                if L == 2 and n is not None:
                    pool.wait_ge(xt_ready.sem, xt_ready.at(2, n))
                    if m is not None:
                        pool.wait_ge(exp_made.sem, exp_made.at(2, m))
                    pool.sem_inc(passed, 1)
                    pool.tensor_copy(xtm[:], xt[:]).then_inc(xtm_ready.sem, 1)
                if L == 0 and m is not None:
                    pool.wait_ge(var1_ready.sem, var1_ready.at(0, m))
                    pool.tensor_tensor(rstd[:], var_eps[:], neg_half[:], ALU.pow).then_inc(rstd1_ready.sem, 1)

            for L in range(3):
                load_prep(L, 0)
                if L < 2:
                    load_mask(L, 0)
                    load_ctx(L, 0)
                body(L, None, 0, 1)
                for m in range(FIRST[L]):
                    body(L, m, m + 1, m + 2)
                with pool.Fori(FIRST[L], B - 2) as t:
                    body(L, t, t + 1, t + 2)
                body(L, B - 2, B - 1, None)
                body(L, B - 1, None, None)
                if L < 2:
                    layer_end(pool, L)

        @block.scalar
        def _(act):
            act.wait_ge(const_in, NCONST)
            act.activation(tg[:], gates_in[:], ACT.Tanh).then_inc(gates_ready, 1)
            act.wait_ge(const_ready, NREADY)
            for k in range(KT):
                act.activation(cell[:, k, :], zeros[:], ACT.Identity, bias=col["in_c"][:, k:k + 1])\
                    .then_inc(gates_ready, 1)

            def prep(L, n):
                if L == 1:
                    act.wait_ge(pre_h.sem, pre_h.at(1, n))
                    act.activation(hx_in[:], hx_in[:], ACT.Tanh).then_inc(tanh_h.sem, 1)
                act.wait_ge(xt_made.sem, xt_made.at(L, n))
                if L == 2:
                    act.wait_ge(xtm_ready.sem, xtm_ready.at(2, n - 1))
                act.activation(xt[:], work[:, 0, :], ACT.Copy).then_inc(xt_ready.sem, 1)
                act.wait_ge(q_made.sem, q_made.at(L, n))
                act.wait_ge(parts_stored.sem, parts_stored.at(L, n - 1))
                for k in range(KT):
                    act.activation(qhl[:, 0, k, :], work[:, 1, k * S:(k + 1) * S], ACT.Identity,
                                   bias=col[f"bq{L}"][:, k:k + 1]).then_inc(qh_ready.sem, 1)
                act.wait_ge(k_made.sem, k_made.at(L, n))
                for k in range(KT):
                    act.activation(khl[:, 0, k, 0:KN[L]], work[:, 0, k * S:k * S + KN[L]], ACT.Identity,
                                   bias=col[f"bk{L}"][:, k:k + 1]).then_inc(kh_ready.sem, 1)

            def main(L, m):
                act.wait_ge(shift_t_made.sem, shift_t_made.at(L, m))
                act.activation(shift_t[0:2 * H, :], work[0:2 * H, 1, 0:S], ACT.Copy).then_inc(shift_t_ready.sem, 1)
                for u in range(NU[L]):
                    act.wait_ge(scores_made.sem, scores_made.at(L, m, u + 1))
                    if u >= NPR:
                        act.wait_ge(pv_made.sem, pv_made.at(L, m, u - NPR + 1))
                    act.activation(probs[0:KQ[L], u % NPR, :], score[0:KQ[L], u % 2, :], ACT.Exp, scale=SCALE)\
                        .then_inc(probs_ready.sem, 1)
                act.wait_ge(pv_made.sem, pv_made.at(L, m))
                for g in range(2):
                    act.activation(att_t[:, 2 * g:2 * g + 2, :], o_ps[:, g, :], ACT.Copy).then_inc(att_t_ready.sem, 1)

            def late(L, m):
                if L < 2:
                    act.wait_ge(att_n_made.sem, att_n_made.at(L, m))
                    act.activation(att_n[:], work[:, 1, :], ACT.Copy).then_inc(att_n_ready.sem, 1)
                else:
                    act.wait_ge(logits_ready.sem, logits_ready.at(2, m))
                    for t in range(QT):
                        act.activation(ge[:, t, :], lg[:, t, :], ACT.Exp, bias=nmx[:, t:t + 1],
                                       accum_out=gsum[:, t:t + 1]).then_inc(gexp_ready.sem, 1)
                    act.wait_ge(comb_t_made.sem, comb_t_made.at(2, m))
                    act.activation(comb_t[:], work[0:E, 1, 0:S], ACT.Copy).then_inc(comb_t_ready.sem, 1)

            def recur(r):
                act.wait_ge(xt1_made.sem, xt1_made.at(0, r))
                act.activation(xt1[:], dense[:, 0, :], ACT.Copy).then_inc(xt1_ready.sem, 1)
                for g, (dst, b, s, bk) in enumerate(((gf, "bf", 0.5, 1), (gi, "bi", 0.5, 0), (gc, "bc", 1.0, 1))):
                    act.wait_ge(gate_made.sem, gate_made.at(0, r, g + 1))
                    if g == 0:
                        act.wait_ge(cell_ready.sem, cell_ready.at(0, r - 1))
                    for k in range(KT):
                        ins = act.activation(dst[:, k, :], dense[:, bk, k * S:(k + 1) * S], ACT.Tanh,
                                             bias=col[b][:, k:k + 1], scale=s)
                    ins.then_inc(gate_ready.sem, 1)
                act.wait_ge(hx_made.sem, hx_made.at(0, r))
                act.wait_ge(hx_stored.sem, hx_stored.at(0, r - 1))
                act.activation(hx[:], dense[:, 0, :], ACT.Copy).then_inc(hx_ready.sem, 1)

            def body(L, m, n, r):
                if n is not None:
                    prep(L, n)
                if m is not None:
                    main(L, m)
                if r is not None:
                    recur(r)
                if m is not None:
                    late(L, m)

            for L in range(3):
                steps(act, L, lambda m, n, r: body(L, m, n, r))
                if L < 2:
                    layer_end(act, L)

        @block.vector
        def _(dve):
            chain = Chain(dve, dve_chain)
            link = chain.link
            dve.memset(zeros[:], 0.0).then_inc(const_ready, 1)
            dve.memset(q_stack[:].bitcast(F32), 0.0).then_inc(vx_set, 1)
            dve.memset(k_stack[:].bitcast(F32), 0.0).then_inc(vx_set, 1)
            dve.memset(vx[:], 0.0).then_inc(vx_set, 1)
            dve.memset(shift_t[:].bitcast(F32), 0.0).then_inc(vx_set, 1)
            dve.wait_ge(vx_set, 4)
            dve.memset(vx[:, :, :, HD:HD + 1], 1.0).then_inc(const_ready, 1)
            dve.wait_ge(const_in, NCONST)
            dve.tensor_copy(identb[:], ident[:]).then_inc(vx_set, 1)
            dve.tensor_copy(sel[:].rearrange("p h k -> p (h k)"), sel_f[:]).then_inc(vx_set, 1)
            for n in ("bf", "bi"):
                dve.tensor_scalar(col[n][:], col[n][:], 0.5, None, ALU.mult).then_inc(vx_set, 1)
            dve.wait_ge(vx_set, 8)
            dve.tensor_copy(nmx[:], zeros[:, 0:QT]).then_inc(const_ready, 1)
            dve.wait_ge(gates_ready, 1 + KT)

            def spread(src):
                ks = [link(dve.bn_stats(stats[:, t, :], src[:, t, :])) for t in range(QT)]
                for t in range(QT):
                    dve.wait_ge(dve_chain, chain.at(ks[t]))
                    dve.sem_inc(passed, 1)
                    last = link(dve.bn_aggr(mv[:, t, :], stats[:, t, :]))
                dve.wait_ge(dve_chain, chain.at(last))
                return dve.tensor_scalar(var_eps[:], mv[:, :, 1], EPS, None, ALU.add)

            def normal(dst, src):
                for t in range(QT):
                    ins = dve.tensor_scalar(dst[:, t, :], src[:, t, :], mv[:, t, 0:1], rstd[:, t:t + 1],
                                            ALU.subtract, ALU.mult)
                return ins

            def prep_stats(L, n):
                dve.wait_ge(x_loaded.sem, x_loaded.at(L, n))
                src = x_in
                if L == 1:
                    link(dve.tensor_tensor(hx_in[:], hx_in[:], cu[:], ALU.add))
                    dve.wait_ge(dve_chain, chain.at())
                    dve.sem_inc(pre_h.sem, 1)
                    dve.wait_ge(tanh_h.sem, tanh_h.at(1, n))
                    dve.wait_ge(x2_stored.sem, x2_stored.at(1, n - 1))
                    link(dve.scalar_tensor_tensor(x2[:], hx_in[:], tg[:, 2:3], x_in[:], ALU.mult, ALU.add))
                    dve.wait_ge(dve_chain, chain.at())
                    dve.sem_inc(x2_ready.sem, 1)
                    src = x2
                spread(src).then_inc(var_ready.sem, 1)

            def prep_norm(L, n):
                dve.wait_ge(rstd_ready.sem, rstd_ready.at(L, n))
                dve.wait_ge(xt_made.sem, xt_made.at(L, n - 1))
                normal(xn, x2 if L == 1 else x_in).then_inc(xn_ready.sem, 1)

            def prep_low(L, n):
                for made, high, ready, part, bk, b in ((q_made, qh_ready, ql_ready, qhl, 1, "bq"),
                                                       (k_made, kh_ready, kl_ready, khl, 0, "bk")):
                    N = S if part is qhl else KN[L]
                    dve.wait_ge(made.sem, made.at(L, n))
                    dve.wait_ge(high.sem, high.at(L, n))
                    for k in range(KT):
                        dve.scalar_tensor_tensor(part[:, 1, k, 0:N], work[:, bk, k * S:k * S + N],
                                                 col[f"{b}{L}"][:, k:k + 1], part[:, 0, k, 0:N].bitcast(F32),
                                                 ALU.add, ALU.subtract).then_inc(ready.sem, 1)

            def values(L, m, n):
                dve.wait_ge(v_made.sem, v_made.at(L, n))
                if m is not None:
                    dve.wait_ge(pv_made.sem, pv_made.at(L, m))
                nt = 1 if L < 2 else 2
                for t in range(nt):
                    ins = dve.tensor_tensor(
                        vx[0:KQ[L], t, :, 0:HD],
                        work[0:KQ[L], 0, t * D:(t + 1) * D].rearrange("p (h d) -> p h d", h=H),
                        row[f"bv{L}"][0:KQ[L], :].rearrange("p (h d) -> p h d", h=H), ALU.add)
                ins.then_inc(v_ready.sem, 1)

            def maxima(L, m, lo, hi):
                if L < 2:
                    for u in range(lo, hi):
                        t, j = divmod(u, 4)
                        dve.wait_ge(tops_made.sem, tops_made.at(L, m, u + 1))
                        dve.tensor_reduce(top[:, t, 4 * j:4 * j + 4],
                                          score[:, u % 2, 0:4 * S2].rearrange("p (h k) -> p h k", h=4),
                                          AX.X, ALU.max).then_inc(tops_read.sem, 1)
                else:
                    for u in range(2 * lo, 2 * hi):
                        t, j = divmod(u, PAIRS)
                        dve.wait_ge(tops_made.sem, tops_made.at(L, m, u + 1))
                        dve.tensor_reduce(top[:, t, 2 * j:2 * j + 2],
                                          score[:, u % 2, :].rearrange("p (h k) -> p h k", h=2),
                                          AX.X, ALU.max).then_inc(tops_read.sem, 1)

            def shift(L, m):
                dve.wait_ge(tops_read.sem, tops_read.at(L, m))
                if L == 0:
                    link(dve.tensor_scalar(top2[:], top[:], -1.0, CLIP, ALU.mult, ALU.min))
                    dve.wait_ge(dve_chain, chain.at())
                    link(dve.tensor_scalar(top2[:], top2[:], -CLIP, None, ALU.max))
                else:
                    link(dve.tensor_scalar(top2[:], top[:], -1.0, None, ALU.mult))
                dve.wait_ge(dve_chain, chain.at())
                dve.wait_ge(shift_t_made.sem, shift_t_made.at(L, m - 1))
                link(dve.tensor_copy(shift_hl[:, :, 0:H], top2[:]))
                dve.wait_ge(dve_chain, chain.at())
                dve.tensor_tensor(shift_hl[:, :, H:2 * H], top2[:], shift_hl[:, :, 0:H].bitcast(F32),
                                  ALU.subtract).then_inc(shift_ready.sem, 1)

            def pass_work(L, m):
                if L == 0:
                    for u in range(NU[0]):
                        dve.wait_ge(raw_made.sem, raw_made.at(0, m, u + 1))
                        dve.tensor_scalar(score[0:S2, u % 2, :], score[0:S2, u % 2, :], CLIP, -CLIP,
                                          ALU.min, ALU.max).then_inc(clipped.sem, 1)
                if L == 1:
                    dve.wait_ge(prob_loaded.sem, prob_loaded.at(1, m))
                    for u in range(NU[1]):
                        dve.wait_ge(probs_ready.sem, probs_ready.at(1, m, u + 1))
                        if u >= NPR:
                            dve.wait_ge(pv_made.sem, pv_made.at(1, m, u - NPR + 1))
                        dve.tensor_tensor(probs_g[0:S2, u % NPR, :].rearrange("p (a q) -> p a q", a=2),
                                          probs[0:S2, u % NPR, :].rearrange("p (a q) -> p a q", a=2),
                                          prob_k[0:S2, :].unsqueeze(1).to_broadcast([S2, 2, S]),
                                          ALU.mult).then_inc(probs_g_ready.sem, 1)

            def attended(L, m):
                for t in range(QT):
                    dve.wait_ge(att_made.sem, att_made.at(L, m, t + 1))
                    rows = dense[:, t, :].rearrange("p (h c) -> p h c", h=H)
                    link(dve.reciprocal(rec[:, t, :], rows[:, :, HD]))
                    dve.wait_ge(dve_chain, chain.at())
                    dve.tensor_tensor(att[:, t, :].rearrange("p (h d) -> p h d", h=H), rows[:, :, 0:HD],
                                      rec[:, t, :].unsqueeze(2).to_broadcast([P, H, HD]), ALU.mult)\
                        .then_inc(att_ready.sem, 1)

            def project(L, m):
                dve.wait_ge(y_made.sem, y_made.at(L, m))
                link(dve.tensor_tensor(y2[:], work[:, 1, :].rearrange("p (t d) -> p t d", t=QT),
                                       row[f"bo{L}"][:].unsqueeze(1).to_broadcast([P, QT, D]), ALU.add))
                dve.wait_ge(dve_chain, chain.at())
                dve.wait_ge(res_loaded.sem, res_loaded.at(L, m))
                dve.wait_ge(y_stored.sem, y_stored.at(L, m - 1))
                link(dve.scalar_tensor_tensor(y[:], y2[:], tg[:, L:L + 1], x_res[:], ALU.mult, ALU.add))
                dve.wait_ge(dve_chain, chain.at())
                dve.sem_inc(y_ready.sem, 1)
                if L == 0:
                    spread(y).then_inc(var1_ready.sem, 1)
                    dve.wait_ge(rstd1_ready.sem, rstd1_ready.at(0, m))
                    dve.wait_ge(xt1_made.sem, xt1_made.at(0, m - 1))
                    normal(xn1, y).then_inc(xn1_ready.sem, 1)

            def recur(r):
                dve.wait_ge(gate_ready.sem, gate_ready.at(0, r, 1))
                a = link(dve.scalar_tensor_tensor(ca[:], gf[:], 1.0, cell[:], ALU.add, ALU.mult))
                dve.wait_ge(gate_ready.sem, gate_ready.at(0, r, 3))
                link(dve.scalar_tensor_tensor(cb[:], gi[:], 1.0, gc[:], ALU.add, ALU.mult))
                dve.wait_ge(dve_chain, chain.at())
                link(dve.tensor_tensor(ca[:], ca[:], cb[:], ALU.add))
                dve.wait_ge(dve_chain, chain.at())
                dve.tensor_scalar(cell[:], ca[:], 0.5, None, ALU.mult).then_inc(cell_ready.sem, 1)

            def experts(m):
                dve.wait_ge(logits_made.sem, logits_made.at(2, m))
                link(dve.tensor_tensor(lg[:], work[:, 1, 0:QT * E].rearrange("p (t e) -> p t e", t=QT),
                                       b_gate[:].unsqueeze(1).to_broadcast([P, QT, E]), ALU.add))
                dve.wait_ge(dve_chain, chain.at())
                dve.tensor_reduce(nmx[:], lg[:], AX.X, ALU.max, negate=True).then_inc(logits_ready.sem, 1)
                attended(2, m)
                dve.wait_ge(gexp_ready.sem, gexp_ready.at(2, m))
                link(dve.reciprocal(grec[:], gsum[:]))
                mine = ge[:].unsqueeze(3).to_broadcast([P, QT, E, E])
                other = ge[:].unsqueeze(2).to_broadcast([P, QT, E, E])
                link(dve.tensor_tensor(cmp1[:], other, mine, ALU.is_equal))
                link(dve.tensor_tensor(cmp2[:], other, mine, ALU.is_gt))
                dve.wait_ge(dve_chain, chain.at())
                link(dve.tensor_tensor(cmp1[:], cmp1[:], earlier[:].unsqueeze(1).to_broadcast([P, QT, E, E]), ALU.mult))
                dve.wait_ge(dve_chain, chain.at())
                link(dve.tensor_tensor(cmp1[:], cmp1[:], cmp2[:], ALU.add))
                dve.wait_ge(dve_chain, chain.at())
                link(dve.tensor_reduce(rank[:], cmp1[:], AX.X, ALU.add))
                dve.wait_ge(dve_chain, chain.at())
                link(dve.scalar_tensor_tensor(comb[:], rank[:], 2.0, ge[:], ALU.is_lt, ALU.mult))
                dve.wait_ge(dve_chain, chain.at())
                dve.tensor_tensor(comb[:], comb[:], grec[:].unsqueeze(2).to_broadcast([P, QT, E]), ALU.mult)\
                    .then_inc(comb_ready.sem, 1)
                dve.wait_ge(comb_ready.sem, comb_ready.at(2, m))
                last = [[None, None], [None, None]]
                for u in range(8):
                    pair, t = divmod(u, 2)
                    dve.wait_ge(exp_made.sem, exp_made.at(2, m, u + 1))
                    if u == 6:
                        pass
                    for a in range(2):
                        e = 2 * pair + a
                        src = dense[:, t, a * D:(a + 1) * D]
                        if pair == 0:
                            if a == 0:
                                dve.wait_ge(att_ready.sem, att_ready.at(2, m))
                                ins = dve.scalar_tensor_tensor(acc[0][:, t, :], src, comb[:, t, e:e + 1],
                                                               att[:, t, :], ALU.mult, ALU.add)
                            else:
                                ins = dve.tensor_scalar(acc[1][:, t, :], src, comb[:, t, e:e + 1], None, ALU.mult)
                        else:
                            dve.wait_ge(dve_chain, chain.at(last[a][t]))
                            ins = dve.scalar_tensor_tensor(acc[a][:, t, :], src, comb[:, t, e:e + 1],
                                                           acc[a][:, t, :], ALU.mult, ALU.add)
                        last[a][t] = link(ins)
                    dve.wait_ge(dve_chain, chain.at())
                    dve.sem_inc(exp_read.sem, 1)
                dve.wait_ge(ebias_made.sem, ebias_made.at(2, m))
                k1 = link(dve.tensor_tensor(acc[0][:], acc[0][:], acc[1][:], ALU.add))
                dve.wait_ge(dve_chain, chain.at())
                link(dve.tensor_tensor(acc[0][:], acc[0][:], work[:, 1, :].rearrange("p (t d) -> p t d", t=QT),
                                       ALU.add))
                dve.wait_ge(dve_chain, chain.at())
                dve.sem_inc(ebias_read.sem, 1)
                dve.wait_ge(res_loaded.sem, res_loaded.at(2, m))
                dve.wait_ge(y_stored.sem, y_stored.at(2, m - 1))
                dve.scalar_tensor_tensor(y[:], acc[0][:], tg[:, 3:4], x_res[:], ALU.mult, ALU.add)\
                    .then_inc(y_ready.sem, 1)

            def body(L, m, n, r, base):
                chain.step(base)
                if n is not None:
                    prep_stats(L, n)
                if m is not None:
                    maxima(L, m, 0, 4)
                if n is not None:
                    prep_norm(L, n)
                if m is not None:
                    maxima(L, m, 4, 8)
                    shift(L, m)
                if n is not None:
                    prep_low(L, n)
                if m is not None:
                    pass_work(L, m)
                if n is not None:
                    values(L, m, n)
                if m is not None and L < 2:
                    attended(L, m)
                if r is not None:
                    recur(r)
                if m is not None and L < 2:
                    project(L, m)
                if m is not None and L == 2:
                    experts(m)
                chain.close()

            body(0, None, 0, None, 0)
            body(0, 0, 1, None, 1)
            body(0, 1, 2, 0, 2)
            with dve.Fori(FIRST[0], B - 1) as t:
                body(0, t, t + 1, t - 1, t + 1)
            body(0, B - 1, None, B - 2, B)
            body(0, None, None, B - 1, B + 1)
            dve.wait_ge(cell_final, 1)
            dve.tensor_tensor(cu[:], work[:, 0, :].rearrange("p (t d) -> p t d", t=QT),
                              row["bo_f"][:].unsqueeze(1).to_broadcast([P, QT, D]), ALU.add).then_inc(cu_ready, 1)
            dve.memset(vx[:, :, :, HD:HD + 1], 0.0).then_inc(cu_ready, 1)
            dve.wait_ge(cu_ready, 2)
            layer_end(dve, 0)
            for L in (1, 2):
                first = L * (B + 1) + 1
                body(L, None, 0, None, first)
                body(L, 0, 1, None, first + 1)
                with dve.Fori(FIRST[L], B - 1) as t:
                    body(L, t, t + 1, None, t + first + 1)
                body(L, B - 1, None, None, first + B)
                if L == 1:
                    dve.memset(vx[:, :, :, HD:HD + 1], 1.0).then_inc(cu_ready, 1)
                    dve.wait_ge(cu_ready, 3)
                    layer_end(dve, 1)

        @block.tensor
        def _(pe):
            pe.wait_ge(const_in, NCONST)
            pe.wait_ge(const_ready, NREADY)
            pe.wait_ge(gates_ready, 1 + KT)

            last_use = [y_ready, y_ready, ebias_read]

            def mm(dst, lhs, rhs, start=True, stop=True):
                return pe.matmul(dst, lhs, rhs, start=start, stop=stop, skip_group_check=True)

            def turn(dst, src, parts):
                for t in range(QT):
                    for k in range(KT):
                        ins = pe.transpose(dst[:, k * S + t * P:k * S + (t + 1) * P], src[:, t, k * P:(k + 1) * P],
                                           ident[:])
                return ins

            def features(dst, weight, rhs, N):
                for o in range(KT):
                    for k in range(KT):
                        ins = mm(dst[:, o * S:o * S + N], weight[:, k, o * P:(o + 1) * P], rhs[:, k, 0:N],
                                 start=k == 0, stop=k == KT - 1)
                return ins

            def rows(dst, lhs, weight, tiles=QT, M=P):
                for t in range(tiles):
                    for k in range(KT):
                        ins = mm(dst[0:M, t * D:(t + 1) * D], lhs[:, k, t * P:t * P + M], weight[:, k, :],
                                 start=k == 0, stop=k == KT - 1)
                return ins

            def prep(L, n):
                pe.wait_ge(xn_ready.sem, xn_ready.at(L, n))
                pe.wait_ge(v_ready.sem, v_ready.at(L, n - 1))
                turn(work[:, 0, :], xn, None).then_inc(xt_made.sem, 1)
                pe.wait_ge(xt_ready.sem, xt_ready.at(L, n))
                pe.wait_ge(last_use[L].sem, last_use[L].at(L, n - 2))
                features(work[:, 1, :], w[f"wq{L}"], xt, S).then_inc(q_made.sem, 1)
                if L < 2:
                    pe.wait_ge(ctx_loaded.sem, ctx_loaded.at(L, n))
                features(work[:, 0, :], w[f"wk{L}"], ctx_t if L < 2 else xt, KN[L]).then_inc(k_made.sem, 1)

            def tops(L, m):
                pe.wait_ge(stack_loaded.sem, stack_loaded.at(L, m))
                if L < 2:
                    pe.wait_ge(mask_q_ready.sem, mask_q_ready.at(L, m))
                    for u in range(8):
                        t, jj = divmod(u, 4)
                        if u < 2:
                            pe.wait_ge(probs_ready.sem, probs_ready.at(L, m - 1))
                        else:
                            pe.wait_ge(tops_read.sem, tops_read.at(L, m, u - 1))
                        mm(score[:, u % 2, 0:4 * S2].rearrange("p (h k) -> p h k", h=4), identb[:],
                           mask_q[:, t, :].unsqueeze(1).to_broadcast([P, 4, S2]), start=True, stop=False)
                        for a in range(2):
                            j = 2 * jj + a
                            ins = mm(score[:, u % 2, a * 2 * S2:(a + 1) * 2 * S2].rearrange("p (h k) -> p h k", h=2),
                                     q_stack[:, j, t * P:(t + 1) * P], k_stack[:, j, :, 0:S2],
                                     start=False, stop=True)
                        ins.then_inc(tops_made.sem, 1)
                else:
                    for u in range(16):
                        t, j = divmod(u, PAIRS)
                        if u < 2:
                            pe.wait_ge(probs_ready.sem, probs_ready.at(L, m - 1))
                        else:
                            pe.wait_ge(tops_read.sem, tops_read.at(L, m, u - 1))
                        ins = mm(score[:, u % 2, :], q_stack[:, j, t * P:(t + 1) * P],
                                 k_stack[:, j, :, :].rearrange("p a k -> p (a k)"))
                        ins.then_inc(tops_made.sem, 1)

            def shifts(L, m):
                pe.wait_ge(shift_ready.sem, shift_ready.at(L, m))
                if isinstance(m, int) and m == B - 1:
                    pe.wait_ge(last_use[L].sem, last_use[L].at(L, m - 1))
                else:
                    pe.wait_ge(ql_ready.sem, ql_ready.at(L, m + 1))
                    pe.wait_ge(qh_ready.sem, qh_ready.at(L, m + 1))
                for t in range(QT):
                    ins = pe.transpose(work[0:2 * H, 1, t * P:(t + 1) * P], shift_hl[:, t, :].bitcast(F32), ident[:])
                ins.then_inc(shift_t_made.sem, 1)

            def stacked(L, u, start):
                kq = KQ[L]
                j, kt = (u, 0) if L < 2 else divmod(u, 2)
                for par in range(2):
                    ins = mm(score[0:kq, u % 2, par * S:(par + 1) * S], k_stack[:, j, par, kt * P:kt * P + kq],
                             q_stack[:, j, :],
                             start=start and par == 0, stop=False)
                return ins

            def masked(u):
                return mm(score[0:S2, u % 2, :].rearrange("p (a q) -> p a q", a=2), identb[0:S2, 0:S2],
                          mask_k[0:S2, :].unsqueeze(1).to_broadcast([S2, 2, S]), start=False, stop=False)

            def shifted(L, u):
                kq = KQ[L]
                j = u if L < 2 else u // 2
                for par in range(2):
                    ins = mm(score[0:kq, u % 2, par * S:(par + 1) * S], sel[:, 2 * j + par, 0:kq], shift_t[:],
                             start=False, stop=par == 1)
                return ins

            def products(L, m, u):
                kq = KQ[L]
                j, kt = (u, 0) if L < 2 else divmod(u, 2)
                nt = 1 if L < 2 else 2
                pe.wait_ge(probs_ready.sem, probs_ready.at(L, m, u + 1))
                if L == 1:
                    pe.wait_ge(probs_g_ready.sem, probs_g_ready.at(L, m, u + 1))
                for par in range(2):
                    h = 2 * j + par
                    c, g = h % 4, h // 4
                    dst = o_ps[32 * c:32 * c + VW, g // 2, (g % 2) * S:(g % 2 + 1) * S]
                    p = probs[0:kq, u % NPR, par * S:(par + 1) * S]
                    if L == 1:
                        mm(dst, vx[0:kq, 0, h, :], probs_g[0:kq, u % NPR, par * S:(par + 1) * S],
                           start=True, stop=False)
                        ins = mm(dst, ones_col[0:kq, :], p, start=False, stop=True)
                    else:
                        ins = mm(dst, vx[0:kq, kt, h, :], p, start=kt == 0, stop=kt == nt - 1)
                ins.then_inc(pv_made.sem, 1)

            def probabilities(L, m):
                pe.wait_ge(shift_t_ready.sem, shift_t_ready.at(L, m))
                pe.wait_ge(v_ready.sem, v_ready.at(L, m))
                pe.wait_ge(tops_read.sem, tops_read.at(L, m))
                if L < 2:
                    pe.wait_ge(mask_k_ready.sem, mask_k_ready.at(L, m))
                pe.wait_ge(att_t_ready.sem, att_t_ready.at(L, m - 1))
                if L == 0:
                    def first(u):
                        if u >= 2:
                            pe.wait_ge(probs_ready.sem, probs_ready.at(L, m, u - 1))
                        stacked(L, u, True).then_inc(raw_made.sem, 1)

                    first(0)
                    first(1)
                    for u in range(NU[0]):
                        pe.wait_ge(clipped.sem, clipped.at(L, m, u + 1))
                        masked(u)
                        shifted(L, u).then_inc(scores_made.sem, 1)
                        if u >= 1:
                            products(L, m, u - 1)
                            if u + 1 < NU[0]:
                                first(u + 1)
                    products(L, m, NU[0] - 1)
                else:
                    for u in range(NU[L]):
                        if u >= 2:
                            pe.wait_ge(probs_ready.sem, probs_ready.at(L, m, u - 1))
                        stacked(L, u, True)
                        if L == 1:
                            masked(u)
                        shifted(L, u).then_inc(scores_made.sem, 1)
                        if u >= 2:
                            products(L, m, u - 2)
                    products(L, m, NU[L] - 2)
                    products(L, m, NU[L] - 1)

            def vals(L, n):
                pe.wait_ge(kh_ready.sem, kh_ready.at(L, n))
                pe.wait_ge(kl_ready.sem, kl_ready.at(L, n))
                if L < 2:
                    rows(work[:, 0, :], ctx_t, w[f"wv{L}"], tiles=1, M=S2).then_inc(v_made.sem, 1)
                else:
                    rows(work[:, 0, :], xt, w["wv2"]).then_inc(v_made.sem, 1)

            def turned(L, m):
                pe.wait_ge(att_t_ready.sem, att_t_ready.at(L, m))
                if L == 0:
                    pe.wait_ge(att_ready.sem, att_ready.at(0, m - 1))
                    pe.wait_ge(hx_ready.sem, hx_ready.at(0, m - 2))
                elif L == 1:
                    pe.wait_ge(att_ready.sem, att_ready.at(1, m - 1))
                else:
                    pe.wait_ge(exp_read.sem, exp_read.at(2, m - 1))
                for t in range(QT):
                    for g in range(4):
                        ins = pe.transpose(dense[:, t, g * P:(g + 1) * P], att_t[:, g, t * P:(t + 1) * P], ident[:])
                    ins.then_inc(att_made.sem, 1)

            def att_back(L, m):
                pe.wait_ge(att_ready.sem, att_ready.at(L, m))
                pe.wait_ge(shift_t_ready.sem, shift_t_ready.at(L, m))
                turn(work[:, 1, :], att, None).then_inc(att_n_made.sem, 1)

            def att_project(L, m):
                pe.wait_ge(att_n_ready.sem, att_n_ready.at(L, m))
                rows(work[:, 1, :], att_n, w[f"wo{L}"]).then_inc(y_made.sem, 1)

            def gate(r, g, bk, wn, un):
                for o in range(KT):
                    for k in range(2 * KT):
                        rhs = xt1[:, k, :] if k < KT else cell[:, k - KT, :]
                        ws = w[wn] if k < KT else w[un]
                        ins = mm(dense[:, bk, o * S:(o + 1) * S], ws[:, k % KT, o * P:(o + 1) * P], rhs,
                                 start=k == 0, stop=k == 2 * KT - 1)
                ins.then_inc(gate_made.sem, 1)

            def recur_turn(r, m):
                pe.wait_ge(xn1_ready.sem, xn1_ready.at(0, r))
                if m is not None:
                    pe.wait_ge(att_ready.sem, att_ready.at(0, m))
                else:
                    pe.wait_ge(hx_ready.sem, hx_ready.at(0, r - 1))
                turn(dense[:, 0, :], xn1, None).then_inc(xt1_made.sem, 1)
                pe.wait_ge(xt1_ready.sem, xt1_ready.at(0, r))
                pe.wait_ge(cell_ready.sem, cell_ready.at(0, r - 1))
                gate(r, 0, 1, "wf", "uf")
                gate(r, 1, 0, "wi", "ui")

            def recur_rest(r):
                pe.wait_ge(gate_ready.sem, gate_ready.at(0, r, 1))
                gate(r, 2, 1, "wc", "uc")
                pe.wait_ge(gate_ready.sem, gate_ready.at(0, r, 2))
                rows(dense[:, 0, :], xt1, w["wo_f"]).then_inc(hx_made.sem, 1)

            def expert(m, u):
                pair, t = divmod(u, 2)
                if pair == 0:
                    pe.wait_ge(att_ready.sem, att_ready.at(2, m, t + 1))
                else:
                    pe.wait_ge(exp_read.sem, exp_read.at(2, m, u - 1))
                for k in range(KT):
                    ins = mm(dense[:, t, :], xtm[:, k, t * P:(t + 1) * P],
                             w_exp[:, k, 2 * pair:2 * pair + 2, :].rearrange("p e d -> p (e d)"),
                             start=k == 0, stop=k == KT - 1)
                ins.then_inc(exp_made.sem, 1)

            def experts(m):
                pe.wait_ge(xtm_ready.sem, xtm_ready.at(2, m))
                pe.wait_ge(shift_t_ready.sem, shift_t_ready.at(2, m))
                for t in range(QT):
                    for k in range(KT):
                        ins = mm(work[:, 1, t * E:(t + 1) * E], xtm[:, k, t * P:(t + 1) * P], w_gate[:, k, :],
                                 start=k == 0, stop=k == KT - 1)
                ins.then_inc(logits_made.sem, 1)
                turned(2, m)
                for u in range(8):
                    if u == 2:
                        pe.wait_ge(comb_ready.sem, comb_ready.at(2, m))
                        for t in range(QT):
                            ins = pe.transpose(work[0:E, 1, t * P:(t + 1) * P], comb[:, t, :], ident[:])
                        ins.then_inc(comb_t_made.sem, 1)
                    if u == 6:
                        pe.wait_ge(comb_t_ready.sem, comb_t_ready.at(2, m))
                        for t in range(QT):
                            ins = mm(work[:, 1, t * D:(t + 1) * D], comb_t[:, t * P:(t + 1) * P], b_exp[:])
                        ins.then_inc(ebias_made.sem, 1)
                    expert(m, u)

            def body(L, m, n, r):
                if m is not None:
                    tops(L, m)
                if n is not None:
                    prep(L, n)
                if m is not None:
                    shifts(L, m)
                    probabilities(L, m)
                if n is not None:
                    vals(L, n)
                if m is not None and L < 2:
                    turned(L, m)
                if r is not None:
                    recur_turn(r, m)
                if m is not None and L < 2:
                    att_back(L, m)
                if r is not None:
                    recur_rest(r)
                if m is not None and L < 2:
                    att_project(L, m)
                if m is not None and L == 2:
                    experts(m)

            for L in range(3):
                steps(pe, L, lambda m, n, r: body(L, m, n, r))
                if L == 0:
                    pe.wait_ge(cell_ready.sem, cell_ready.at(0, B - 1))
                    pe.wait_ge(v_ready.sem, v_ready.at(0, B - 1))
                    rows(work[:, 0, :], cell, w["uo_f"]).then_inc(cell_final, 1)
                if L < 2:
                    layer_end(pe, L)


def _layout(i):
    c = np.ascontiguousarray
    a = {k: np.asarray(v) for k, v in i.items()}
    z = {"x": a["x"], "ctx_t": c(a["ctx_1024"].transpose(0, 2, 1)),
         "mask0": c(a["mask_Bx1xSxS2_ik1"][:, 0]), "mask0_t": c(a["mask_Bx1xSxS2_ik1"][:, 0].transpose(0, 2, 1)),
         "mask1": a["mask_BxSxS2_ik1"], "mask1_t": c(a["mask_BxSxS2_ik1"].transpose(0, 2, 1)),
         "prob_t": c(a["fside_BxSxS2_0"].transpose(0, 2, 1)), "g_xattn": a["g_xattn"], "g_ffn": a["g_ffn"]}
    for n in "qkvo":
        z[f"w{n}0"] = c(a[f"L0_xattn_w{n}"].T)
        z[f"b{n}0"] = a[f"L0_xattn_b{n}"]
        z[f"w{n}1"] = a[f"L1_xattn_w{n}_k"]
        z[f"b{n}1"] = a[f"L1_xattn_w{n}_b"]
    for s, n in enumerate("qkv"):
        z[f"w{n}2"] = c(a["L1_ffn_W_qkv"][:, s * D:(s + 1) * D])
        z[f"b{n}2"] = c(a["L1_ffn_b_qkv"][s * D:(s + 1) * D])
    for n in "fic":
        z[f"w{n}"], z[f"u{n}"], z[f"b{n}"] = c(a[f"L0_ffn_w{n}"].T), c(a[f"L0_ffn_u{n}"].T), a[f"L0_ffn_b{n}"]
    z["wo_f"], z["uo_f"], z["bo_f"] = c(a["L0_ffn_wo"].T), c(a["L0_ffn_uo"].T), a["L0_ffn_bo"]
    z["in_c"] = a["L0_ffn_in_c"]
    z["w_gate"], z["b_gate"] = a["L1_ffn_W_gate"], a["L1_ffn_b_gate"]
    z["w_exp"], z["b_exp"] = a["L1_ffn_W_experts"], a["L1_ffn_b_experts"]
    z["ident"] = np.eye(P, dtype=np.float32)
    z["sel"] = np.zeros((P, H * P), np.float32)
    z["sel"][0:2 * H] = np.repeat(np.tile(np.eye(H, dtype=np.float32), (2, 1)), P, axis=1)
    z["earlier"] = np.tril(np.ones((E, E), np.float32), -1).reshape(-1)
    for n in ("bq0", "bk0", "bq1", "bk1", "bq2", "bk2", "bf", "bi", "bc", "in_c"):
        z[n] = z[n].reshape(KT, P).T
    return {k: c(v) for k, v in z.items()}


def kernel(**inputs):
    import concourse.bacc as _bacc
    from concourse.bass_utils import run_bass_kernel_spmd as _run

    arrays = _layout(inputs)
    batches = arrays["x"].shape[0]
    nc = _bacc.Bacc("TRN2", target_bir_lowering=False, num_devices=1)
    io = {n: nc.dram_tensor("in_" + n, a.shape, mybir.dt.from_np(a.dtype), kind="ExternalInput").ap()
          for n, a in arrays.items()}
    out = nc.dram_tensor("out_x", arrays["x"].shape, F32, kind="ExternalOutput").ap()
    flamingo_block(nc, io, out, batches)
    r = _run(nc, [{"in_" + n: a for n, a in arrays.items()}], core_ids=[0])
    return r.results[0]["out_x"]
```

```python
from contextlib import ExitStack

import numpy as np

import concourse.bass as bass
from concourse import mybir

F32 = mybir.dt.float32
F32R = mybir.dt.float32r
BF16 = mybir.dt.bfloat16
I32 = mybir.dt.int32
ALU = mybir.AluOpType
ACT = mybir.ActivationFunctionType
AX = mybir.AxisListType

P = 128
D = 256
KT = D // P
S = 256
QT = S // P
S2 = 120
H = 16
HD = D // H
PAIRS = H // 2
VW = 32
E = 8
SCALE = HD ** -0.5
CLIP = 100.0 / SCALE
MASKED = 998244352.0 / SCALE
EPS = 1e-5
LINKS = 160


class Signal:

    def __init__(self, sem, per, steps):
        self.sem, self.per, self.start, at = sem, per, [], 0
        for p in per:
            self.start.append(at)
            at += steps * p

    def at(self, L, n, k=None):
        if isinstance(n, int) and n < 0:
            return self.start[L]
        return self.start[L] + n * self.per[L] + (self.per[L] if k is None else k)


class Chain:

    def __init__(self, eng, sem):
        self.eng, self.sem, self.base, self.k = eng, sem, 0, 0

    def step(self, base):
        self.base, self.k = base, 0

    def link(self, ins):
        ins.then_inc(self.sem, 1)
        self.k += 1
        return self.k

    def at(self, k=None):
        return self.base * LINKS + (self.k if k is None else k)

    def close(self):
        assert self.k < LINKS
        self.eng.sem_inc(self.sem, LINKS - self.k)


def flamingo_block(nc, io, out, B):
    ctx = ExitStack()
    with ctx:
        def sb(name, shape, dt=F32):
            return ctx.enter_context(nc.sbuf_tensor(name, shape, dt))

        def sem(name):
            return ctx.enter_context(nc.semaphore(name))

        def signal(name, *per):
            return Signal(sem(name), per, B)

        x1_d = nc.dram_tensor("x1_d", [B, S, D], F32, kind="Internal").ap()
        hx_d = nc.dram_tensor("hx_d", [B, S, D], F32, kind="Internal").ap()
        x2_d = nc.dram_tensor("x2_d", [B, S, D], F32, kind="Internal").ap()
        x3_d = nc.dram_tensor("x3_d", [B, S, D], F32, kind="Internal").ap()
        q_d = [nc.dram_tensor(f"q_d{L}", [B, 2, D, S], F32, kind="Internal").ap() for L in range(3)]
        k_d = [nc.dram_tensor(f"k_d{L}", [B, 2, D, S2 if L < 2 else S], F32, kind="Internal").ap() for L in range(3)]

        ident = sb("ident", [P, P])
        identb = sb("identb", [P, P], BF16)
        sel = sb("sel", [P, H, P], F32R)
        earlier = sb("earlier", [P, E, E])
        ones_col = sb("ones_col", [P, VW])
        zeros = sb("zeros", [P, S])
        neg_half = sb("neg_half", [P, QT])
        gates_in = sb("gates_in", [P, 4])
        tg = sb("tg", [P, 4])
        first_w = ["wq0", "wk0", "wv0", "wo0"]
        later_w = ["uo_f", "wq1", "wk1", "wv1", "wo1"]
        w = {n: sb("w_" + n, [P, KT, D]) for n in first_w + later_w}
        col0 = ["bq0", "bk0", "bf", "bi", "bc", "in_c"]
        col1 = ["bq1", "bk1", "bq2", "bk2"]
        col = {n: sb("col_" + n, [P, KT]) for n in col0 + col1}
        row0 = ["bv0", "bo0"]
        row1 = ["bo_f", "bv1", "bo1", "bv2"]
        row = {n: sb("row_" + n, [P, D]) for n in row0 + row1}
        b_gate = sb("b_gate", [P, E])
        b_exp = sb("b_exp", [E, D])
        split_w = ["wf", "uf", "wi", "ui", "wc", "uc", "wo_f"]
        NEXP = KT * E * D
        NSPLIT = max(len(split_w) * KT * D, NEXP + 3 * KT * D + KT * E)
        parts_w = sb("parts_w", [P, 2, NSPLIT], F32R)

        def split_view(at, *shape):
            n = int(np.prod(shape))
            v = parts_w[:, :, at:at + n]
            if len(shape) == 2:
                return v.rearrange("p l (k o) -> p l k o", k=shape[0])
            return v.rearrange("p l (k e o) -> p l k e o", k=shape[0], e=shape[1])

        ws = {n: split_view(i * KT * D, KT, D) for i, n in enumerate(split_w)}
        w_exp = split_view(0, KT, E, D)
        for i, n in enumerate(("wq2", "wk2", "wv2")):
            ws[n] = split_view(NEXP + i * KT * D, KT, D)
        ws["w_gate"] = split_view(NEXP + 3 * KT * D, KT, E)

        x_in = sb("x_in", [P, QT, D])
        x_res = sb("x_res", [P, QT, D])
        ctx_t = sb("ctx_t", [P, KT, S2])
        stats = sb("stats", [P, QT, 6])
        mv = sb("mv", [P, QT, 2])
        var_eps = sb("var_eps", [P, QT])
        rstd = sb("rstd", [P, QT])
        stats1 = sb("stats1", [P, QT, 6])
        mv1 = sb("mv1", [P, QT, 2])
        var_eps1 = sb("var_eps1", [P, QT])
        rstd1 = sb("rstd1", [P, QT])
        xn = sb("xn", [P, QT, D])
        xt = sb("xt", [P, KT, S])
        turned_parts = sb("turned_parts", [P, 2, 2, KT, S], F32R)
        xt1, cell_parts = turned_parts[:, 0], turned_parts[:, 1]
        qhl = sb("qhl", [P, 2, KT, S], F32R)
        khl = sb("khl", [P, 2, KT, S], F32R)
        q_stack = sb("q_stack", [P, 2, PAIRS, S], F32R)
        k_stack = sb("k_stack", [P, 2, PAIRS, 2, S], F32R)
        vx = sb("vx", [P, 2, 2, H, VW])
        mask_i = sb("mask_i", [P, QT, S2], I32)
        mask_ti = sb("mask_ti", [P, S], I32)
        mask_q = sb("mask_q", [P, QT, S2], BF16)
        mask_k = sb("mask_k", [P, S], BF16)
        prob_k = sb("prob_k", [P, S])
        top = sb("top", [P, QT, H])
        top2 = sb("top2", [P, QT, H])
        shift_hl = sb("shift_hl", [P, QT, 2 * H], F32R)
        shift_t = sb("shift_t", [P, S], F32R)
        NPR = 4
        probs = sb("probs", [P, NPR, 2 * S])
        att_t = sb("att_t", [P, 4, S])
        rec = sb("rec", [P, QT, H])
        att = sb("att", [P, QT, D])
        att_n = sb("att_n", [P, KT, S])
        y = sb("y", [P, QT, D])
        y2 = sb("y2", [P, QT, D])
        xn1 = sb("xn1", [P, QT, D])
        cell = sb("cell", [P, KT, S])
        hx = sb("hx", [P, QT, D])
        x2, hx_in = xn1, hx
        cu = sb("cu", [P, QT, D])
        by_layer = sb("by_layer", [P, 5, KT * S])
        gf, gi, gc, ca, cb = (by_layer[:, i].rearrange("p (k t) -> p k t", k=KT) for i in range(5))
        probs_g = by_layer[:, 0:NPR]
        acc = [[by_layer[:, 2 * s + a].rearrange("p (t d) -> p t d", t=QT) for a in range(2)] for s in range(2)]
        ebias = by_layer[:, 4].rearrange("p (t d) -> p t d", t=QT)
        lg = sb("lg", [P, QT, E])
        nmx = sb("nmx", [P, QT])
        ge = sb("ge", [P, QT, E])
        gsum = sb("gsum", [P, QT])
        grec = sb("grec", [P, QT])
        cmp1 = sb("cmp1", [P, QT, E, E])
        cmp2 = sb("cmp2", [P, QT, E, E])
        rank = sb("rank", [P, QT, E])
        comb = sb("comb", [P, 2, QT, E])
        comb_t = sb("comb_t", [E, S])

        def bank(name, n=1):
            return ctx.enter_context(nc.psum_tensor(name, [P, n, 512], F32))
        work = bank("work", 2)
        score = bank("score", 2)
        o_ps = bank("o_ps", 2)
        dense = bank("dense", 2)

        NU = [PAIRS, PAIRS, 2 * PAIRS]
        first_in = sem("first_in")
        later_in = sem("later_in")
        stage_in = [sem("stage0_in"), sem("stage1_in")]
        stage_used = sem("stage_used")
        split_done = sem("split_done")
        const_ready = sem("const_ready")
        zeroed = sem("zeroed")
        ones_cleared = sem("ones_cleared")
        halved = sem("halved")
        gates_ready = sem("gates_ready")
        layer_done = sem("layer_done")
        cell_final = sem("cell_final")
        cu_ready = sem("cu_ready")
        dve_chain = sem("dve_chain")
        passed = sem("passed")
        x_loaded = signal("x_loaded", 16, 32, 16)
        ctx_loaded = signal("ctx_loaded", 16, 16, 0)
        mask_loaded = signal("mask_loaded", 32, 32, 0)
        prob_loaded = signal("prob_loaded", 0, 16, 0)
        res_loaded = signal("res_loaded", 16, 16, 16)
        parts_stored = signal("parts_stored", 64, 64, 64)
        stack_loaded = signal("stack_loaded", 192, 192, 192)
        y_stored = signal("y_stored", 16, 16, 16)
        hx_stored = signal("hx_stored", 16, 0, 0)
        x2_stored = signal("x2_stored", 0, 16, 0)
        pre_h = signal("pre_h", 0, 1, 0)
        tanh_h = signal("tanh_h", 0, 1, 0)
        x2_ready = signal("x2_ready", 0, 1, 0)
        var_ready = signal("var_ready", 1, 1, 1)
        rstd_ready = signal("rstd_ready", 1, 1, 1)
        xn_ready = signal("xn_ready", 1, 1, 1)
        mask_q_ready = signal("mask_q_ready", 1, 1, 0)
        mask_k_ready = signal("mask_k_ready", 1, 1, 0)
        xt_made = signal("xt_made", 1, 1, 1)
        xt_ready = signal("xt_ready", 1, 1, 1)
        xt_low = signal("xt_low", 0, 0, 1)
        q_made = signal("q_made", 1, 1, 1)
        k_made = signal("k_made", 1, 1, 1)
        v_made = signal("v_made", 1, 1, 1)
        qh_ready = signal("qh_ready", 2, 2, 2)
        kh_ready = signal("kh_ready", 2, 2, 2)
        ql_ready = signal("ql_ready", 2, 2, 2)
        kl_ready = signal("kl_ready", 2, 2, 2)
        v_ready = signal("v_ready", 1, 1, 1)
        tops_made = signal("tops_made", *NU)
        tops_read = signal("tops_read", *NU)
        shift_ready = signal("shift_ready", 1, 1, 1)
        shift_t_made = signal("shift_t_made", 1, 1, 1)
        shift_t_ready = signal("shift_t_ready", 1, 1, 1)
        raw_made = signal("raw_made", 8, 0, 0)
        clipped = signal("clipped", 8, 0, 0)
        scores_made = signal("scores_made", *NU)
        probs_ready = signal("probs_ready", *NU)
        probs_g_ready = signal("probs_g_ready", 0, NU[1], 0)
        pv_made = signal("pv_made", *NU)
        att_t_ready = signal("att_t_ready", 2, 2, 2)
        att_made = signal("att_made", 2, 2, 2)
        att_ready = signal("att_ready", 2, 2, 2)
        att_n_made = signal("att_n_made", 1, 1, 0)
        att_n_ready = signal("att_n_ready", 1, 1, 0)
        y_made = signal("y_made", 1, 1, 0)
        y_read = signal("y_read", 1, 1, 0)
        y_ready = signal("y_ready", 1, 1, 1)
        var1_ready = signal("var1_ready", 1, 0, 0)
        rstd1_ready = signal("rstd1_ready", 1, 0, 0)
        xn1_ready = signal("xn1_ready", 1, 0, 0)
        xt1_made = signal("xt1_made", 1, 0, 0)
        xt1_ready = signal("xt1_ready", 1, 0, 0)
        xt1_low = signal("xt1_low", 1, 0, 0)
        gate_made = signal("gate_made", 3, 0, 0)
        gate_ready = signal("gate_ready", 3, 0, 0)
        cell_ready = signal("cell_ready", 1, 0, 0)
        hx_made = signal("hx_made", 1, 0, 0)
        hx_ready = signal("hx_ready", 1, 0, 0)
        logits_made = signal("logits_made", 0, 0, 1)
        logits_ready = signal("logits_ready", 0, 0, 1)
        gexp_ready = signal("gexp_ready", 0, 0, 2)
        comb_ready = signal("comb_ready", 0, 0, 1)
        comb_t_made = signal("comb_t_made", 0, 0, 1)
        comb_t_ready = signal("comb_t_ready", 0, 0, 1)
        ebias_made = signal("ebias_made", 0, 0, 1)
        ebias_ready = signal("ebias_ready", 0, 0, 1)
        exp_made = signal("exp_made", 0, 0, 8)
        exp_read = signal("exp_read", 0, 0, 8)

        KQ = [S2, S2, P]
        KN = [S2, S2, S]

        def tokens(ap):
            return ap.rearrange("(t p) d -> p t d", p=P)

        FIRST = [4, 2, 2]
        STEPS = B + 4

        def steps(eng, L, body):
            def step(t, slot):
                def within(b):
                    return b if not isinstance(b, int) or 0 <= b < B else None
                body(slot, within(t), within(t + 1), within(t - 1), within(t - 2) if L == 0 else None, within(t + 2),
                     t + L * STEPS + 2)

            for t in range(-2, FIRST[L]):
                step(t, t % 2)
            with eng.Fori(FIRST[L], B - 3, 2) as t:
                step(t, 0)
                step(t + 1, 1)
            for t in range(B - 2, B + 2):
                step(t, t % 2)

        def layer_end(eng, L):
            eng.drain().then_inc(layer_done, 1)
            eng.wait_ge(layer_done, 5 * (L + 1))

        def weight(n):
            return io[n].rearrange("(k p) o -> p k o", p=P)

        first = [(ident[:], io["ident"])]
        first += [(w[n][:], weight(n)) for n in first_w]
        first += [(col[n][:], io[n]) for n in col0] + [(row[n][:], io[n].partition_broadcast(P)) for n in row0]
        first += [(gates_in[:, 0:2], io["g_xattn"].partition_broadcast(P)),
                  (gates_in[:, 2:4], io["g_ffn"].partition_broadcast(P))]
        later = [(w[n][:], weight(n)) for n in later_w]
        later += [(col[n][:], io[n]) for n in col1] + [(row[n][:], io[n].partition_broadcast(P)) for n in row1]
        later += [(b_gate[:], io["b_gate"].partition_broadcast(P)), (b_exp[:], io["b_exp"]),
                  (earlier[:].rearrange("p a b -> p (a b)"), io["earlier"].partition_broadcast(P))]
        NREADY = 6

        stage = [probs[:].rearrange("p a b -> p (a b)"), by_layer[:, 0:4].rearrange("p a b -> p (a b)")]
        NW = KT * D

        def flat(part, at, n):
            return parts_w[:, part, at:at + n]

        rounds = [[], [], []]
        rounds[0].append(([(0, H * P, io["sel"])], (sel[:].rearrange("p h k -> p (h k)"), None, H * P)))
        for lo in (0, 4):
            some = split_w[lo:lo + 4]
            rounds[0].append(([(i * NW, NW, weight(n)) for i, n in enumerate(some)],
                              (flat(0, lo * NW, len(some) * NW), flat(1, lo * NW, len(some) * NW), len(some) * NW)))
        for k in range(KT):
            rounds[2].append(([(0, E * D, io["w_exp"][:, k * P:(k + 1) * P, :].rearrange("e p o -> p e o"))],
                              (flat(0, k * E * D, E * D), flat(1, k * E * D, E * D), E * D)))
        rest = [(i * NW, NW, weight(n)) for i, n in enumerate(("wq2", "wk2", "wv2"))]
        rest.append((3 * NW, KT * E, weight("w_gate")))
        rounds[2].append((rest, (flat(0, NEXP, 3 * NW + KT * E), flat(1, NEXP, 3 * NW + KT * E), 3 * NW + KT * E)))
        numbered = [(L, r) for L in (0, 2) for r in rounds[L]]
        loaded = [sum(16 * len(r[0]) for _, r in numbered[i % 2:i + 1:2]) for i in range(len(numbered))]

        def load_rounds(eng, L, only=None):
            for i, (of, (loads, _)) in enumerate(numbered):
                if of != L:
                    continue
                if i >= 2:
                    eng.wait_ge(stage_used, i - 1)
                for at, n, src in loads:
                    dst = stage[i % 2][:, at:at + n]
                    if len(src.shape) == 3:
                        dst = dst.rearrange("p (k o) -> p k o", k=src.shape[1])
                    eng.dma_start(dst, src).then_inc(stage_in[i % 2], 16)

        block = ctx.enter_context(nc.Block())

        @block.sync
        def _(sp):
            for dst, src in first:
                sp.dma_start(dst, src).then_inc(first_in, 16)

            def store_parts(L, n, part, hl, ready, dst, N):
                sp.wait_ge(ready.sem, ready.at(L, n))
                sp.dma_start(dst[n, part].rearrange("(m p) t -> p m t", p=P),
                             hl[:, part, :, 0:N].bitcast(F32)).then_inc(parts_stored.sem, 16)

            def load_stacks(L, slot, n):
                sp.wait_ge(parts_stored.sem, parts_stored.at(L, n))
                sp.wait_ge(scores_made.sem, scores_made.at(L, n - 2))
                for stack, src, order in ((q_stack, q_d[L], (0, 0, 1)), (k_stack, k_d[L], (0, 1, 0))):
                    for par in range(2):
                        for i, part in enumerate(order):
                            rows = slice(64 * par + HD * i, 64 * par + HD * i + HD)
                            dst = stack[rows, slot] if stack is q_stack else stack[rows, slot, :, par, 0:KN[L]]
                            sp.dma_start(dst.bitcast(F32),
                                         src[n, part].rearrange("(j a d) t -> a d j t", a=2, d=HD)[par])\
                              .then_inc(stack_loaded.sem, 16)

            def store_y(L, l):
                sp.wait_ge(y_ready.sem, y_ready.at(L, l))
                sp.dma_start(tokens([x1_d, x3_d, out][L][l]), y[:]).then_inc(y_stored.sem, 16)

            def body(L, slot, m, n, l, r, p):
                if n is not None:
                    for part, ready in ((0, kh_ready), (1, kl_ready)):
                        store_parts(L, n, part, khl, ready, k_d[L], KN[L])
                    for part, ready in ((0, qh_ready), (1, ql_ready)):
                        store_parts(L, n, part, qhl, ready, q_d[L], S)
                if l is not None and L < 2:
                    store_y(L, l)
                if n is not None:
                    load_stacks(L, 1 - slot, n)
                if l is not None and L == 2:
                    store_y(L, l)
                if r is not None:
                    sp.wait_ge(hx_ready.sem, hx_ready.at(0, r))
                    sp.dma_start(tokens(hx_d[r]), hx[:]).then_inc(hx_stored.sem, 16)
                if L == 1 and p is not None:
                    sp.wait_ge(x2_ready.sem, x2_ready.at(1, p))
                    sp.dma_start(tokens(x2_d[p]), x2[:]).then_inc(x2_stored.sem, 16)

            for L in range(3):
                steps(sp, L, lambda slot, m, n, l, r, p, number: body(L, slot, m, n, l, r, p))
                sp.wait_ge(y_stored.sem, y_stored.at(L, B - 1))
                if L == 0:
                    sp.wait_ge(hx_stored.sem, hx_stored.at(0, B - 1))
                if L == 1:
                    sp.wait_ge(x2_stored.sem, x2_stored.at(1, B - 1))
                if L < 2:
                    layer_end(sp, L)

        @block.gpsimd
        def _(pool):
            pool.memset(neg_half[:], -0.5).then_inc(const_ready, 1)
            pool.memset(ones_col[:], 0.0).then_inc(ones_cleared, 1)
            pool.wait_ge(ones_cleared, 1)
            pool.memset(ones_col[:, HD:HD + 1], 1.0).then_inc(const_ready, 1)

            def load_x(L, p):
                if L == 1:
                    pool.wait_ge(x2_ready.sem, x2_ready.at(1, p - 1))
                    pool.sem_inc(passed, 1)
                    pool.dma_start(hx_in[:], tokens(hx_d[p])).then_inc(x_loaded.sem, 16)
                else:
                    pool.wait_ge(xn_ready.sem, xn_ready.at(L, p - 1))
                pool.sem_inc(passed, 1)
                pool.dma_start(x_in[:], tokens([io["x"], x1_d, x3_d][L][p])).then_inc(x_loaded.sem, 16)

            def load_ctx(L, n):
                pool.wait_ge(v_made.sem, v_made.at(L, n - 1))
                pool.sem_inc(passed, 1)
                pool.dma_start(ctx_t[:], io["ctx_t"][n].rearrange("(k p) t -> p k t", p=P)).then_inc(ctx_loaded.sem, 16)

            def load_mask(L, n):
                pool.wait_ge(mask_k_ready.sem, mask_k_ready.at(L, n - 1))
                pool.wait_ge(mask_q_ready.sem, mask_q_ready.at(L, n - 1))
                pool.sem_inc(passed, 1)
                pool.dma_start(mask_i[:], io[f"mask{L}"][n].rearrange("(t p) k -> p t k", p=P))\
                    .then_inc(mask_loaded.sem, 16)
                pool.dma_start(mask_ti[0:S2, :], io[f"mask{L}_t"][n]).then_inc(mask_loaded.sem, 16)

            def body(L, slot, m, n, l, r, p, ahead):
                if L == 0 and l is not None:
                    pool.wait_ge(var1_ready.sem, var1_ready.at(0, l))
                    pool.tensor_tensor(rstd1[:], var_eps1[:], neg_half[:], ALU.pow).then_inc(rstd1_ready.sem, 1)
                if m is not None:
                    pool.wait_ge(y_ready.sem, y_ready.at(L, m - 1))
                    pool.sem_inc(passed, 1)
                    if L == 1:
                        pool.wait_ge(x2_stored.sem, x2_stored.at(1, m))
                        pool.sem_inc(passed, 1)
                    pool.dma_start(x_res[:], tokens([io["x"], x2_d, x3_d][L][m])).then_inc(res_loaded.sem, 16)
                if L < 2 and n is not None:
                    pool.wait_ge(mask_loaded.sem, mask_loaded.at(L, n))
                    pool.sem_inc(passed, 1)
                    pool.wait_ge(tops_made.sem, tops_made.at(L, n - 1))
                    pool.sem_inc(passed, 1)
                    pool.tensor_scalar(mask_q[:], mask_i[:], MASKED, -MASKED, ALU.mult, ALU.add)\
                        .then_inc(mask_q_ready.sem, 1)
                if p is not None:
                    pool.wait_ge(var_ready.sem, var_ready.at(L, p))
                    pool.tensor_tensor(rstd[:], var_eps[:], neg_half[:], ALU.pow).then_inc(rstd_ready.sem, 1)
                if L < 2 and n is not None:
                    pool.wait_ge(scores_made.sem, scores_made.at(L, n - 1))
                    pool.sem_inc(passed, 1)
                    pool.tensor_scalar(mask_k[0:S2, :], mask_ti[0:S2, :], MASKED, -MASKED, ALU.mult, ALU.add)\
                        .then_inc(mask_k_ready.sem, 1)
                if L == 1 and n is not None:
                    pool.wait_ge(probs_g_ready.sem, probs_g_ready.at(1, n - 1))
                    pool.sem_inc(passed, 1)
                    pool.dma_start(prob_k[0:S2, :], io["prob_t"][n]).then_inc(prob_loaded.sem, 16)
                if L < 2 and p is not None:
                    load_mask(L, p)
                    load_ctx(L, p)
                if ahead is not None:
                    load_x(L, ahead)

            def step(L, slot, m, n, l, r, p):
                ahead = None if p is None or (isinstance(p, int) and p == B - 1) else p + 1
                body(L, slot, m, n, l, r, p, ahead)

            load_rounds(pool, 0)
            for L in range(3):
                if L == 2:
                    load_rounds(pool, 2)
                load_x(L, 0)
                for t in range(-2, FIRST[L]):
                    step(L, t % 2, *[b if 0 <= b < B else None for b in (t, t + 1, t - 1, t - 2, t + 2)])
                with pool.Fori(FIRST[L], B - 3) as t:
                    step(L, 0, t, t + 1, t - 1, t - 2, t + 2)
                for t in range(B - 3, B + 2):
                    step(L, t % 2, *[b if 0 <= b < B else None for b in (t, t + 1, t - 1, t - 2, t + 2)])
                if L < 2:
                    layer_end(pool, L)

        @block.scalar
        def _(act):
            for dst, src in later:
                act.dma_start(dst, src).then_inc(later_in, 16)
            act.wait_ge(first_in, 16 * len(first))
            act.activation(tg[:], gates_in[:], ACT.Tanh).then_inc(gates_ready, 1)
            act.wait_ge(const_ready, NREADY)
            for k in range(KT):
                act.activation(cell[:, k, :], zeros[:], ACT.Identity, bias=col["in_c"][:, k:k + 1])\
                    .then_inc(gates_ready, 1)

            def high(L, n, made, ready, part, bk, b, N):
                act.wait_ge(made.sem, made.at(L, n))
                act.wait_ge(parts_stored.sem, parts_stored.at(L, n - 1))
                for k in range(KT):
                    act.activation(part[:, 0, k, 0:N], work[:, bk, k * S:k * S + N], ACT.Identity,
                                   bias=col[f"{b}{L}"][:, k:k + 1]).then_inc(ready.sem, 1)

            def gate(r, g):
                dst, b, s, bk = ((gf, "bf", 0.5, 1), (gi, "bi", 0.5, 0), (gc, "bc", 1.0, 1))[g]
                act.wait_ge(gate_made.sem, gate_made.at(0, r, g + 1))
                if g == 0:
                    act.wait_ge(cell_ready.sem, cell_ready.at(0, r - 1))
                for k in range(KT):
                    ins = act.activation(dst[:, k, :], dense[:, bk, k * S:(k + 1) * S], ACT.Tanh,
                                         bias=col[b][:, k:k + 1], scale=s)
                ins.then_inc(gate_ready.sem, 1)

            def hidden(r):
                act.wait_ge(hx_made.sem, hx_made.at(0, r))
                act.wait_ge(hx_stored.sem, hx_stored.at(0, r - 1))
                act.activation(hx[:], dense[:, 0, :], ACT.Copy).then_inc(hx_ready.sem, 1)

            def exponential(L, m, u):
                act.wait_ge(scores_made.sem, scores_made.at(L, m, u + 1))
                if u >= NPR:
                    act.wait_ge(pv_made.sem, pv_made.at(L, m, u - NPR + 1))
                act.activation(probs[0:KQ[L], u % NPR, :], score[0:KQ[L], u % 2, :], ACT.Exp, scale=SCALE)\
                    .then_inc(probs_ready.sem, 1)

            def body(L, slot, m, n, l, r, p):
                if n is not None:
                    act.wait_ge(xt_made.sem, xt_made.at(L, n))
                    dst = xt[:] if L < 2 else turned_parts[:, 1 - slot, 0]
                    if L == 2:
                        act.wait_ge(exp_made.sem, exp_made.at(2, n - 2))
                    act.activation(dst, work[:, 0, :], ACT.Copy).then_inc(xt_ready.sem, 1)
                if l is not None and L < 2:
                    act.wait_ge(att_n_made.sem, att_n_made.at(L, l))
                    act.activation(att_n[:], work[:, 1, :], ACT.Copy).then_inc(att_n_ready.sem, 1)
                if r is not None:
                    act.wait_ge(xt1_made.sem, xt1_made.at(0, r))
                    act.activation(xt1[:, 0], dense[:, 0, :], ACT.Copy).then_inc(xt1_ready.sem, 1)
                if n is not None:
                    if L < 2:
                        high(L, n, k_made, kh_ready, khl, 0, "bk", KN[L])
                        high(L, n, q_made, qh_ready, qhl, 1, "bq", S)
                    else:
                        high(L, n, q_made, qh_ready, qhl, 1, "bq", S)
                        high(L, n, k_made, kh_ready, khl, 0, "bk", KN[L])
                if r is not None:
                    gate(r, 0)
                if L == 1 and p is not None:
                    act.wait_ge(pre_h.sem, pre_h.at(1, p))
                    act.activation(hx_in[:], hx_in[:], ACT.Tanh).then_inc(tanh_h.sem, 1)
                if m is not None:
                    act.wait_ge(shift_t_made.sem, shift_t_made.at(L, m))
                    act.activation(shift_t[0:2 * H, :], work[0:2 * H, 1, 0:S], ACT.Copy).then_inc(shift_t_ready.sem, 1)
                for u in range(NU[L]):
                    if m is not None:
                        exponential(L, m, u)
                    if r is not None:
                        if u == 1:
                            gate(r, 1)
                        if u == 3:
                            gate(r, 2)
                        if u == 5:
                            hidden(r)
                    if L == 2 and n is not None:
                        if u == 7:
                            act.wait_ge(logits_ready.sem, logits_ready.at(2, n))
                            for t in range(QT):
                                act.activation(ge[:, t, :], lg[:, t, :], ACT.Exp, bias=nmx[:, t:t + 1],
                                               accum_out=gsum[:, t:t + 1]).then_inc(gexp_ready.sem, 1)
                        if u == 15:
                            act.wait_ge(comb_t_made.sem, comb_t_made.at(2, n))
                            act.activation(comb_t[:], work[0:E, 1, 0:S], ACT.Copy).then_inc(comb_t_ready.sem, 1)
                if m is not None:
                    act.wait_ge(pv_made.sem, pv_made.at(L, m))
                    if L == 2:
                        act.wait_ge(att_made.sem, att_made.at(2, m - 1))
                    for g in range(2):
                        act.activation(att_t[:, 2 * g:2 * g + 2, :], o_ps[:, g, :], ACT.Copy)\
                            .then_inc(att_t_ready.sem, 1)
                if L == 2 and n is not None:
                    act.wait_ge(ebias_made.sem, ebias_made.at(2, n))
                    act.wait_ge(exp_read.sem, exp_read.at(2, n - 1))
                    act.activation(ebias, work[:, 1, :], ACT.Copy).then_inc(ebias_ready.sem, 1)

            for L in range(3):
                steps(act, L, lambda slot, m, n, l, r, p, number: body(L, slot, m, n, l, r, p))
                if L < 2:
                    layer_end(act, L)

        @block.vector
        def _(dve):
            chain = Chain(dve, dve_chain)
            link = chain.link
            dve.memset(zeros[:], 0.0).then_inc(const_ready, 1)
            dve.memset(q_stack[:].bitcast(F32), 0.0).then_inc(zeroed, 1)
            dve.memset(k_stack[:].bitcast(F32), 0.0).then_inc(zeroed, 1)
            dve.memset(vx[:], 0.0).then_inc(zeroed, 1)
            dve.memset(shift_t[:].bitcast(F32), 0.0).then_inc(zeroed, 1)
            dve.wait_ge(zeroed, 4)
            dve.memset(vx[:, :, :, :, HD:HD + 1], 1.0).then_inc(const_ready, 1)
            dve.wait_ge(first_in, 16 * len(first))
            dve.tensor_copy(identb[:], ident[:]).then_inc(const_ready, 1)
            for n in ("bf", "bi"):
                dve.tensor_scalar(col[n][:], col[n][:], 0.5, None, ALU.mult).then_inc(halved, 1)
            dve.wait_ge(halved, 2)
            dve.tensor_copy(nmx[:], zeros[:, 0:QT]).then_inc(const_ready, 1)

            def split_rounds(L):
                for i, (of, (_, (high, low, n))) in enumerate(numbered):
                    if of != L:
                        continue
                    dve.wait_ge(stage_in[i % 2], loaded[i])
                    src = stage[i % 2][:, 0:n]
                    ins = dve.tensor_copy(high, src)
                    ins.then_inc(split_done, 1)
                    dve.wait_ge(split_done, i + 1)
                    if low is not None:
                        ins = dve.tensor_tensor(low, src, high.bitcast(F32), ALU.subtract)
                    else:
                        ins = dve.tensor_copy(nmx[:], zeros[:, 0:QT])
                    ins.then_inc(stage_used, 1)

            split_rounds(0)
            dve.wait_ge(gates_ready, 1 + KT)
            dve.tensor_copy(cell_parts[:, 0], cell[:]).then_inc(halved, 1)
            dve.wait_ge(halved, 3)
            dve.tensor_tensor(cell_parts[:, 1], cell[:], cell_parts[:, 0].bitcast(F32), ALU.subtract)\
                .then_inc(halved, 1)

            def spread(st, mean_var, var, src):
                ks = [link(dve.bn_stats(st[:, t, :], src[:, t, :])) for t in range(QT)]
                for t in range(QT):
                    dve.wait_ge(dve_chain, chain.at(ks[t]))
                    dve.sem_inc(passed, 1)
                    last = link(dve.bn_aggr(mean_var[:, t, :], st[:, t, :]))
                dve.wait_ge(dve_chain, chain.at(last))
                return dve.tensor_scalar(var[:], mean_var[:, :, 1], EPS, None, ALU.add)

            def normal(dst, src, mean_var, scale):
                for t in range(QT):
                    ins = dve.tensor_scalar(dst[:, t, :], src[:, t, :], mean_var[:, t, 0:1], scale[:, t:t + 1],
                                            ALU.subtract, ALU.mult)
                return ins

            def low(L, n, made, high, ready, part, bk, b, N):
                dve.wait_ge(high.sem, high.at(L, n))
                for k in range(KT):
                    dve.scalar_tensor_tensor(part[:, 1, k, 0:N], work[:, bk, k * S:k * S + N],
                                             col[f"{b}{L}"][:, k:k + 1], part[:, 0, k, 0:N].bitcast(F32),
                                             ALU.add, ALU.subtract).then_inc(ready.sem, 1)

            def queries_low(L, n):
                low(L, n, q_made, qh_ready, ql_ready, qhl, 1, "bq", S)

            def keys_low(L, n):
                low(L, n, k_made, kh_ready, kl_ready, khl, 0, "bk", KN[L])

            def values(L, slot, n):
                dve.wait_ge(v_made.sem, v_made.at(L, n))
                dve.wait_ge(pv_made.sem, pv_made.at(L, n - 2))
                for t in range(1 if L < 2 else 2):
                    ins = dve.tensor_tensor(
                        vx[0:KQ[L], slot, t, :, 0:HD],
                        work[0:KQ[L], 0, t * D:(t + 1) * D].rearrange("p (h d) -> p h d", h=H),
                        row[f"bv{L}"][0:KQ[L], :].rearrange("p (h d) -> p h d", h=H), ALU.add)
                ins.then_inc(v_ready.sem, 1)

            def maximum(L, m, u):
                heads, keys = (4, S2) if L < 2 else (2, S)
                t, j = divmod(u, H // heads)
                dve.wait_ge(tops_made.sem, tops_made.at(L, m, u + 1))
                dve.tensor_reduce(top[:, t, heads * j:heads * (j + 1)],
                                  score[:, u % 2, 0:heads * keys].rearrange("p (h k) -> p h k", h=heads),
                                  AX.X, ALU.max).then_inc(tops_read.sem, 1)

            def shift(L, m):
                dve.wait_ge(tops_read.sem, tops_read.at(L, m))
                if L == 0:
                    link(dve.tensor_scalar(top2[:], top[:], -1.0, CLIP, ALU.mult, ALU.min))
                    dve.wait_ge(dve_chain, chain.at())
                    link(dve.tensor_scalar(top2[:], top2[:], -CLIP, None, ALU.max))
                else:
                    link(dve.tensor_scalar(top2[:], top[:], -1.0, None, ALU.mult))
                dve.wait_ge(shift_t_made.sem, shift_t_made.at(L, m - 1))
                dve.wait_ge(dve_chain, chain.at())
                link(dve.tensor_copy(shift_hl[:, :, 0:H], top2[:]))
                dve.wait_ge(dve_chain, chain.at())
                dve.tensor_tensor(shift_hl[:, :, H:2 * H], top2[:], shift_hl[:, :, 0:H].bitcast(F32),
                                  ALU.subtract).then_inc(shift_ready.sem, 1)

            def clip(m, u):
                dve.wait_ge(raw_made.sem, raw_made.at(0, m, u + 1))
                dve.tensor_scalar(score[0:S2, u % 2, :], score[0:S2, u % 2, :], CLIP, -CLIP,
                                  ALU.min, ALU.max).then_inc(clipped.sem, 1)

            def group(m, u):
                dve.wait_ge(probs_ready.sem, probs_ready.at(1, m, u + 1))
                if u == 0:
                    dve.wait_ge(prob_loaded.sem, prob_loaded.at(1, m))
                if u >= NPR:
                    dve.wait_ge(pv_made.sem, pv_made.at(1, m, u - NPR + 1))
                dve.tensor_tensor(probs_g[0:S2, u % NPR, :].rearrange("p (a q) -> p a q", a=2),
                                  probs[0:S2, u % NPR, :].rearrange("p (a q) -> p a q", a=2),
                                  prob_k[0:S2, :].unsqueeze(1).to_broadcast([S2, 2, S]),
                                  ALU.mult).then_inc(probs_g_ready.sem, 1)

            def attended(L, l):
                for t in range(QT):
                    dve.wait_ge(att_made.sem, att_made.at(L, l, t + 1))
                    rows = dense[:, t, :].rearrange("p (h c) -> p h c", h=H)
                    link(dve.reciprocal(rec[:, t, :], rows[:, :, HD]))
                    dve.wait_ge(dve_chain, chain.at())
                    dve.tensor_tensor(att[:, t, :].rearrange("p (h d) -> p h d", h=H), rows[:, :, 0:HD],
                                      rec[:, t, :].unsqueeze(2).to_broadcast([P, H, HD]), ALU.mult)\
                        .then_inc(att_ready.sem, 1)

            def add_bias(L, l):
                dve.wait_ge(y_made.sem, y_made.at(L, l))
                dve.tensor_tensor(y2[:], work[:, 1, :].rearrange("p (t d) -> p t d", t=QT),
                                  row[f"bo{L}"][:].unsqueeze(1).to_broadcast([P, QT, D]), ALU.add)\
                    .then_inc(y_read.sem, 1)

            def add_rows(L, l):
                dve.wait_ge(y_read.sem, y_read.at(L, l))
                dve.wait_ge(res_loaded.sem, res_loaded.at(L, l))
                dve.wait_ge(y_stored.sem, y_stored.at(L, l - 1))
                dve.scalar_tensor_tensor(y[:], y2[:], tg[:, L:L + 1], x_res[:], ALU.mult, ALU.add)\
                    .then_inc(y_ready.sem, 1)
                if L == 0:
                    dve.wait_ge(y_ready.sem, y_ready.at(0, l))
                    spread(stats1, mv1, var_eps1, y).then_inc(var1_ready.sem, 1)

            def recur(r):
                dve.wait_ge(gate_ready.sem, gate_ready.at(0, r, 1))
                link(dve.scalar_tensor_tensor(ca[:], gf[:], 1.0, cell[:], ALU.add, ALU.mult))
                dve.wait_ge(gate_ready.sem, gate_ready.at(0, r, 3))
                link(dve.scalar_tensor_tensor(cb[:], gi[:], 1.0, gc[:], ALU.add, ALU.mult))
                dve.wait_ge(dve_chain, chain.at())
                link(dve.tensor_tensor(ca[:], ca[:], cb[:], ALU.add))
                dve.wait_ge(dve_chain, chain.at())
                link(dve.tensor_scalar(cell[:], ca[:], 0.5, None, ALU.mult))
                dve.wait_ge(dve_chain, chain.at())
                link(dve.tensor_copy(cell_parts[:, 0], cell[:]))
                dve.wait_ge(dve_chain, chain.at())
                dve.tensor_tensor(cell_parts[:, 1], cell[:], cell_parts[:, 0].bitcast(F32), ALU.subtract)\
                    .then_inc(cell_ready.sem, 1)

            def before_tanh(p):
                dve.wait_ge(x_loaded.sem, x_loaded.at(1, p))
                dve.tensor_tensor(hx_in[:], hx_in[:], cu[:], ALU.add).then_inc(pre_h.sem, 1)

            def stats_of(L, p):
                dve.wait_ge(x_loaded.sem, x_loaded.at(L, p))
                if L == 1:
                    dve.wait_ge(tanh_h.sem, tanh_h.at(1, p))
                    dve.wait_ge(x2_stored.sem, x2_stored.at(1, p - 1))
                    dve.scalar_tensor_tensor(x2[:], hx_in[:], tg[:, 2:3], x_in[:], ALU.mult, ALU.add)\
                        .then_inc(x2_ready.sem, 1)
                    dve.wait_ge(x2_ready.sem, x2_ready.at(1, p))
                spread(stats, mv, var_eps, x2 if L == 1 else x_in).then_inc(var_ready.sem, 1)

            def normalised(L, p):
                dve.wait_ge(rstd_ready.sem, rstd_ready.at(L, p))
                dve.wait_ge(xt_made.sem, xt_made.at(L, p - 1))
                normal(xn, x2 if L == 1 else x_in, mv, rstd).then_inc(xn_ready.sem, 1)

            def cross_body(L, slot, m, n, l, r, p):
                for u in range(8):
                    if m is not None:
                        maximum(L, m, u)
                    if u == 1 and l is not None:
                        attended(L, l)
                    if u == 5 and r is not None:
                        dve.wait_ge(xt1_ready.sem, xt1_ready.at(0, r))
                        dve.tensor_tensor(xt1[:, 1], dense[:, 0, :].rearrange("p (k t) -> p k t", k=KT),
                                          xt1[:, 0].bitcast(F32), ALU.subtract).then_inc(xt1_low.sem, 1)
                if m is not None:
                    shift(L, m)
                if l is not None:
                    add_bias(L, l)
                if n is not None:
                    keys_low(L, n)
                if l is not None:
                    add_rows(L, l)
                if n is not None:
                    queries_low(L, n)
                    values(L, 1 - slot, n)
                if L == 1 and p is not None:
                    before_tanh(p)
                for u in range(8):
                    if m is not None:
                        if L == 0:
                            clip(m, u)
                        else:
                            group(m, u)
                    if u == 2 and L == 0 and l is not None:
                        dve.wait_ge(rstd1_ready.sem, rstd1_ready.at(0, l))
                        dve.wait_ge(xt1_made.sem, xt1_made.at(0, l - 1))
                        normal(xn1, y, mv1, rstd1).then_inc(xn1_ready.sem, 1)
                if p is not None:
                    stats_of(L, p)
                if r is not None:
                    recur(r)
                if p is not None:
                    normalised(L, p)

            def expert(slot, m, u):
                pair, t = divmod(u, 2)
                dve.wait_ge(exp_made.sem, exp_made.at(2, m, u + 1))
                if pair > 0:
                    dve.wait_ge(exp_read.sem, exp_read.at(2, m, u - 1))
                for a in range(2):
                    e = 2 * pair + a
                    src = dense[:, t, a * D:(a + 1) * D]
                    c = comb[:, slot, t, e:e + 1]
                    if pair == 0 and a == 0:
                        dve.wait_ge(ebias_ready.sem, ebias_ready.at(2, m))
                        ins = dve.scalar_tensor_tensor(acc[slot][a][:, t, :], src, c, ebias[:, t, :],
                                                       ALU.mult, ALU.add)
                    elif pair == 0:
                        ins = dve.tensor_scalar(acc[slot][a][:, t, :], src, c, None, ALU.mult)
                    else:
                        ins = dve.scalar_tensor_tensor(acc[slot][a][:, t, :], src, c, acc[slot][a][:, t, :],
                                                       ALU.mult, ALU.add)
                ins.then_inc(exp_read.sem, 1)

            def layer_output(slot, l):
                dve.wait_ge(exp_read.sem, exp_read.at(2, l))
                dve.wait_ge(att_ready.sem, att_ready.at(2, l))
                a, b = acc[slot]
                link(dve.tensor_tensor(a, a, b, ALU.add))
                dve.wait_ge(dve_chain, chain.at())
                link(dve.tensor_tensor(a, a, att[:], ALU.add))
                dve.wait_ge(dve_chain, chain.at())
                dve.wait_ge(res_loaded.sem, res_loaded.at(2, l))
                dve.wait_ge(y_stored.sem, y_stored.at(2, l - 1))
                dve.scalar_tensor_tensor(y[:], a, tg[:, 3:4], x_res[:], ALU.mult, ALU.add).then_inc(y_ready.sem, 1)

            def logits(n):
                dve.wait_ge(logits_made.sem, logits_made.at(2, n))
                link(dve.tensor_tensor(lg[:], work[:, 1, 0:QT * E].rearrange("p (t e) -> p t e", t=QT),
                                       b_gate[:].unsqueeze(1).to_broadcast([P, QT, E]), ALU.add))
                dve.wait_ge(dve_chain, chain.at())
                dve.tensor_reduce(nmx[:], lg[:], AX.X, ALU.max, negate=True).then_inc(logits_ready.sem, 1)

            def combine(slot, n):
                dve.wait_ge(gexp_ready.sem, gexp_ready.at(2, n))
                link(dve.reciprocal(grec[:], gsum[:]))
                mine = ge[:].unsqueeze(3).to_broadcast([P, QT, E, E])
                other = ge[:].unsqueeze(2).to_broadcast([P, QT, E, E])
                k = link(dve.tensor_tensor(cmp1[:], other, mine, ALU.is_equal))
                link(dve.tensor_tensor(cmp2[:], other, mine, ALU.is_gt))
                dve.wait_ge(dve_chain, chain.at(k))
                link(dve.tensor_tensor(cmp1[:], cmp1[:], earlier[:].unsqueeze(1).to_broadcast([P, QT, E, E]), ALU.mult))
                dve.wait_ge(dve_chain, chain.at())
                link(dve.tensor_tensor(cmp1[:], cmp1[:], cmp2[:], ALU.add))
                dve.wait_ge(dve_chain, chain.at())
                link(dve.tensor_reduce(rank[:], cmp1[:], AX.X, ALU.add))
                dve.wait_ge(dve_chain, chain.at())
                link(dve.scalar_tensor_tensor(comb[:, slot], rank[:], 2.0, ge[:], ALU.is_lt, ALU.mult))
                dve.wait_ge(dve_chain, chain.at())
                dve.tensor_tensor(comb[:, slot], comb[:, slot], grec[:].unsqueeze(2).to_broadcast([P, QT, E]),
                                  ALU.mult).then_inc(comb_ready.sem, 1)

            def experts_body(L, slot, m, n, l, r, p):
                other = 1 - slot
                for u in range(16):
                    if m is not None:
                        maximum(2, m, u)
                    if u == 1 and l is not None:
                        attended(2, l)
                    if u == 5 and n is not None:
                        dve.wait_ge(xt_ready.sem, xt_ready.at(2, n))
                        dve.tensor_tensor(turned_parts[:, other, 1], work[:, 0, :].rearrange("p (k t) -> p k t", k=KT),
                                          turned_parts[:, other, 0].bitcast(F32), ALU.subtract).then_inc(xt_low.sem, 1)
                    if m is not None and u in (7, 9):
                        expert(slot, m, (u - 7) // 2)
                    if n is not None and u == 11:
                        queries_low(2, n)
                    if n is not None and u == 13:
                        keys_low(2, n)
                if m is not None:
                    shift(2, m)
                    expert(slot, m, 2)
                    expert(slot, m, 3)
                if n is not None:
                    values(2, other, n)
                if l is not None:
                    layer_output(other, l)
                if n is not None:
                    logits(n)
                if m is not None:
                    expert(slot, m, 4)
                    expert(slot, m, 5)
                if n is not None:
                    combine(other, n)
                if m is not None:
                    expert(slot, m, 6)
                if p is not None:
                    stats_of(2, p)
                if m is not None:
                    expert(slot, m, 7)
                if p is not None:
                    normalised(2, p)

            def body(L, slot, m, n, l, r, p, number):
                chain.step(number)
                (cross_body if L < 2 else experts_body)(L, slot, m, n, l, r, p)
                chain.close()

            for L in range(3):
                if L == 2:
                    split_rounds(2)
                steps(dve, L, lambda slot, m, n, l, r, p, number: body(L, slot, m, n, l, r, p, number))
                if L == 0:
                    dve.wait_ge(later_in, 16 * len(later))
                    dve.wait_ge(cell_final, 1)
                    dve.tensor_tensor(cu[:], work[:, 0, :].rearrange("p (t d) -> p t d", t=QT),
                                      row["bo_f"][:].unsqueeze(1).to_broadcast([P, QT, D]), ALU.add)\
                        .then_inc(cu_ready, 1)
                    dve.memset(vx[:, :, :, :, HD:HD + 1], 0.0).then_inc(cu_ready, 1)
                    dve.wait_ge(cu_ready, 2)
                if L == 1:
                    dve.memset(vx[:, :, :, :, HD:HD + 1], 1.0).then_inc(cu_ready, 1)
                    dve.wait_ge(cu_ready, 3)
                if L < 2:
                    layer_end(dve, L)

        @block.tensor
        def _(pe):
            pe.wait_ge(first_in, 16 * len(first))
            pe.wait_ge(const_ready, NREADY)

            def mm(dst, lhs, rhs, start=True, stop=True):
                return pe.matmul(dst, lhs, rhs, start=start, stop=stop, skip_group_check=True)

            def mm3(dst, lhs, rhs, start, stop):
                mm(dst, lhs[0], rhs[0], start=start, stop=False)
                mm(dst, lhs[0], rhs[1], start=False, stop=False)
                return mm(dst, lhs[1], rhs[0], start=False, stop=stop)

            def turn(dst, src):
                for t in range(QT):
                    for k in range(KT):
                        ins = pe.transpose(dst[:, k * S + t * P:k * S + (t + 1) * P], src[:, t, k * P:(k + 1) * P],
                                           ident[:])
                return ins

            def features(dst, weight, rhs, N):
                for o in range(KT):
                    for k in range(KT):
                        ins = mm(dst[:, o * S:o * S + N], weight[:, k, o * P:(o + 1) * P], rhs[:, k, 0:N],
                                 start=k == 0, stop=k == KT - 1)
                return ins

            def features3(dst, o, weights, rhs):
                n = len(weights) * KT
                for i in range(n):
                    wt, x, k = weights[i // KT], rhs[i // KT], i % KT
                    ins = mm3(dst[:, o * S:(o + 1) * S], [wt[:, part, k, o * P:(o + 1) * P] for part in range(2)],
                              [x[:, part, k, :] for part in range(2)], start=i == 0, stop=i == n - 1)
                return ins

            def rows(dst, lhs, weight, tiles=QT, M=P):
                for t in range(tiles):
                    for k in range(KT):
                        ins = mm(dst[0:M, t * D:(t + 1) * D], lhs[:, k, t * P:t * P + M], weight[:, k, :],
                                 start=k == 0, stop=k == KT - 1)
                return ins

            def rows3(dst, t, lhs, weight, N=D):
                for k in range(KT):
                    ins = mm3(dst[:, t * N:(t + 1) * N], [lhs[:, part, k, t * P:(t + 1) * P] for part in range(2)],
                              [weight[:, part, k, :] for part in range(2)], start=k == 0, stop=k == KT - 1)
                return ins

            def turn_rows(L, n):
                pe.wait_ge(xn_ready.sem, xn_ready.at(L, n))
                pe.wait_ge(v_ready.sem, v_ready.at(L, n - 1))
                turn(work[:, 0, :], xn).then_inc(xt_made.sem, 1)

            def queries(L, n, xp=None):
                pe.wait_ge(ql_ready.sem, ql_ready.at(L, n - 1))
                if L < 2:
                    pe.wait_ge(xt_ready.sem, xt_ready.at(L, n))
                    pe.wait_ge(y_read.sem, y_read.at(L, n - 2))
                    features(work[:, 1, :], w[f"wq{L}"], xt, S).then_inc(q_made.sem, 1)
                else:
                    pe.wait_ge(xt_low.sem, xt_low.at(2, n))
                    pe.wait_ge(ebias_ready.sem, ebias_ready.at(2, n - 1))
                    for o in range(KT):
                        ins = features3(work[:, 1, :], o, [ws["wq2"]], [xp])
                    ins.then_inc(q_made.sem, 1)

            def keys(L, n, xp=None):
                pe.wait_ge(xt_ready.sem, xt_ready.at(L, n))
                if L < 2:
                    pe.wait_ge(ctx_loaded.sem, ctx_loaded.at(L, n))
                    features(work[:, 0, :], w[f"wk{L}"], ctx_t, S2).then_inc(k_made.sem, 1)
                else:
                    pe.wait_ge(xt_low.sem, xt_low.at(2, n))
                    for o in range(KT):
                        ins = features3(work[:, 0, :], o, [ws["wk2"]], [xp])
                    ins.then_inc(k_made.sem, 1)

            def vals(L, n, xp=None):
                pe.wait_ge(kl_ready.sem, kl_ready.at(L, n))
                if L < 2:
                    ins = rows(work[:, 0, :], ctx_t, w[f"wv{L}"], tiles=1, M=S2)
                else:
                    for t in range(QT):
                        ins = rows3(work[:, 0, :], t, xp, ws["wv2"])
                ins.then_inc(v_made.sem, 1)

            def tops(L, slot, m, u):
                if u == 0:
                    pe.wait_ge(stack_loaded.sem, stack_loaded.at(L, m))
                    if L < 2:
                        pe.wait_ge(mask_q_ready.sem, mask_q_ready.at(L, m))
                if u < 2:
                    pe.wait_ge(probs_ready.sem, probs_ready.at(L, m - 1, NU[L] - 1 + u))
                else:
                    pe.wait_ge(tops_read.sem, tops_read.at(L, m, u - 1))
                if L < 2:
                    t, jj = divmod(u, 4)
                    mm(score[:, u % 2, 0:4 * S2].rearrange("p (h k) -> p h k", h=4), identb[:],
                       mask_q[:, t, :].unsqueeze(1).to_broadcast([P, 4, S2]), start=True, stop=False)
                    for a in range(2):
                        j = 2 * jj + a
                        ins = mm(score[:, u % 2, a * 2 * S2:(a + 1) * 2 * S2].rearrange("p (h k) -> p h k", h=2),
                                 q_stack[:, slot, j, t * P:(t + 1) * P], k_stack[:, slot, j, :, 0:S2],
                                 start=False, stop=True)
                else:
                    t, j = divmod(u, PAIRS)
                    ins = mm(score[:, u % 2, :], q_stack[:, slot, j, t * P:(t + 1) * P],
                             k_stack[:, slot, j].rearrange("p a k -> p (a k)"))
                ins.then_inc(tops_made.sem, 1)

            def shifts(L, m, n):
                pe.wait_ge(shift_ready.sem, shift_ready.at(L, m))
                if n is not None:
                    pe.wait_ge(ql_ready.sem, ql_ready.at(L, n))
                elif L < 2:
                    pe.wait_ge(y_read.sem, y_read.at(L, m - 1))
                else:
                    pe.wait_ge(ebias_ready.sem, ebias_ready.at(2, m))
                for t in range(QT):
                    ins = pe.transpose(work[0:2 * H, 1, t * P:(t + 1) * P], shift_hl[:, t, :].bitcast(F32), ident[:])
                ins.then_inc(shift_t_made.sem, 1)

            def stacked(L, slot, u):
                kq = KQ[L]
                j, kt = (u, 0) if L < 2 else divmod(u, 2)
                for par in range(2):
                    ins = mm(score[0:kq, u % 2, par * S:(par + 1) * S], k_stack[:, slot, j, par, kt * P:kt * P + kq],
                             q_stack[:, slot, j, :], start=par == 0, stop=False)
                return ins

            def masked(u):
                return mm(score[0:S2, u % 2, :].rearrange("p (a q) -> p a q", a=2), identb[0:S2, 0:S2],
                          mask_k[0:S2, :].unsqueeze(1).to_broadcast([S2, 2, S]), start=False, stop=False)

            def shifted(L, u):
                kq = KQ[L]
                j = u if L < 2 else u // 2
                for par in range(2):
                    ins = mm(score[0:kq, u % 2, par * S:(par + 1) * S], sel[:, 2 * j + par, 0:kq], shift_t[:],
                             start=False, stop=par == 1)
                return ins

            def products(L, slot, m, u):
                kq = KQ[L]
                j, kt = (u, 0) if L < 2 else divmod(u, 2)
                pe.wait_ge(probs_ready.sem, probs_ready.at(L, m, u + 1))
                if L == 1:
                    pe.wait_ge(probs_g_ready.sem, probs_g_ready.at(L, m, u + 1))
                for par in range(2):
                    h = 2 * j + par
                    c, g = h % 4, h // 4
                    dst = o_ps[32 * c:32 * c + VW, g // 2, (g % 2) * S:(g % 2 + 1) * S]
                    p = probs[0:kq, u % NPR, par * S:(par + 1) * S]
                    if L == 1:
                        mm(dst, vx[0:kq, slot, 0, h, :], probs_g[0:kq, u % NPR, par * S:(par + 1) * S],
                           start=True, stop=False)
                        ins = mm(dst, ones_col[0:kq, :], p, start=False, stop=True)
                    else:
                        ins = mm(dst, vx[0:kq, slot, kt, h, :], p, start=kt == 0, stop=L == 0 or kt == 1)
                ins.then_inc(pv_made.sem, 1)

            def probabilities(L, slot, m, between):
                if m is None:
                    for u in range(NU[L]):
                        between(u)
                    return
                pe.wait_ge(shift_t_ready.sem, shift_t_ready.at(L, m))
                pe.wait_ge(v_ready.sem, v_ready.at(L, m))
                pe.wait_ge(tops_read.sem, tops_read.at(L, m))
                if L < 2:
                    pe.wait_ge(mask_k_ready.sem, mask_k_ready.at(L, m))
                pe.wait_ge(att_t_ready.sem, att_t_ready.at(L, m - 1))
                if L == 0:
                    stacked(0, slot, 0).then_inc(raw_made.sem, 1)
                    stacked(0, slot, 1).then_inc(raw_made.sem, 1)
                    for u in range(NU[0]):
                        pe.wait_ge(clipped.sem, clipped.at(0, m, u + 1))
                        masked(u)
                        shifted(0, u).then_inc(scores_made.sem, 1)
                        between(u)
                        if u >= 1:
                            products(0, slot, m, u - 1)
                            if u + 1 < NU[0]:
                                stacked(0, slot, u + 1).then_inc(raw_made.sem, 1)
                    products(0, slot, m, NU[0] - 1)
                else:
                    for u in range(NU[L]):
                        if u >= 2:
                            pe.wait_ge(probs_ready.sem, probs_ready.at(L, m, u - 1))
                        stacked(L, slot, u)
                        if L == 1:
                            masked(u)
                        shifted(L, u).then_inc(scores_made.sem, 1)
                        between(u)
                        if u >= 2:
                            products(L, slot, m, u - 2)
                    products(L, slot, m, NU[L] - 2)
                    products(L, slot, m, NU[L] - 1)

            def turn_attended(L, l):
                pe.wait_ge(att_t_ready.sem, att_t_ready.at(L, l))
                pe.wait_ge(att_ready.sem, att_ready.at(L, l - 1))
                if L == 0:
                    pe.wait_ge(hx_ready.sem, hx_ready.at(0, l - 2))
                if L == 2:
                    pe.wait_ge(exp_read.sem, exp_read.at(2, l))
                for t in range(QT):
                    for g in range(4):
                        ins = pe.transpose(dense[:, t, g * P:(g + 1) * P], att_t[:, g, t * P:(t + 1) * P], ident[:])
                    ins.then_inc(att_made.sem, 1)

            def turn_back(L, l):
                pe.wait_ge(att_ready.sem, att_ready.at(L, l))
                pe.wait_ge(shift_t_ready.sem, shift_t_ready.at(L, l))
                turn(work[:, 1, :], att).then_inc(att_n_made.sem, 1)

            def att_project(L, l):
                pe.wait_ge(att_n_ready.sem, att_n_ready.at(L, l))
                rows(work[:, 1, :], att_n, w[f"wo{L}"]).then_inc(y_made.sem, 1)

            def turn_recurrent(r, l):
                pe.wait_ge(xn1_ready.sem, xn1_ready.at(0, r))
                pe.wait_ge(hx_ready.sem, hx_ready.at(0, r - 1))
                if l is not None:
                    pe.wait_ge(att_ready.sem, att_ready.at(0, l))
                turn(dense[:, 0, :], xn1).then_inc(xt1_made.sem, 1)

            def gate_half(r, l, g, o):
                bk, wn, un = ((1, "wf", "uf"), (0, "wi", "ui"), (1, "wc", "uc"))[g]
                if o == 0:
                    if g == 0:
                        if l is not None:
                            pe.wait_ge(att_ready.sem, att_ready.at(0, l))
                        pe.wait_ge(cell_ready.sem, cell_ready.at(0, r - 1))
                    if g < 2:
                        pe.wait_ge(xt1_low.sem, xt1_low.at(0, r))
                    else:
                        pe.wait_ge(gate_ready.sem, gate_ready.at(0, r, 1))
                ins = features3(dense[:, bk, :], o, [ws[wn], ws[un]], [xt1, cell_parts])
                if o == KT - 1:
                    ins.then_inc(gate_made.sem, 1)

            def hidden_half(r, t):
                if t == 0:
                    pe.wait_ge(gate_ready.sem, gate_ready.at(0, r, 2))
                ins = rows3(dense[:, 0, :], t, xt1, ws["wo_f"])
                if t == QT - 1:
                    ins.then_inc(hx_made.sem, 1)

            def cross_body(L, slot, m, n, l, r, p):
                for u in range(8):
                    if m is not None:
                        tops(L, slot, m, u)
                    if u == 1 and l is not None:
                        turn_attended(L, l)
                    if u == 3 and n is not None:
                        turn_rows(L, n)
                    if u == 4 and l is not None:
                        turn_back(L, l)
                    if u == 5 and r is not None:
                        turn_recurrent(r, l)
                    if u == 6 and l is not None:
                        att_project(L, l)
                if n is not None:
                    keys(L, n)
                if r is not None:
                    gate_half(r, l, 0, 0)
                if n is not None:
                    queries(L, n)
                if r is not None:
                    gate_half(r, l, 0, 1)
                if n is not None:
                    vals(L, n)
                if m is not None:
                    shifts(L, m, n)

                def between(u):
                    if r is not None and u < 4:
                        gate_half(r, l, 1 + u // 2, u % 2)
                    if r is not None and 4 <= u < 6:
                        hidden_half(r, u - 4)

                probabilities(L, slot, m, between)

            def expert(slot, m, l, u):
                pair, t = divmod(u, 2)
                if pair == 0:
                    pe.wait_ge(exp_read.sem, exp_read.at(2, m - 1))
                    if l is not None:
                        pe.wait_ge(att_ready.sem, att_ready.at(2, l))
                else:
                    pe.wait_ge(exp_read.sem, exp_read.at(2, m, u - 1))
                xp = turned_parts[:, slot]
                for k in range(KT):
                    ins = mm3(dense[:, t, :], [xp[:, part, k, t * P:(t + 1) * P] for part in range(2)],
                              [w_exp[:, part, k, 2 * pair:2 * pair + 2, :].rearrange("p e d -> p (e d)")
                               for part in range(2)], start=k == 0, stop=k == KT - 1)
                ins.then_inc(exp_made.sem, 1)

            def experts_body(L, slot, m, n, l, r, p):
                xp = turned_parts[:, 1 - slot]
                for u in range(16):
                    if m is not None:
                        tops(2, slot, m, u)
                    if u == 1 and l is not None:
                        turn_attended(2, l)
                    if u == 3 and n is not None:
                        turn_rows(2, n)
                    if m is not None and u in (5, 7):
                        expert(slot, m, l, (u - 5) // 2)
                    if n is not None and u == 9:
                        queries(2, n, xp)
                    if n is not None and u == 11:
                        keys(2, n, xp)
                    if m is not None and u == 13:
                        expert(slot, m, l, 2)
                if m is not None:
                    expert(slot, m, l, 3)
                if n is not None:
                    vals(2, n, xp)
                if m is not None:
                    shifts(2, m, n)
                if n is not None:
                    if m is not None:
                        pe.wait_ge(shift_t_ready.sem, shift_t_ready.at(2, m))
                    pe.wait_ge(ql_ready.sem, ql_ready.at(2, n))
                    for t in range(QT):
                        ins = rows3(work[:, 1, :], t, xp, ws["w_gate"], N=E)
                    ins.then_inc(logits_made.sem, 1)

                def between(u):
                    if m is not None and u in (2, 5, 9, 13):
                        expert(slot, m, l, 4 + (2, 5, 9, 13).index(u))
                    if n is not None and u == 14:
                        pe.wait_ge(comb_ready.sem, comb_ready.at(2, n))
                        for t in range(QT):
                            ins = pe.transpose(work[0:E, 1, t * P:(t + 1) * P], comb[:, 1 - slot, t, :], ident[:])
                        ins.then_inc(comb_t_made.sem, 1)

                probabilities(2, slot, m, between)
                if n is not None:
                    pe.wait_ge(comb_t_ready.sem, comb_t_ready.at(2, n))
                    for t in range(QT):
                        ins = mm(work[:, 1, t * D:(t + 1) * D], comb_t[:, t * P:(t + 1) * P], b_exp[:])
                    ins.then_inc(ebias_made.sem, 1)

            def body(L, slot, m, n, l, r, p):
                (cross_body if L < 2 else experts_body)(L, slot, m, n, l, r, p)

            for L in range(3):
                if L == 0:
                    pe.wait_ge(stage_used, len(rounds[0]))
                    pe.wait_ge(halved, 4)
                if L == 2:
                    pe.wait_ge(stage_used, len(numbered))
                steps(pe, L, lambda slot, m, n, l, r, p, number: body(L, slot, m, n, l, r, p))
                if L == 0:
                    pe.wait_ge(later_in, 16 * len(later))
                    pe.wait_ge(cell_ready.sem, cell_ready.at(0, B - 1))
                    pe.wait_ge(v_ready.sem, v_ready.at(0, B - 1))
                    rows(work[:, 0, :], cell, w["uo_f"]).then_inc(cell_final, 1)
                if L < 2:
                    layer_end(pe, L)


def _layout(i):
    c = np.ascontiguousarray
    a = {k: np.asarray(v) for k, v in i.items()}
    z = {"x": a["x"], "ctx_t": c(a["ctx_1024"].transpose(0, 2, 1)),
         "mask0": c(a["mask_Bx1xSxS2_ik1"][:, 0]), "mask0_t": c(a["mask_Bx1xSxS2_ik1"][:, 0].transpose(0, 2, 1)),
         "mask1": a["mask_BxSxS2_ik1"], "mask1_t": c(a["mask_BxSxS2_ik1"].transpose(0, 2, 1)),
         "prob_t": c(a["fside_BxSxS2_0"].transpose(0, 2, 1)), "g_xattn": a["g_xattn"], "g_ffn": a["g_ffn"]}
    for n in "qkvo":
        z[f"w{n}0"] = c(a[f"L0_xattn_w{n}"].T)
        z[f"b{n}0"] = a[f"L0_xattn_b{n}"]
        z[f"w{n}1"] = a[f"L1_xattn_w{n}_k"]
        z[f"b{n}1"] = a[f"L1_xattn_w{n}_b"]
    for s, n in enumerate("qkv"):
        z[f"w{n}2"] = c(a["L1_ffn_W_qkv"][:, s * D:(s + 1) * D])
        z[f"b{n}2"] = c(a["L1_ffn_b_qkv"][s * D:(s + 1) * D])
    for n in "fic":
        z[f"w{n}"], z[f"u{n}"], z[f"b{n}"] = c(a[f"L0_ffn_w{n}"].T), c(a[f"L0_ffn_u{n}"].T), a[f"L0_ffn_b{n}"]
    z["wo_f"], z["uo_f"], z["bo_f"] = c(a["L0_ffn_wo"].T), c(a["L0_ffn_uo"].T), a["L0_ffn_bo"]
    z["in_c"] = a["L0_ffn_in_c"]
    z["w_gate"], z["b_gate"] = a["L1_ffn_W_gate"], a["L1_ffn_b_gate"]
    z["w_exp"], z["b_exp"] = a["L1_ffn_W_experts"], a["L1_ffn_b_experts"]
    z["ident"] = np.eye(P, dtype=np.float32)
    z["sel"] = np.zeros((P, H * P), np.float32)
    z["sel"][0:2 * H] = np.repeat(np.tile(np.eye(H, dtype=np.float32), (2, 1)), P, axis=1)
    z["earlier"] = np.tril(np.ones((E, E), np.float32), -1).reshape(-1)
    for n in ("bq0", "bk0", "bq1", "bk1", "bq2", "bk2", "bf", "bi", "bc", "in_c"):
        z[n] = z[n].reshape(KT, P).T
    return {k: c(v) for k, v in z.items()}


def kernel(**inputs):
    import concourse.bacc as _bacc
    from concourse.bass_utils import run_bass_kernel_spmd as _run

    arrays = _layout(inputs)
    batches = arrays["x"].shape[0]
    nc = _bacc.Bacc("TRN2", target_bir_lowering=False, num_devices=1)
    io = {n: nc.dram_tensor("in_" + n, a.shape, mybir.dt.from_np(a.dtype), kind="ExternalInput").ap()
          for n, a in arrays.items()}
    out = nc.dram_tensor("out_x", arrays["x"].shape, F32, kind="ExternalOutput").ap()
    flamingo_block(nc, io, out, batches)
    r = _run(nc, [{"in_" + n: a for n, a in arrays.items()}], core_ids=[0])
    return r.results[0]["out_x"]
```

```python
from contextlib import ExitStack

import numpy as np

import concourse.bass as bass
from concourse import mybir

F32 = mybir.dt.float32
F32R = mybir.dt.float32r
BF16 = mybir.dt.bfloat16
I32 = mybir.dt.int32
ALU = mybir.AluOpType
ACT = mybir.ActivationFunctionType
AX = mybir.AxisListType

P = 128
D = 256
KT = D // P
S = 256
QT = S // P
S2 = 120
H = 16
HD = D // H
PAIRS = H // 2
VW = 32
E = 8
SCALE = HD ** -0.5
CLIP = 100.0 / SCALE
MASKED = 998244352.0 / SCALE
EPS = 1e-5
LINKS = 160


class Signal:

    def __init__(self, sem, per, steps):
        self.sem, self.per, self.start, at = sem, per, [], 0
        for p in per:
            self.start.append(at)
            at += steps * p

    def at(self, L, n, k=None):
        if isinstance(n, int) and n < 0:
            return self.start[L]
        return self.start[L] + n * self.per[L] + (self.per[L] if k is None else k)


class Chain:

    def __init__(self, eng, sem):
        self.eng, self.sem, self.base, self.k = eng, sem, 0, 0

    def step(self, base):
        self.base, self.k = base, 0

    def link(self, ins):
        ins.then_inc(self.sem, 1)
        self.k += 1
        return self.k

    def at(self, k=None):
        return self.base * LINKS + (self.k if k is None else k)

    def close(self):
        assert self.k < LINKS
        self.eng.sem_inc(self.sem, LINKS - self.k)


def flamingo_block(nc, io, out, B):
    ctx = ExitStack()
    with ctx:
        def sb(name, shape, dt=F32):
            return ctx.enter_context(nc.sbuf_tensor(name, shape, dt))

        def sem(name):
            return ctx.enter_context(nc.semaphore(name))

        def signal(name, *per):
            return Signal(sem(name), per, B)

        x1_d = nc.dram_tensor("x1_d", [B, S, D], F32, kind="Internal").ap()
        hx_d = nc.dram_tensor("hx_d", [B, S, D], F32, kind="Internal").ap()
        x2_d = nc.dram_tensor("x2_d", [B, S, D], F32, kind="Internal").ap()
        x3_d = nc.dram_tensor("x3_d", [B, S, D], F32, kind="Internal").ap()
        q_d = [nc.dram_tensor(f"q_d{L}", [B, 2, D, S], F32, kind="Internal").ap() for L in range(3)]
        k_d = [nc.dram_tensor(f"k_d{L}", [B, 2, D, S2 if L < 2 else S], F32, kind="Internal").ap() for L in range(3)]

        ident = sb("ident", [P, P])
        identb = sb("identb", [P, P], BF16)
        sel = sb("sel", [P, H, P], F32R)
        earlier = sb("earlier", [P, E, E])
        ones_col = sb("ones_col", [P, VW])
        zeros = sb("zeros", [P, S])
        neg_half = sb("neg_half", [P, QT])
        gates_in = sb("gates_in", [P, 4])
        tg = sb("tg", [P, 4])
        first_w = ["wq0", "wk0", "wv0", "wo0"]
        later_w = ["uo_f", "wq1", "wk1", "wv1", "wo1"]
        w = {n: sb("w_" + n, [P, KT, D]) for n in first_w + later_w}
        col0 = ["bq0", "bk0", "bf", "bi", "bc", "in_c"]
        col1 = ["bq1", "bk1", "bq2", "bk2"]
        col = {n: sb("col_" + n, [P, KT]) for n in col0 + col1}
        row0 = ["bv0", "bo0"]
        row1 = ["bo_f", "bv1", "bo1", "bv2"]
        row = {n: sb("row_" + n, [P, D]) for n in row0 + row1}
        b_gate = sb("b_gate", [P, E])
        b_exp = sb("b_exp", [E, D])
        split_w = ["wf", "uf", "wi", "ui", "wc", "uc", "wo_f"]
        NEXP = KT * E * D
        NSPLIT = max(len(split_w) * KT * D, NEXP + 3 * KT * D + KT * E)
        parts_w = sb("parts_w", [P, 2, NSPLIT], F32R)

        def split_view(at, *shape):
            n = int(np.prod(shape))
            v = parts_w[:, :, at:at + n]
            if len(shape) == 2:
                return v.rearrange("p l (k o) -> p l k o", k=shape[0])
            return v.rearrange("p l (k e o) -> p l k e o", k=shape[0], e=shape[1])

        ws = {n: split_view(i * KT * D, KT, D) for i, n in enumerate(split_w)}
        w_exp = split_view(0, KT, E, D)
        for i, n in enumerate(("wq2", "wk2", "wv2")):
            ws[n] = split_view(NEXP + i * KT * D, KT, D)
        ws["w_gate"] = split_view(NEXP + 3 * KT * D, KT, E)

        x_in = sb("x_in", [P, QT, D])
        x_res = sb("x_res", [P, QT, D])
        ctx_t = sb("ctx_t", [P, KT, S2])
        stats = sb("stats", [P, QT, 6])
        mv = sb("mv", [P, QT, 2])
        var_eps = sb("var_eps", [P, QT])
        rstd = sb("rstd", [P, QT])
        stats1 = sb("stats1", [P, QT, 6])
        mv1 = sb("mv1", [P, QT, 2])
        var_eps1 = sb("var_eps1", [P, QT])
        rstd1 = sb("rstd1", [P, QT])
        xn = sb("xn", [P, QT, D])
        xt = sb("xt", [P, KT, S])
        turned_parts = sb("turned_parts", [P, 2, 2, KT, S], F32R)
        xt1, cell_parts = turned_parts[:, 0], turned_parts[:, 1]
        qhl = sb("qhl", [P, 2, KT, S], F32R)
        khl = sb("khl", [P, 2, KT, S], F32R)
        q_stack = sb("q_stack", [P, 2, PAIRS, S], F32R)
        STACK = 3 * HD * 2
        SHIFTED = STACK + 4
        k_stack = sb("k_stack", [P, 2, PAIRS, 2, S], F32R)
        vx = sb("vx", [P, 2, 2, H, VW])
        mask_i = sb("mask_i", [P, QT, S2], I32)
        mask_ti = sb("mask_ti", [P, S], I32)
        mask_q = sb("mask_q", [P, QT, S2], BF16)
        mask_k = sb("mask_k", [P, S], BF16)
        prob_k = sb("prob_k", [P, S])
        top = sb("top", [P, QT, H])
        top2 = sb("top2", [P, QT, H])
        shift_hl = sb("shift_hl", [P, QT, 2 * H], F32R)
        shift_t = sb("shift_t", [P, S], F32R)
        NPR = 4
        probs = sb("probs", [P, NPR, 2 * S])
        att_t = sb("att_t", [P, 4, S])
        rec = sb("rec", [P, QT, H])
        att = sb("att", [P, QT, D])
        att_n = sb("att_n", [P, KT, S])
        y = sb("y", [P, QT, D])
        y2 = sb("y2", [P, QT, D])
        xn1 = sb("xn1", [P, QT, D])
        cell = sb("cell", [P, KT, S])
        hx = sb("hx", [P, QT, D])
        x2, hx_in = xn1, hx
        cu = sb("cu", [P, QT, D])
        by_layer = sb("by_layer", [P, 5, KT * S])
        gf, gi, gc, ca, cb = (by_layer[:, i].rearrange("p (k t) -> p k t", k=KT) for i in range(5))
        probs_g = by_layer[:, 0:NPR]
        acc = [[by_layer[:, 2 * s + a].rearrange("p (t d) -> p t d", t=QT) for a in range(2)] for s in range(2)]
        ebias = by_layer[:, 4].rearrange("p (t d) -> p t d", t=QT)
        acc_tile = [[by_layer[:, 2 * s:2 * s + 2, t * D:(t + 1) * D] for t in range(QT)] for s in range(2)]
        scaled = [y2, att_n]
        lg = sb("lg", [P, QT, E])
        nmx = sb("nmx", [P, QT])
        ge = sb("ge", [P, QT, E])
        gsum = sb("gsum", [P, QT])
        grec = sb("grec", [P, QT])
        cmp1 = sb("cmp1", [P, QT, E, E])
        cmp2 = sb("cmp2", [P, QT, E, E])
        rank = sb("rank", [P, QT, E])
        comb = sb("comb", [P, 2, QT, E])
        comb_t = sb("comb_t", [E, S])

        def bank(name, n=1):
            return ctx.enter_context(nc.psum_tensor(name, [P, n, 512], F32))
        work = bank("work", 2)
        score = bank("score", 2)
        o_ps = bank("o_ps", 2)
        dense = bank("dense", 2)

        NU = [PAIRS, PAIRS, 2 * PAIRS]
        first_in = sem("first_in")
        later_in = sem("later_in")
        stage_in = [sem("stage0_in"), sem("stage1_in")]
        stage_used = sem("stage_used")
        split_done = sem("split_done")
        const_ready = sem("const_ready")
        zeroed = sem("zeroed")
        ones_cleared = sem("ones_cleared")
        halved = sem("halved")
        gates_ready = sem("gates_ready")
        layer_done = sem("layer_done")
        cell_final = sem("cell_final")
        cu_ready = sem("cu_ready")
        shift_rows_set = sem("shift_rows_set")
        dve_chain = sem("dve_chain")
        passed = sem("passed")
        x_loaded = signal("x_loaded", 16, 32, 16)
        ctx_loaded = signal("ctx_loaded", 16, 16, 0)
        mask_loaded = signal("mask_loaded", 32, 32, 0)
        prob_loaded = signal("prob_loaded", 0, 16, 0)
        res_loaded = signal("res_loaded", 16, 16, 16)
        parts_stored = signal("parts_stored", 64, 64, 64)
        stack_loaded = signal("stack_loaded", 192, 192, 192)
        y_stored = signal("y_stored", 16, 16, 16)
        hx_stored = signal("hx_stored", 16, 0, 0)
        x2_stored = signal("x2_stored", 0, 16, 0)
        pre_h = signal("pre_h", 0, 1, 0)
        tanh_h = signal("tanh_h", 0, 1, 0)
        gated_h = signal("gated_h", 0, 1, 0)
        x2_ready = signal("x2_ready", 0, 1, 0)
        var_ready = signal("var_ready", 1, 1, 1)
        rstd_ready = signal("rstd_ready", 1, 1, 1)
        xn_ready = signal("xn_ready", 1, 1, 1)
        mask_q_ready = signal("mask_q_ready", 1, 1, 0)
        mask_k_ready = signal("mask_k_ready", 1, 1, 0)
        xt_made = signal("xt_made", 1, 1, 1)
        xt_ready = signal("xt_ready", 1, 1, 1)
        xt_low = signal("xt_low", 0, 0, 1)
        q_made = signal("q_made", 1, 1, 1)
        k_made = signal("k_made", 1, 1, 1)
        v_made = signal("v_made", 1, 1, 1)
        qh_ready = signal("qh_ready", 2, 2, 2)
        kh_ready = signal("kh_ready", 2, 2, 2)
        ql_ready = signal("ql_ready", 2, 2, 2)
        kl_ready = signal("kl_ready", 2, 2, 2)
        v_ready = signal("v_ready", 1, 1, 1)
        tops_made = signal("tops_made", *NU)
        tops_read = signal("tops_read", *NU)
        shift_ready = signal("shift_ready", 1, 1, 1)
        shift_t_made = signal("shift_t_made", 1, 1, 1)
        shift_t_ready = signal("shift_t_ready", 1, 1, 1)
        shift_moved = signal("shift_moved", 0, 0, 64)
        raw_made = signal("raw_made", 8, 0, 0)
        clipped = signal("clipped", 8, 0, 0)
        scores_made = signal("scores_made", *NU)
        probs_ready = signal("probs_ready", *NU)
        probs_g_ready = signal("probs_g_ready", 0, NU[1], 0)
        pv_made = signal("pv_made", *NU)
        att_t_ready = signal("att_t_ready", 2, 2, 2)
        att_made = signal("att_made", 2, 2, 2)
        att_ready = signal("att_ready", 2, 2, 2)
        att_n_made = signal("att_n_made", 1, 1, 0)
        att_n_ready = signal("att_n_ready", 1, 1, 0)
        y_made = signal("y_made", 1, 1, 0)
        y_read = signal("y_read", 1, 1, 0)
        y_ready = signal("y_ready", 1, 1, 1)
        var1_ready = signal("var1_ready", 1, 0, 0)
        rstd1_ready = signal("rstd1_ready", 1, 0, 0)
        xn1_ready = signal("xn1_ready", 1, 0, 0)
        xt1_made = signal("xt1_made", 1, 0, 0)
        xt1_ready = signal("xt1_ready", 1, 0, 0)
        xt1_low = signal("xt1_low", 1, 0, 0)
        gate_made = signal("gate_made", 3, 0, 0)
        gate_ready = signal("gate_ready", 3, 0, 0)
        cell_ready = signal("cell_ready", 1, 0, 0)
        recur_done = signal("recur_done", 5, 0, 0)
        hx_made = signal("hx_made", 1, 0, 0)
        hx_ready = signal("hx_ready", 1, 0, 0)
        logits_made = signal("logits_made", 0, 0, 1)
        logits_ready = signal("logits_ready", 0, 0, 1)
        gexp_ready = signal("gexp_ready", 0, 0, 2)
        comb_ready = signal("comb_ready", 0, 0, 1)
        comb_t_made = signal("comb_t_made", 0, 0, 1)
        comb_t_ready = signal("comb_t_ready", 0, 0, 1)
        ebias_made = signal("ebias_made", 0, 0, 1)
        ebias_ready = signal("ebias_ready", 0, 0, 1)
        exp_made = signal("exp_made", 0, 0, 8)
        exp_read = signal("exp_read", 0, 0, 2)
        exp_scaled = signal("exp_scaled", 0, 0, 6)
        exp_summed = signal("exp_summed", 0, 0, 4)

        KQ = [S2, S2, P]
        KN = [S2, S2, S]

        def tokens(ap):
            return ap.rearrange("(t p) d -> p t d", p=P)

        FIRST = [4, 2, 2]
        STEPS = B + 4

        def steps(eng, L, body):
            def step(t, slot):
                def within(b):
                    return b if not isinstance(b, int) or 0 <= b < B else None
                body(slot, within(t), within(t + 1), within(t - 1), within(t - 2) if L == 0 else None, within(t + 2),
                     t + L * STEPS + 2)

            for t in range(-2, FIRST[L]):
                step(t, t % 2)
            with eng.Fori(FIRST[L], B - 3, 2) as t:
                step(t, 0)
                step(t + 1, 1)
            for t in range(B - 2, B + 2):
                step(t, t % 2)

        def layer_end(eng, L):
            eng.drain().then_inc(layer_done, 1)
            eng.wait_ge(layer_done, 5 * (L + 1))

        def weight(n):
            return io[n].rearrange("(k p) o -> p k o", p=P)

        first = [(ident[:], io["ident"])]
        first += [(w[n][:], weight(n)) for n in first_w]
        first += [(col[n][:], io[n]) for n in col0] + [(row[n][:], io[n].partition_broadcast(P)) for n in row0]
        first += [(gates_in[:, 0:2], io["g_xattn"].partition_broadcast(P)),
                  (gates_in[:, 2:4], io["g_ffn"].partition_broadcast(P))]
        later = [(w[n][:], weight(n)) for n in later_w]
        later += [(col[n][:], io[n]) for n in col1] + [(row[n][:], io[n].partition_broadcast(P)) for n in row1]
        later += [(b_gate[:], io["b_gate"].partition_broadcast(P)), (b_exp[:], io["b_exp"]),
                  (earlier[:].rearrange("p a b -> p (a b)"), io["earlier"].partition_broadcast(P))]
        NREADY = 6

        stage = [probs[:].rearrange("p a b -> p (a b)"), by_layer[:, 0:4].rearrange("p a b -> p (a b)")]
        NW = KT * D

        def flat(part, at, n):
            return parts_w[:, part, at:at + n]

        rounds = [[], [], []]
        rounds[0].append(([(0, H * P, io["sel"])], (sel[:].rearrange("p h k -> p (h k)"), None, H * P)))
        for lo in (0, 4):
            some = split_w[lo:lo + 4]
            rounds[0].append(([(i * NW, NW, weight(n)) for i, n in enumerate(some)],
                              (flat(0, lo * NW, len(some) * NW), flat(1, lo * NW, len(some) * NW), len(some) * NW)))
        for k in range(KT):
            rounds[2].append(([(0, E * D, io["w_exp"][:, k * P:(k + 1) * P, :].rearrange("e p o -> p e o"))],
                              (flat(0, k * E * D, E * D), flat(1, k * E * D, E * D), E * D)))
        rest = [(i * NW, NW, weight(n)) for i, n in enumerate(("wq2", "wk2", "wv2"))]
        rest.append((3 * NW, KT * E, weight("w_gate")))
        rounds[2].append((rest, (flat(0, NEXP, 3 * NW + KT * E), flat(1, NEXP, 3 * NW + KT * E), 3 * NW + KT * E)))
        numbered = [(L, r) for L in (0, 2) for r in rounds[L]]
        loaded = [sum(16 * len(r[0]) for _, r in numbered[i % 2:i + 1:2]) for i in range(len(numbered))]

        def load_rounds(eng, L, only=None):
            for i, (of, (loads, _)) in enumerate(numbered):
                if of != L:
                    continue
                if i >= 2:
                    eng.wait_ge(stage_used, i - 1)
                for at, n, src in loads:
                    dst = stage[i % 2][:, at:at + n]
                    if len(src.shape) == 3:
                        dst = dst.rearrange("p (k o) -> p k o", k=src.shape[1])
                    eng.dma_start(dst, src).then_inc(stage_in[i % 2], 16)

        block = ctx.enter_context(nc.Block())

        @block.sync
        def _(sp):
            for dst, src in first:
                sp.dma_start(dst, src).then_inc(first_in, 16)

            def store_parts(L, n, part, hl, ready, dst, N):
                sp.wait_ge(ready.sem, ready.at(L, n))
                sp.dma_start(dst[n, part].rearrange("(m p) t -> p m t", p=P),
                             hl[:, part, :, 0:N].bitcast(F32)).then_inc(parts_stored.sem, 16)

            def load_stacks(L, slot, n):
                sp.wait_ge(parts_stored.sem, parts_stored.at(L, n))
                sp.wait_ge(scores_made.sem, scores_made.at(L, n - 2))
                for stack, src, order in ((q_stack, q_d[L], (0, 0, 1)), (k_stack, k_d[L], (0, 1, 0))):
                    for par in range(2):
                        for i, part in enumerate(order):
                            rows = slice((3 * par + i) * HD, (3 * par + i + 1) * HD)
                            dst = stack[rows, slot] if stack is q_stack else stack[rows, slot, :, par, 0:KN[L]]
                            sp.dma_start(dst.bitcast(F32),
                                         src[n, part].rearrange("(j a d) t -> a d j t", a=2, d=HD)[par])\
                              .then_inc(stack_loaded.sem, 16)

            def move_shifts(L, slot, m):
                sp.wait_ge(shift_t_ready.sem, shift_t_ready.at(L, m))
                for par in range(2):
                    for part in range(2):
                        row_at = STACK + 2 * par + part
                        sp.dma_start(q_stack[row_at:row_at + 1, slot].bitcast(F32),
                                     shift_t[H * part + par:H * part + H:2, :].bitcast(F32))\
                            .then_inc(shift_moved.sem, 16)

            def store_y(L, l):
                sp.wait_ge(y_ready.sem, y_ready.at(L, l))
                sp.dma_start(tokens([x1_d, x3_d, out][L][l]), y[:]).then_inc(y_stored.sem, 16)

            def body(L, slot, m, n, l, r, p):
                if n is not None:
                    for part, ready in ((0, qh_ready), (1, ql_ready)):
                        store_parts(L, n, part, qhl, ready, q_d[L], S)
                if L == 2 and m is not None:
                    move_shifts(2, slot, m)
                if n is not None:
                    for part, ready in ((0, kh_ready), (1, kl_ready)):
                        store_parts(L, n, part, khl, ready, k_d[L], KN[L])
                    load_stacks(L, 1 - slot, n)
                if L == 1 and p is not None:
                    sp.wait_ge(x2_ready.sem, x2_ready.at(1, p))
                    sp.dma_start(tokens(x2_d[p]), x2[:]).then_inc(x2_stored.sem, 16)
                if l is not None:
                    store_y(L, l)
                if r is not None:
                    sp.wait_ge(hx_ready.sem, hx_ready.at(0, r))
                    sp.dma_start(tokens(hx_d[r]), hx[:]).then_inc(hx_stored.sem, 16)

            for L in range(3):
                steps(sp, L, lambda slot, m, n, l, r, p, number: body(L, slot, m, n, l, r, p))
                sp.wait_ge(y_stored.sem, y_stored.at(L, B - 1))
                if L == 0:
                    sp.wait_ge(hx_stored.sem, hx_stored.at(0, B - 1))
                if L == 1:
                    sp.wait_ge(x2_stored.sem, x2_stored.at(1, B - 1))
                if L < 2:
                    layer_end(sp, L)

        @block.gpsimd
        def _(pool):
            pool.memset(neg_half[:], -0.5).then_inc(const_ready, 1)
            pool.memset(ones_col[:], 0.0).then_inc(ones_cleared, 1)
            pool.wait_ge(ones_cleared, 1)
            pool.memset(ones_col[:, HD:HD + 1], 1.0).then_inc(const_ready, 1)

            def load_x(L, p):
                if L == 1:
                    pool.wait_ge(x2_ready.sem, x2_ready.at(1, p - 1))
                    pool.sem_inc(passed, 1)
                    pool.dma_start(hx_in[:], tokens(hx_d[p])).then_inc(x_loaded.sem, 16)
                else:
                    pool.wait_ge(xn_ready.sem, xn_ready.at(L, p - 1))
                pool.sem_inc(passed, 1)
                pool.dma_start(x_in[:], tokens([io["x"], x1_d, x3_d][L][p])).then_inc(x_loaded.sem, 16)

            def load_ctx(L, n):
                pool.wait_ge(v_made.sem, v_made.at(L, n - 1))
                pool.sem_inc(passed, 1)
                pool.dma_start(ctx_t[:], io["ctx_t"][n].rearrange("(k p) t -> p k t", p=P)).then_inc(ctx_loaded.sem, 16)

            def load_mask(L, n):
                pool.wait_ge(mask_k_ready.sem, mask_k_ready.at(L, n - 1))
                pool.wait_ge(mask_q_ready.sem, mask_q_ready.at(L, n - 1))
                pool.sem_inc(passed, 1)
                pool.dma_start(mask_i[:], io[f"mask{L}"][n].rearrange("(t p) k -> p t k", p=P))\
                    .then_inc(mask_loaded.sem, 16)
                pool.dma_start(mask_ti[0:S2, :], io[f"mask{L}_t"][n]).then_inc(mask_loaded.sem, 16)

            def recur(r):
                done = recur_done
                pool.wait_ge(gate_ready.sem, gate_ready.at(0, r, 3))
                pool.sem_inc(passed, 1)
                pool.tensor_scalar(by_layer[:, 0:2], by_layer[:, 0:2], 0.5, 0.5, ALU.mult, ALU.add)\
                    .then_inc(done.sem, 1)
                pool.wait_ge(done.sem, done.at(0, r, 1))
                pool.tensor_tensor(ca[:], gf[:], cell[:], ALU.mult).then_inc(done.sem, 1)
                pool.tensor_tensor(cb[:], gi[:], gc[:], ALU.mult).then_inc(done.sem, 1)
                pool.wait_ge(done.sem, done.at(0, r, 3))
                pool.tensor_tensor(cell[:], ca[:], cb[:], ALU.add).then_inc(done.sem, 1)
                pool.wait_ge(done.sem, done.at(0, r, 4))
                pool.sem_inc(passed, 1)
                pool.tensor_copy(cell_parts[:, 0], cell[:]).then_inc(done.sem, 1)
                pool.wait_ge(done.sem, done.at(0, r, 5))
                pool.tensor_tensor(cell_parts[:, 1], cell[:], cell_parts[:, 0].bitcast(F32), ALU.subtract)\
                    .then_inc(cell_ready.sem, 1)

            def before_tanh(p):
                pool.wait_ge(x_loaded.sem, x_loaded.at(1, p))
                pool.tensor_tensor(hx_in[:], hx_in[:], cu[:], ALU.add).then_inc(pre_h.sem, 1)

            def after_tanh(p):
                pool.wait_ge(tanh_h.sem, tanh_h.at(1, p))
                pool.sem_inc(passed, 1)
                pool.tensor_scalar(hx_in[:], hx_in[:], tg[:, 2:3], None, ALU.mult).then_inc(gated_h.sem, 1)
                pool.wait_ge(x2_stored.sem, x2_stored.at(1, p - 1))
                pool.sem_inc(passed, 1)
                pool.wait_ge(xn_ready.sem, xn_ready.at(1, p - 1))
                pool.sem_inc(passed, 1)
                pool.wait_ge(gated_h.sem, gated_h.at(1, p))
                pool.tensor_tensor(x2[:], hx_in[:], x_in[:], ALU.add).then_inc(x2_ready.sem, 1)

            def first_experts(slot, m):
                pool.wait_ge(exp_scaled.sem, exp_scaled.at(2, m, 2))
                pool.wait_ge(ebias_ready.sem, ebias_ready.at(2, m))
                pool.tensor_tensor(acc[slot][0], acc[slot][0], ebias, ALU.add).then_inc(exp_summed.sem, 1)
                pool.wait_ge(exp_summed.sem, exp_summed.at(2, m, 1))
                pool.wait_ge(exp_scaled.sem, exp_scaled.at(2, m, 4))
                for t in range(QT):
                    sums = acc_tile[slot][t]
                    ins = pool.tensor_tensor(sums, sums, scaled[t][:], ALU.add)
                ins.then_inc(exp_summed.sem, 1)

            def last_experts(slot, m):
                for pair in (2, 3):
                    pool.wait_ge(exp_scaled.sem, exp_scaled.at(2, m, pair + 3))
                    pool.wait_ge(exp_summed.sem, exp_summed.at(2, m, pair))
                    sums = acc_tile[slot][1]
                    pool.tensor_tensor(sums, sums, scaled[pair % 2][:], ALU.add).then_inc(exp_summed.sem, 1)

            def body(L, slot, m, n, l, r, p, ahead):
                if L == 2 and m is not None:
                    first_experts(slot, m)
                if L == 1 and p is not None:
                    before_tanh(p)
                if L < 2 and n is not None:
                    pool.wait_ge(mask_loaded.sem, mask_loaded.at(L, n))
                    pool.sem_inc(passed, 1)
                    pool.wait_ge(tops_made.sem, tops_made.at(L, n - 1))
                    pool.sem_inc(passed, 1)
                    pool.tensor_scalar(mask_q[:], mask_i[:], MASKED, -MASKED, ALU.mult, ALU.add)\
                        .then_inc(mask_q_ready.sem, 1)
                if L < 2 and p is not None:
                    load_ctx(L, p)
                if L == 1 and p is not None:
                    after_tanh(p)
                if p is not None:
                    pool.wait_ge(var_ready.sem, var_ready.at(L, p))
                    pool.tensor_tensor(rstd[:], var_eps[:], neg_half[:], ALU.pow).then_inc(rstd_ready.sem, 1)
                if ahead is not None:
                    load_x(L, ahead)
                if L == 0 and l is not None:
                    pool.wait_ge(var1_ready.sem, var1_ready.at(0, l))
                    pool.tensor_tensor(rstd1[:], var_eps1[:], neg_half[:], ALU.pow).then_inc(rstd1_ready.sem, 1)
                if m is not None:
                    pool.wait_ge(y_ready.sem, y_ready.at(L, m - 1))
                    pool.sem_inc(passed, 1)
                    if L == 1:
                        pool.wait_ge(x2_stored.sem, x2_stored.at(1, m))
                        pool.sem_inc(passed, 1)
                    pool.dma_start(x_res[:], tokens([io["x"], x2_d, x3_d][L][m])).then_inc(res_loaded.sem, 16)
                if L == 2 and m is not None:
                    last_experts(slot, m)
                if L == 0 and r is not None:
                    recur(r)
                if L < 2 and n is not None:
                    pool.wait_ge(scores_made.sem, scores_made.at(L, n - 1))
                    pool.sem_inc(passed, 1)
                    pool.tensor_scalar(mask_k[0:S2, :], mask_ti[0:S2, :], MASKED, -MASKED, ALU.mult, ALU.add)\
                        .then_inc(mask_k_ready.sem, 1)
                if L == 1 and n is not None:
                    pool.wait_ge(probs_g_ready.sem, probs_g_ready.at(1, n - 1))
                    pool.sem_inc(passed, 1)
                    pool.dma_start(prob_k[0:S2, :], io["prob_t"][n]).then_inc(prob_loaded.sem, 16)
                if L < 2 and p is not None:
                    load_mask(L, p)

            def step(L, slot, m, n, l, r, p):
                ahead = None if p is None or (isinstance(p, int) and p == B - 1) else p + 1
                body(L, slot, m, n, l, r, p, ahead)

            load_rounds(pool, 0)
            for L in range(3):
                if L == 2:
                    load_rounds(pool, 2)
                load_x(L, 0)
                for t in range(-2, FIRST[L]):
                    step(L, t % 2, *[b if 0 <= b < B else None for b in (t, t + 1, t - 1, t - 2, t + 2)])
                with pool.Fori(FIRST[L], B - 5, 2) as t:
                    step(L, 0, t, t + 1, t - 1, t - 2, t + 2)
                    step(L, 1, t + 1, t + 2, t, t - 1, t + 3)
                for t in range(B - 4, B + 2):
                    step(L, t % 2, *[b if 0 <= b < B else None for b in (t, t + 1, t - 1, t - 2, t + 2)])
                if L < 2:
                    layer_end(pool, L)

        @block.scalar
        def _(act):
            for dst, src in later:
                act.dma_start(dst, src).then_inc(later_in, 16)
            act.wait_ge(first_in, 16 * len(first))
            act.activation(tg[:], gates_in[:], ACT.Tanh).then_inc(gates_ready, 1)
            act.wait_ge(const_ready, NREADY)
            for k in range(KT):
                act.activation(cell[:, k, :], zeros[:], ACT.Identity, bias=col["in_c"][:, k:k + 1])\
                    .then_inc(gates_ready, 1)

            def high(L, n, made, ready, part, bk, b, N):
                act.wait_ge(made.sem, made.at(L, n))
                act.wait_ge(parts_stored.sem, parts_stored.at(L, n - 1))
                for k in range(KT):
                    act.activation(part[:, 0, k, 0:N], work[:, bk, k * S:k * S + N], ACT.Identity,
                                   bias=col[f"{b}{L}"][:, k:k + 1]).then_inc(ready.sem, 1)

            def gate(r, g):
                dst, b, s, bk = ((gf, "bf", 0.5, 1), (gi, "bi", 0.5, 0), (gc, "bc", 1.0, 1))[g]
                act.wait_ge(gate_made.sem, gate_made.at(0, r, g + 1))
                if g == 0:
                    act.wait_ge(cell_ready.sem, cell_ready.at(0, r - 1))
                for k in range(KT):
                    ins = act.activation(dst[:, k, :], dense[:, bk, k * S:(k + 1) * S], ACT.Tanh,
                                         bias=col[b][:, k:k + 1], scale=s)
                ins.then_inc(gate_ready.sem, 1)

            def hidden(r):
                act.wait_ge(hx_made.sem, hx_made.at(0, r))
                act.wait_ge(hx_stored.sem, hx_stored.at(0, r - 1))
                act.activation(hx[:], dense[:, 0, :], ACT.Copy).then_inc(hx_ready.sem, 1)

            def exponential(L, m, u):
                act.wait_ge(scores_made.sem, scores_made.at(L, m, u + 1))
                if u >= NPR:
                    act.wait_ge(pv_made.sem, pv_made.at(L, m, u - NPR + 1))
                act.activation(probs[0:KQ[L], u % NPR, :], score[0:KQ[L], u % 2, :], ACT.Exp, scale=SCALE)\
                    .then_inc(probs_ready.sem, 1)

            def attended_turned(L, m):
                act.wait_ge(pv_made.sem, pv_made.at(L, m))
                if L == 2:
                    act.wait_ge(att_made.sem, att_made.at(2, m - 1))
                for g in range(2):
                    act.activation(att_t[:, 2 * g:2 * g + 2, :], o_ps[:, g, :], ACT.Copy).then_inc(att_t_ready.sem, 1)

            def shifts_turned(L, m):
                act.wait_ge(shift_t_made.sem, shift_t_made.at(L, m))
                if L == 2:
                    act.wait_ge(shift_moved.sem, shift_moved.at(L, m - 1))
                act.activation(shift_t[0:2 * H, :], work[0:2 * H, 1, 0:S], ACT.Copy).then_inc(shift_t_ready.sem, 1)

            def turned_back(L, l):
                act.wait_ge(att_n_made.sem, att_n_made.at(L, l))
                act.activation(att_n[:], work[:, 1, :], ACT.Copy).then_inc(att_n_ready.sem, 1)

            def cross_body(L, slot, m, n, l, r, p):
                if n is not None:
                    act.wait_ge(xt_made.sem, xt_made.at(L, n))
                    act.activation(xt[:], work[:, 0, :], ACT.Copy).then_inc(xt_ready.sem, 1)
                if n is not None:
                    high(L, n, q_made, qh_ready, qhl, 1, "bq", S)
                    high(L, n, k_made, kh_ready, khl, 0, "bk", S2)
                if r is not None:
                    act.wait_ge(xt1_made.sem, xt1_made.at(0, r))
                    act.activation(xt1[:, 0], dense[:, 0, :], ACT.Copy).then_inc(xt1_ready.sem, 1)
                if m is not None:
                    shifts_turned(L, m)
                for u in range(8):
                    if m is not None:
                        exponential(L, m, u)
                    if u == 0 and L == 1 and p is not None:
                        act.wait_ge(pre_h.sem, pre_h.at(1, p))
                        act.activation(hx_in[:], hx_in[:], ACT.Tanh).then_inc(tanh_h.sem, 1)
                    if u in (1, 3, 5) and r is not None:
                        gate(r, u // 2)
                    if u == 1 and l is not None:
                        turned_back(L, l)
                if r is not None:
                    hidden(r)
                if m is not None:
                    attended_turned(L, m)

            def expert(slot, m, pair, t):
                act.wait_ge(exp_made.sem, exp_made.at(2, m, 2 * pair + t + 1))
                if pair == 0:
                    act.wait_ge(comb_ready.sem, comb_ready.at(2, m))
                    act.wait_ge(y_ready.sem, y_ready.at(2, m - 2))
                elif pair == 1:
                    act.wait_ge(exp_summed.sem, exp_summed.at(2, m - 1))
                else:
                    act.wait_ge(exp_summed.sem, exp_summed.at(2, m, 2))
                for a in range(2):
                    e = 2 * pair + a
                    dst = acc[slot][a][:, t, :] if pair == 0 else scaled[t if pair == 1 else pair % 2][:, a, :]
                    ins = act.activation(dst, dense[:, t, a * D:(a + 1) * D], ACT.Copy,
                                         scale=comb[:, slot, t, e:e + 1])
                ins.then_inc(exp_scaled.sem, 1)

            def experts_body(L, slot, m, n, l, r, p):
                if n is not None:
                    act.wait_ge(xt_made.sem, xt_made.at(2, n))
                    act.wait_ge(exp_made.sem, exp_made.at(2, n - 2))
                    act.activation(turned_parts[:, 1 - slot, 0], work[:, 0, :], ACT.Copy).then_inc(xt_ready.sem, 1)
                if m is not None:
                    expert(slot, m, 0, 0)
                    expert(slot, m, 0, 1)
                if n is not None:
                    high(2, n, q_made, qh_ready, qhl, 1, "bq", S)
                if m is not None:
                    expert(slot, m, 1, 0)
                if n is not None:
                    high(2, n, k_made, kh_ready, khl, 0, "bk", S)
                if m is not None:
                    expert(slot, m, 1, 1)
                    shifts_turned(2, m)
                for u in range(16):
                    if m is not None:
                        exponential(2, m, u)
                        if u in (3, 11):
                            expert(slot, m, 2 + u // 11, 1)
                    if n is not None and u == 2:
                        act.wait_ge(logits_ready.sem, logits_ready.at(2, n))
                        for t in range(QT):
                            act.activation(ge[:, t, :], lg[:, t, :], ACT.Exp, bias=nmx[:, t:t + 1],
                                           accum_out=gsum[:, t:t + 1]).then_inc(gexp_ready.sem, 1)
                    if n is not None and u == 14:
                        act.wait_ge(comb_t_made.sem, comb_t_made.at(2, n))
                        act.activation(comb_t[:], work[0:E, 1, 0:S], ACT.Copy).then_inc(comb_t_ready.sem, 1)
                if m is not None:
                    attended_turned(2, m)
                if n is not None:
                    act.wait_ge(ebias_made.sem, ebias_made.at(2, n))
                    act.wait_ge(exp_read.sem, exp_read.at(2, n - 1))
                    act.wait_ge(exp_summed.sem, exp_summed.at(2, n - 1))
                    act.activation(ebias, work[:, 1, :], ACT.Copy).then_inc(ebias_ready.sem, 1)

            def body(L, slot, m, n, l, r, p):
                (cross_body if L < 2 else experts_body)(L, slot, m, n, l, r, p)

            for L in range(3):
                steps(act, L, lambda slot, m, n, l, r, p, number: body(L, slot, m, n, l, r, p))
                if L < 2:
                    layer_end(act, L)

        @block.vector
        def _(dve):
            chain = Chain(dve, dve_chain)
            link = chain.link
            dve.memset(zeros[:], 0.0).then_inc(const_ready, 1)
            dve.memset(q_stack[:].bitcast(F32), 0.0).then_inc(zeroed, 1)
            dve.memset(k_stack[:].bitcast(F32), 0.0).then_inc(zeroed, 1)
            dve.memset(vx[:], 0.0).then_inc(zeroed, 1)
            dve.memset(shift_t[:].bitcast(F32), 0.0).then_inc(zeroed, 1)
            dve.wait_ge(zeroed, 4)
            dve.memset(vx[:, :, :, :, HD:HD + 1], 1.0).then_inc(const_ready, 1)
            dve.wait_ge(first_in, 16 * len(first))
            dve.tensor_copy(identb[:], ident[:]).then_inc(const_ready, 1)
            for n in ("bf", "bi"):
                dve.tensor_scalar(col[n][:], col[n][:], 0.5, None, ALU.mult).then_inc(halved, 1)
            dve.wait_ge(halved, 2)
            dve.tensor_copy(nmx[:], zeros[:, 0:QT]).then_inc(const_ready, 1)

            def split_rounds(L):
                for i, (of, (_, (high, low, n))) in enumerate(numbered):
                    if of != L:
                        continue
                    dve.wait_ge(stage_in[i % 2], loaded[i])
                    src = stage[i % 2][:, 0:n]
                    ins = dve.tensor_copy(high, src)
                    ins.then_inc(split_done, 1)
                    dve.wait_ge(split_done, i + 1)
                    if low is not None:
                        ins = dve.tensor_tensor(low, src, high.bitcast(F32), ALU.subtract)
                    else:
                        ins = dve.tensor_copy(nmx[:], zeros[:, 0:QT])
                    ins.then_inc(stage_used, 1)

            split_rounds(0)
            dve.wait_ge(gates_ready, 1 + KT)
            dve.tensor_copy(cell_parts[:, 0], cell[:]).then_inc(halved, 1)
            dve.wait_ge(halved, 3)
            dve.tensor_tensor(cell_parts[:, 1], cell[:], cell_parts[:, 0].bitcast(F32), ALU.subtract)\
                .then_inc(halved, 1)

            def spread(st, mean_var, var, src):
                ks = [link(dve.bn_stats(st[:, t, :], src[:, t, :])) for t in range(QT)]
                for t in range(QT):
                    dve.wait_ge(dve_chain, chain.at(ks[t]))
                    dve.sem_inc(passed, 1)
                    last = link(dve.bn_aggr(mean_var[:, t, :], st[:, t, :]))
                dve.wait_ge(dve_chain, chain.at(last))
                return dve.tensor_scalar(var[:], mean_var[:, :, 1], EPS, None, ALU.add)

            def normal(dst, src, mean_var, scale):
                for t in range(QT):
                    ins = dve.tensor_scalar(dst[:, t, :], src[:, t, :], mean_var[:, t, 0:1], scale[:, t:t + 1],
                                            ALU.subtract, ALU.mult)
                return ins

            def low(L, n, made, high, ready, part, bk, b, N):
                dve.wait_ge(high.sem, high.at(L, n))
                for k in range(KT):
                    dve.scalar_tensor_tensor(part[:, 1, k, 0:N], work[:, bk, k * S:k * S + N],
                                             col[f"{b}{L}"][:, k:k + 1], part[:, 0, k, 0:N].bitcast(F32),
                                             ALU.add, ALU.subtract).then_inc(ready.sem, 1)

            def queries_low(L, n):
                low(L, n, q_made, qh_ready, ql_ready, qhl, 1, "bq", S)

            def keys_low(L, n):
                low(L, n, k_made, kh_ready, kl_ready, khl, 0, "bk", KN[L])

            def values(L, slot, n):
                dve.wait_ge(v_made.sem, v_made.at(L, n))
                dve.wait_ge(pv_made.sem, pv_made.at(L, n - 2))
                for t in range(1 if L < 2 else 2):
                    ins = dve.tensor_tensor(
                        vx[0:KQ[L], slot, t, :, 0:HD],
                        work[0:KQ[L], 0, t * D:(t + 1) * D].rearrange("p (h d) -> p h d", h=H),
                        row[f"bv{L}"][0:KQ[L], :].rearrange("p (h d) -> p h d", h=H), ALU.add)
                ins.then_inc(v_ready.sem, 1)

            def maximum(L, m, u):
                heads, keys = (4, S2) if L < 2 else (2, S)
                t, j = divmod(u, H // heads)
                dve.wait_ge(tops_made.sem, tops_made.at(L, m, u + 1))
                dve.tensor_reduce(top[:, t, heads * j:heads * (j + 1)],
                                  score[:, u % 2, 0:heads * keys].rearrange("p (h k) -> p h k", h=heads),
                                  AX.X, ALU.max).then_inc(tops_read.sem, 1)

            def shift(L, m):
                dve.wait_ge(tops_read.sem, tops_read.at(L, m))
                if L == 0:
                    link(dve.tensor_scalar(top2[:], top[:], -1.0, CLIP, ALU.mult, ALU.min))
                    dve.wait_ge(dve_chain, chain.at())
                    link(dve.tensor_scalar(top2[:], top2[:], -CLIP, None, ALU.max))
                else:
                    link(dve.tensor_scalar(top2[:], top[:], -1.0, None, ALU.mult))
                dve.wait_ge(shift_t_made.sem, shift_t_made.at(L, m - 1))
                dve.wait_ge(dve_chain, chain.at())
                link(dve.tensor_copy(shift_hl[:, :, 0:H], top2[:]))
                dve.wait_ge(dve_chain, chain.at())
                dve.tensor_tensor(shift_hl[:, :, H:2 * H], top2[:], shift_hl[:, :, 0:H].bitcast(F32),
                                  ALU.subtract).then_inc(shift_ready.sem, 1)

            def clip(m, u):
                dve.wait_ge(raw_made.sem, raw_made.at(0, m, u + 1))
                dve.tensor_scalar(score[0:S2, u % 2, :], score[0:S2, u % 2, :], CLIP, -CLIP,
                                  ALU.min, ALU.max).then_inc(clipped.sem, 1)

            def group(m, u):
                dve.wait_ge(probs_ready.sem, probs_ready.at(1, m, u + 1))
                if u == 0:
                    dve.wait_ge(prob_loaded.sem, prob_loaded.at(1, m))
                if u >= NPR:
                    dve.wait_ge(pv_made.sem, pv_made.at(1, m, u - NPR + 1))
                dve.tensor_tensor(probs_g[0:S2, u % NPR, :].rearrange("p (a q) -> p a q", a=2),
                                  probs[0:S2, u % NPR, :].rearrange("p (a q) -> p a q", a=2),
                                  prob_k[0:S2, :].unsqueeze(1).to_broadcast([S2, 2, S]),
                                  ALU.mult).then_inc(probs_g_ready.sem, 1)

            def attended(L, l):
                for t in range(QT):
                    dve.wait_ge(att_made.sem, att_made.at(L, l, t + 1))
                    rows = dense[:, t, :].rearrange("p (h c) -> p h c", h=H)
                    link(dve.reciprocal(rec[:, t, :], rows[:, :, HD]))
                    dve.wait_ge(dve_chain, chain.at())
                    dve.tensor_tensor(att[:, t, :].rearrange("p (h d) -> p h d", h=H), rows[:, :, 0:HD],
                                      rec[:, t, :].unsqueeze(2).to_broadcast([P, H, HD]), ALU.mult)\
                        .then_inc(att_ready.sem, 1)

            def add_bias(L, l):
                dve.wait_ge(y_made.sem, y_made.at(L, l))
                dve.tensor_tensor(y2[:], work[:, 1, :].rearrange("p (t d) -> p t d", t=QT),
                                  row[f"bo{L}"][:].unsqueeze(1).to_broadcast([P, QT, D]), ALU.add)\
                    .then_inc(y_read.sem, 1)

            def add_rows(L, l):
                dve.wait_ge(y_read.sem, y_read.at(L, l))
                dve.wait_ge(res_loaded.sem, res_loaded.at(L, l))
                dve.wait_ge(y_stored.sem, y_stored.at(L, l - 1))
                dve.scalar_tensor_tensor(y[:], y2[:], tg[:, L:L + 1], x_res[:], ALU.mult, ALU.add)\
                    .then_inc(y_ready.sem, 1)
                if L == 0:
                    dve.wait_ge(y_ready.sem, y_ready.at(0, l))
                    spread(stats1, mv1, var_eps1, y).then_inc(var1_ready.sem, 1)

            def stats_of(L, p):
                if L == 1:
                    dve.wait_ge(x2_ready.sem, x2_ready.at(1, p))
                else:
                    dve.wait_ge(x_loaded.sem, x_loaded.at(L, p))
                spread(stats, mv, var_eps, x2 if L == 1 else x_in).then_inc(var_ready.sem, 1)

            def normalised(L, p):
                dve.wait_ge(rstd_ready.sem, rstd_ready.at(L, p))
                dve.wait_ge(xt_made.sem, xt_made.at(L, p - 1))
                normal(xn, x2 if L == 1 else x_in, mv, rstd).then_inc(xn_ready.sem, 1)

            def cross_body(L, slot, m, n, l, r, p):
                for u in range(8):
                    if m is not None:
                        maximum(L, m, u)
                    if u == 1 and r is not None:
                        dve.wait_ge(rstd1_ready.sem, rstd1_ready.at(0, r))
                        dve.wait_ge(xt1_made.sem, xt1_made.at(0, r - 1))
                        normal(xn1, y, mv1, rstd1).then_inc(xn1_ready.sem, 1)
                    if L == 0 and u == 3 and l is not None:
                        attended(0, l)
                    if u == 5 and n is not None:
                        queries_low(L, n)
                if m is not None:
                    shift(L, m)
                if n is not None:
                    keys_low(L, n)
                if r is not None:
                    dve.wait_ge(xt1_ready.sem, xt1_ready.at(0, r))
                    dve.tensor_tensor(xt1[:, 1], dense[:, 0, :].rearrange("p (k t) -> p k t", k=KT),
                                      xt1[:, 0].bitcast(F32), ALU.subtract).then_inc(xt1_low.sem, 1)
                if L == 1 and l is not None:
                    attended(1, l)
                if L == 1 and n is not None:
                    values(1, 1 - slot, n)
                for u in range(8):
                    if m is not None:
                        if L == 0:
                            clip(m, u)
                        else:
                            group(m, u)
                    if u == 1 and L == 0 and n is not None:
                        values(0, 1 - slot, n)
                    if u == 4 - L and p is not None:
                        stats_of(L, p)
                    if u == 6 + L and l is not None:
                        add_bias(L, l)
                    if u == 7 and p is not None:
                        normalised(L, p)
                if l is not None:
                    add_rows(L, l)

            def expert(slot, m, pair):
                dve.wait_ge(exp_made.sem, exp_made.at(2, m, 2 * pair + 1))
                dve.wait_ge(exp_summed.sem, exp_summed.at(2, m, 2))
                if pair == 3:
                    dve.wait_ge(exp_read.sem, exp_read.at(2, m, 1))
                for a in range(2):
                    e = 2 * pair + a
                    dst = acc[slot][a][:, 0, :]
                    ins = dve.scalar_tensor_tensor(dst, dense[:, 0, a * D:(a + 1) * D], comb[:, slot, 0, e:e + 1],
                                                   dst, ALU.mult, ALU.add)
                ins.then_inc(exp_read.sem, 1)

            def layer_output(slot, l):
                dve.wait_ge(exp_read.sem, exp_read.at(2, l))
                dve.wait_ge(exp_summed.sem, exp_summed.at(2, l))
                dve.wait_ge(att_ready.sem, att_ready.at(2, l))
                a, b = acc[slot]
                link(dve.tensor_tensor(a, a, b, ALU.add))
                dve.wait_ge(dve_chain, chain.at())
                link(dve.tensor_tensor(a, a, att[:], ALU.add))
                dve.wait_ge(dve_chain, chain.at())
                dve.wait_ge(res_loaded.sem, res_loaded.at(2, l))
                dve.wait_ge(y_stored.sem, y_stored.at(2, l - 1))
                dve.scalar_tensor_tensor(y[:], a, tg[:, 3:4], x_res[:], ALU.mult, ALU.add).then_inc(y_ready.sem, 1)

            def logits(n):
                dve.wait_ge(logits_made.sem, logits_made.at(2, n))
                link(dve.tensor_tensor(lg[:], work[:, 1, 0:QT * E].rearrange("p (t e) -> p t e", t=QT),
                                       b_gate[:].unsqueeze(1).to_broadcast([P, QT, E]), ALU.add))
                dve.wait_ge(dve_chain, chain.at())
                dve.tensor_reduce(nmx[:], lg[:], AX.X, ALU.max, negate=True).then_inc(logits_ready.sem, 1)

            def combine(slot, n):
                dve.wait_ge(gexp_ready.sem, gexp_ready.at(2, n))
                link(dve.reciprocal(grec[:], gsum[:]))
                mine = ge[:].unsqueeze(3).to_broadcast([P, QT, E, E])
                other = ge[:].unsqueeze(2).to_broadcast([P, QT, E, E])
                k = link(dve.tensor_tensor(cmp1[:], other, mine, ALU.is_equal))
                link(dve.tensor_tensor(cmp2[:], other, mine, ALU.is_gt))
                dve.wait_ge(dve_chain, chain.at(k))
                link(dve.tensor_tensor(cmp1[:], cmp1[:], earlier[:].unsqueeze(1).to_broadcast([P, QT, E, E]), ALU.mult))
                dve.wait_ge(dve_chain, chain.at())
                link(dve.tensor_tensor(cmp1[:], cmp1[:], cmp2[:], ALU.add))
                dve.wait_ge(dve_chain, chain.at())
                link(dve.tensor_reduce(rank[:], cmp1[:], AX.X, ALU.add))
                dve.wait_ge(dve_chain, chain.at())
                link(dve.scalar_tensor_tensor(comb[:, slot], rank[:], 2.0, ge[:], ALU.is_lt, ALU.mult))
                dve.wait_ge(dve_chain, chain.at())
                dve.tensor_tensor(comb[:, slot], comb[:, slot], grec[:].unsqueeze(2).to_broadcast([P, QT, E]),
                                  ALU.mult).then_inc(comb_ready.sem, 1)

            def experts_body(L, slot, m, n, l, r, p):
                other = 1 - slot
                for u in range(16):
                    if m is not None:
                        maximum(2, m, u)
                    if u == 3 and n is not None:
                        dve.wait_ge(xt_ready.sem, xt_ready.at(2, n))
                        dve.tensor_tensor(turned_parts[:, other, 1], work[:, 0, :].rearrange("p (k t) -> p k t", k=KT),
                                          turned_parts[:, other, 0].bitcast(F32), ALU.subtract).then_inc(xt_low.sem, 1)
                    if n is not None and u == 9:
                        queries_low(2, n)
                if m is not None:
                    shift(2, m)
                if n is not None:
                    keys_low(2, n)
                if l is not None:
                    attended(2, l)
                if n is not None:
                    values(2, other, n)
                if n is not None:
                    logits(n)
                if m is not None:
                    expert(slot, m, 2)
                if l is not None:
                    layer_output(other, l)
                if n is not None:
                    combine(other, n)
                if p is not None:
                    stats_of(2, p)
                    normalised(2, p)
                if m is not None:
                    expert(slot, m, 3)

            def body(L, slot, m, n, l, r, p, number):
                chain.step(number)
                (cross_body if L < 2 else experts_body)(L, slot, m, n, l, r, p)
                chain.close()

            for L in range(3):
                if L == 2:
                    split_rounds(2)
                steps(dve, L, lambda slot, m, n, l, r, p, number: body(L, slot, m, n, l, r, p, number))
                if L == 0:
                    dve.memset(k_stack[STACK:STACK + 2, :, :, 0, :].bitcast(F32), 1.0).then_inc(shift_rows_set, 1)
                    dve.memset(k_stack[STACK:SHIFTED, :, :, 1, :].bitcast(F32), 1.0).then_inc(shift_rows_set, 1)
                    dve.wait_ge(shift_rows_set, 2)
                    dve.memset(k_stack[STACK:STACK + 2, :, :, 1, :].bitcast(F32), 0.0).then_inc(shift_rows_set, 1)
                    dve.wait_ge(later_in, 16 * len(later))
                    dve.wait_ge(cell_final, 1)
                    dve.tensor_tensor(cu[:], work[:, 0, :].rearrange("p (t d) -> p t d", t=QT),
                                      row["bo_f"][:].unsqueeze(1).to_broadcast([P, QT, D]), ALU.add)\
                        .then_inc(cu_ready, 1)
                    dve.memset(vx[:, :, :, :, HD:HD + 1], 0.0).then_inc(cu_ready, 1)
                    dve.wait_ge(cu_ready, 2)
                if L == 1:
                    dve.memset(vx[:, :, :, :, HD:HD + 1], 1.0).then_inc(cu_ready, 1)
                    dve.wait_ge(cu_ready, 3)
                if L < 2:
                    layer_end(dve, L)

        @block.tensor
        def _(pe):
            pe.wait_ge(first_in, 16 * len(first))
            pe.wait_ge(const_ready, NREADY)

            def mm(dst, lhs, rhs, start=True, stop=True):
                return pe.matmul(dst, lhs, rhs, start=start, stop=stop, skip_group_check=True)

            def mm3(dst, lhs, rhs, start, stop):
                mm(dst, lhs[0], rhs[0], start=start, stop=False)
                mm(dst, lhs[0], rhs[1], start=False, stop=False)
                return mm(dst, lhs[1], rhs[0], start=False, stop=stop)

            def turn(dst, src):
                for t in range(QT):
                    for k in range(KT):
                        ins = pe.transpose(dst[:, k * S + t * P:k * S + (t + 1) * P], src[:, t, k * P:(k + 1) * P],
                                           ident[:])
                return ins

            def features(dst, weight, rhs, N):
                for o in range(KT):
                    for k in range(KT):
                        ins = mm(dst[:, o * S:o * S + N], weight[:, k, o * P:(o + 1) * P], rhs[:, k, 0:N],
                                 start=k == 0, stop=k == KT - 1)
                return ins

            def features3(dst, o, weights, rhs):
                n = len(weights) * KT
                for i in range(n):
                    wt, x, k = weights[i // KT], rhs[i // KT], i % KT
                    ins = mm3(dst[:, o * S:(o + 1) * S], [wt[:, part, k, o * P:(o + 1) * P] for part in range(2)],
                              [x[:, part, k, :] for part in range(2)], start=i == 0, stop=i == n - 1)
                return ins

            def rows(dst, lhs, weight, tiles=QT, M=P):
                for t in range(tiles):
                    for k in range(KT):
                        ins = mm(dst[0:M, t * D:(t + 1) * D], lhs[:, k, t * P:t * P + M], weight[:, k, :],
                                 start=k == 0, stop=k == KT - 1)
                return ins

            def rows3(dst, t, lhs, weight, N=D):
                for k in range(KT):
                    ins = mm3(dst[:, t * N:(t + 1) * N], [lhs[:, part, k, t * P:(t + 1) * P] for part in range(2)],
                              [weight[:, part, k, :] for part in range(2)], start=k == 0, stop=k == KT - 1)
                return ins

            def turn_rows(L, n):
                pe.wait_ge(xn_ready.sem, xn_ready.at(L, n))
                pe.wait_ge(v_ready.sem, v_ready.at(L, n - 1))
                turn(work[:, 0, :], xn).then_inc(xt_made.sem, 1)

            def queries(L, n):
                pe.wait_ge(ql_ready.sem, ql_ready.at(L, n - 1))
                pe.wait_ge(xt_ready.sem, xt_ready.at(L, n))
                pe.wait_ge(y_read.sem, y_read.at(L, n - 3))
                features(work[:, 1, :], w[f"wq{L}"], xt, S).then_inc(q_made.sem, 1)

            def keys(L, n):
                pe.wait_ge(xt_ready.sem, xt_ready.at(L, n))
                pe.wait_ge(ctx_loaded.sem, ctx_loaded.at(L, n))
                features(work[:, 0, :], w[f"wk{L}"], ctx_t, S2).then_inc(k_made.sem, 1)

            def queries_half(n, xp, o):
                if o == 0:
                    pe.wait_ge(ql_ready.sem, ql_ready.at(2, n - 1))
                    pe.wait_ge(ebias_ready.sem, ebias_ready.at(2, n - 1))
                    pe.wait_ge(xt_low.sem, xt_low.at(2, n))
                ins = features3(work[:, 1, :], o, [ws["wq2"]], [xp])
                if o == KT - 1:
                    ins.then_inc(q_made.sem, 1)

            def keys_half(n, xp, o):
                if o == 0:
                    pe.wait_ge(xt_low.sem, xt_low.at(2, n))
                ins = features3(work[:, 0, :], o, [ws["wk2"]], [xp])
                if o == KT - 1:
                    ins.then_inc(k_made.sem, 1)

            def vals(L, n, xp=None):
                pe.wait_ge(kl_ready.sem, kl_ready.at(L, n))
                if L < 2:
                    ins = rows(work[:, 0, :], ctx_t, w[f"wv{L}"], tiles=1, M=S2)
                else:
                    for t in range(QT):
                        ins = rows3(work[:, 0, :], t, xp, ws["wv2"])
                ins.then_inc(v_made.sem, 1)

            def tops(L, slot, m, u):
                if u == 0:
                    pe.wait_ge(stack_loaded.sem, stack_loaded.at(L, m))
                    if L < 2:
                        pe.wait_ge(mask_q_ready.sem, mask_q_ready.at(L, m))
                if u < 2:
                    pe.wait_ge(probs_ready.sem, probs_ready.at(L, m - 1, NU[L] - 1 + u))
                else:
                    pe.wait_ge(tops_read.sem, tops_read.at(L, m, u - 1))
                if L < 2:
                    t, jj = divmod(u, 4)
                    mm(score[:, u % 2, 0:4 * S2].rearrange("p (h k) -> p h k", h=4), identb[:],
                       mask_q[:, t, :].unsqueeze(1).to_broadcast([P, 4, S2]), start=True, stop=False)
                    for a in range(2):
                        j = 2 * jj + a
                        ins = mm(score[:, u % 2, a * 2 * S2:(a + 1) * 2 * S2].rearrange("p (h k) -> p h k", h=2),
                                 q_stack[0:STACK, slot, j, t * P:(t + 1) * P], k_stack[0:STACK, slot, j, :, 0:S2],
                                 start=False, stop=True)
                else:
                    t, j = divmod(u, PAIRS)
                    ins = mm(score[:, u % 2, :], q_stack[0:STACK, slot, j, t * P:(t + 1) * P],
                             k_stack[0:STACK, slot, j].rearrange("p a k -> p (a k)"))
                ins.then_inc(tops_made.sem, 1)

            def shifts(L, m, n):
                pe.wait_ge(shift_ready.sem, shift_ready.at(L, m))
                if n is not None:
                    pe.wait_ge(ql_ready.sem, ql_ready.at(L, n))
                elif L < 2:
                    pe.wait_ge(y_read.sem, y_read.at(L, m - 2))
                else:
                    pe.wait_ge(ebias_ready.sem, ebias_ready.at(2, m))
                for t in range(QT):
                    ins = pe.transpose(work[0:2 * H, 1, t * P:(t + 1) * P], shift_hl[:, t, :].bitcast(F32), ident[:])
                ins.then_inc(shift_t_made.sem, 1)

            def unit(L, u):
                return (u, 0) if L < 2 else (2 * (u // 4) + u % 2, u // 2 % 2)

            def stacked(L, slot, u):
                kq = KQ[L]
                j, kt = unit(L, u)
                depth = SHIFTED if L == 2 else STACK
                for par in range(2):
                    ins = mm(score[0:kq, u % 2, par * S:(par + 1) * S],
                             k_stack[0:depth, slot, j, par, kt * P:kt * P + kq], q_stack[0:depth, slot, j, :],
                             start=par == 0, stop=L == 2)
                return ins

            def masked(u):
                return mm(score[0:S2, u % 2, :].rearrange("p (a q) -> p a q", a=2), identb[0:S2, 0:S2],
                          mask_k[0:S2, :].unsqueeze(1).to_broadcast([S2, 2, S]), start=False, stop=False)

            def shifted(u):
                j, _ = unit(0, u)
                for par in range(2):
                    ins = mm(score[0:S2, u % 2, par * S:(par + 1) * S], sel[:, 2 * j + par, 0:S2], shift_t[:],
                             start=False, stop=par == 1)
                return ins

            def products(L, slot, m, u):
                kq = KQ[L]
                _, kt = unit(L, u)
                if u == 0:
                    pe.wait_ge(v_ready.sem, v_ready.at(L, m))
                pe.wait_ge(probs_ready.sem, probs_ready.at(L, m, u + 2))
                if L == 1:
                    pe.wait_ge(probs_g_ready.sem, probs_g_ready.at(L, m, u + 2))
                heads = []
                for v in (u, u + 1):
                    for par in range(2):
                        h = 2 * unit(L, v)[0] + par
                        g = h // 4
                        heads.append((h, o_ps[32 * (h % 4):32 * (h % 4) + VW, g // 2, (g % 2) * S:(g % 2 + 1) * S],
                                      slice(par * S, (par + 1) * S), v % NPR))
                for h, dst, part, at in heads:
                    p = probs_g if L == 1 else probs
                    ins = mm(dst, vx[0:kq, slot, kt, h, :], p[0:kq, at, part], start=kt == 0, stop=L == 0 or kt == 1)
                if L == 1:
                    for h, dst, part, at in heads:
                        ins = mm(dst, ones_col[0:kq, :], probs[0:kq, at, part], start=False, stop=True)
                ins.then_inc(pv_made.sem, 2)

            def probabilities(L, slot, m, between):
                if m is None:
                    for u in range(NU[L] + 1):
                        between(u)
                    return
                if L < 2:
                    pe.wait_ge(shift_t_ready.sem, shift_t_ready.at(L, m))
                else:
                    pe.wait_ge(shift_moved.sem, shift_moved.at(2, m))
                pe.wait_ge(tops_read.sem, tops_read.at(L, m))
                if L < 2:
                    pe.wait_ge(mask_k_ready.sem, mask_k_ready.at(L, m))
                pe.wait_ge(att_t_ready.sem, att_t_ready.at(L, m - 1))
                for u in range(NU[L]):
                    if L == 0:
                        pe.wait_ge(clipped.sem, clipped.at(0, m, u + 1))
                        masked(u)
                        shifted(u).then_inc(scores_made.sem, 1)
                        if 1 <= u < NU[0] - 1:
                            pe.wait_ge(probs_ready.sem, probs_ready.at(0, m, u))
                            stacked(0, slot, u + 1).then_inc(raw_made.sem, 1)
                    else:
                        if u >= 2:
                            pe.wait_ge(probs_ready.sem, probs_ready.at(L, m, u - 1))
                        ins = stacked(L, slot, u)
                        if L == 1:
                            masked(u)
                            ins = shifted(u)
                        ins.then_inc(scores_made.sem, 1)
                    between(u)
                    if u % 2 == 1 and u > 1:
                        products(L, slot, m, u - 3)
                between(NU[L])
                products(L, slot, m, NU[L] - 2)

            def turn_attended(L, l, m=None):
                pe.wait_ge(att_t_ready.sem, att_t_ready.at(L, l))
                pe.wait_ge(att_ready.sem, att_ready.at(L, l - 1))
                if L == 0:
                    pe.wait_ge(hx_ready.sem, hx_ready.at(0, l - 2))
                if L == 2:
                    if m is not None:
                        pe.wait_ge(exp_scaled.sem, exp_scaled.at(2, m, 4))
                    else:
                        pe.wait_ge(exp_read.sem, exp_read.at(2, l))
                        pe.wait_ge(exp_scaled.sem, exp_scaled.at(2, l))
                for t in range(QT):
                    for g in range(4):
                        ins = pe.transpose(dense[:, t, g * P:(g + 1) * P], att_t[:, g, t * P:(t + 1) * P], ident[:])
                    ins.then_inc(att_made.sem, 1)

            def turn_back(L, l, m, n):
                pe.wait_ge(att_ready.sem, att_ready.at(L, l))
                pe.wait_ge(y_read.sem, y_read.at(L, l - 1))
                if n is not None:
                    pe.wait_ge(ql_ready.sem, ql_ready.at(L, n))
                if m is not None:
                    pe.wait_ge(shift_t_ready.sem, shift_t_ready.at(L, m))
                turn(work[:, 1, :], att).then_inc(att_n_made.sem, 1)

            def att_project_half(L, l, t):
                if t == 0:
                    pe.wait_ge(att_n_ready.sem, att_n_ready.at(L, l))
                for k in range(KT):
                    ins = mm(work[:, 1, t * D:(t + 1) * D], att_n[:, k, t * P:(t + 1) * P], w[f"wo{L}"][:, k, :],
                             start=k == 0, stop=k == KT - 1)
                if t == QT - 1:
                    ins.then_inc(y_made.sem, 1)

            def turn_recurrent(r, l):
                pe.wait_ge(xn1_ready.sem, xn1_ready.at(0, r))
                pe.wait_ge(hx_ready.sem, hx_ready.at(0, r - 1))
                if l is not None:
                    pe.wait_ge(att_ready.sem, att_ready.at(0, l))
                turn(dense[:, 0, :], xn1).then_inc(xt1_made.sem, 1)

            def gate_half(r, l, g, o):
                bk, wn, un = ((1, "wf", "uf"), (0, "wi", "ui"), (1, "wc", "uc"))[g]
                if o == 0:
                    if g == 0:
                        if l is not None:
                            pe.wait_ge(att_ready.sem, att_ready.at(0, l))
                        pe.wait_ge(cell_ready.sem, cell_ready.at(0, r - 1))
                    if g < 2:
                        pe.wait_ge(xt1_low.sem, xt1_low.at(0, r))
                    else:
                        pe.wait_ge(gate_ready.sem, gate_ready.at(0, r, 1))
                ins = features3(dense[:, bk, :], o, [ws[wn], ws[un]], [xt1, cell_parts])
                if o == KT - 1:
                    ins.then_inc(gate_made.sem, 1)

            def hidden_half(r, t):
                if t == 0:
                    pe.wait_ge(gate_ready.sem, gate_ready.at(0, r, 2))
                ins = rows3(dense[:, 0, :], t, xt1, ws["wo_f"])
                if t == QT - 1:
                    ins.then_inc(hx_made.sem, 1)

            def cross_body(L, slot, m, n, l, r, p):
                for u in range(8):
                    if m is not None:
                        tops(L, slot, m, u)
                    if u == 1 and n is not None:
                        turn_rows(L, n)
                    if L == 0 and u == 3 and l is not None:
                        turn_attended(0, l)
                    if u == 4 and n is not None:
                        queries(L, n)
                if n is not None:
                    keys(L, n)
                if r is not None:
                    turn_recurrent(r, l)
                if L == 1 and l is not None:
                    turn_attended(1, l)
                if m is not None:
                    shifts(L, m, n)
                if L == 0 and m is not None:
                    pe.wait_ge(tops_read.sem, tops_read.at(0, m))
                    stacked(0, slot, 0).then_inc(raw_made.sem, 1)
                    stacked(0, slot, 1).then_inc(raw_made.sem, 1)
                if n is not None:
                    vals(L, n)
                if r is not None:
                    gate_half(r, l, 0, 0)

                def between(u):
                    if r is not None and u < 5:
                        gate_half(r, l, (u + 1) // 2, (u + 1) % 2)
                    if r is not None and u in (6, 8):
                        hidden_half(r, u // 2 - 3)
                    if l is not None and u == 1:
                        turn_back(L, l, m, n)
                    if l is not None and u in (3, 5):
                        att_project_half(L, l, u // 2 - 1)

                probabilities(L, slot, m, between)

            def expert(slot, m, l, u, halves=(0, 1)):
                pair, t = divmod(u, 2)
                xp = turned_parts[:, slot]
                for k in halves:
                    if k == 0:
                        if pair == 0 and t == 0:
                            pe.wait_ge(exp_read.sem, exp_read.at(2, m - 1))
                        elif pair == 0:
                            pe.wait_ge(exp_scaled.sem, exp_scaled.at(2, m - 1))
                        elif pair == 3 and t == 0:
                            pe.wait_ge(exp_read.sem, exp_read.at(2, m, 1))
                        elif pair == 3:
                            pe.wait_ge(exp_scaled.sem, exp_scaled.at(2, m, 5))
                        else:
                            pe.wait_ge(exp_scaled.sem, exp_scaled.at(2, m, u - 1))
                        if pair == 2 and l is not None:
                            pe.wait_ge(att_ready.sem, att_ready.at(2, l, t + 1))
                    ins = mm3(dense[:, t, :], [xp[:, part, k, t * P:(t + 1) * P] for part in range(2)],
                              [w_exp[:, part, k, 2 * pair:2 * pair + 2, :].rearrange("p e d -> p (e d)")
                               for part in range(2)], start=k == 0, stop=k == KT - 1)
                    if k == KT - 1:
                        ins.then_inc(exp_made.sem, 1)

            def experts_body(L, slot, m, n, l, r, p):
                xp = turned_parts[:, 1 - slot]
                for u in range(16):
                    if m is not None:
                        tops(2, slot, m, u)
                    if u == 1 and n is not None:
                        turn_rows(2, n)
                    if m is not None and u in (2, 3, 4, 5):
                        expert(slot, m, l, u // 2 - 1, halves=(u % 2,))
                    if n is not None and u in (6, 7):
                        queries_half(n, xp, u % 2)
                    if m is not None and u in (8, 9):
                        expert(slot, m, l, 2, halves=(u % 2,))
                    if n is not None and u in (11, 12):
                        keys_half(n, xp, u - 11)
                if m is not None:
                    expert(slot, m, l, 3)
                    shifts(2, m, n)
                if l is not None:
                    turn_attended(2, l, m)
                if n is not None:
                    vals(2, n, xp)
                if n is not None:
                    if m is not None:
                        pe.wait_ge(shift_t_ready.sem, shift_t_ready.at(2, m))
                    pe.wait_ge(ql_ready.sem, ql_ready.at(2, n))
                    for t in range(QT):
                        ins = rows3(work[:, 1, :], t, xp, ws["w_gate"], N=E)
                    ins.then_inc(logits_made.sem, 1)
                if m is not None:
                    expert(slot, m, l, 4)

                def between(u):
                    halves = (0, 2, 4, 6, 8, 10)
                    if m is not None and u in halves:
                        expert(slot, m, l, 5 + halves.index(u) // 2, halves=(halves.index(u) % 2,))
                    if n is not None and u == 12:
                        pe.wait_ge(comb_ready.sem, comb_ready.at(2, n))
                        for t in range(QT):
                            ins = pe.transpose(work[0:E, 1, t * P:(t + 1) * P], comb[:, 1 - slot, t, :], ident[:])
                        ins.then_inc(comb_t_made.sem, 1)
                    if n is not None and u == 16:
                        pe.wait_ge(comb_t_ready.sem, comb_t_ready.at(2, n))
                        for t in range(QT):
                            ins = mm(work[:, 1, t * D:(t + 1) * D], comb_t[:, t * P:(t + 1) * P], b_exp[:])
                        ins.then_inc(ebias_made.sem, 1)

                probabilities(2, slot, m, between)

            def body(L, slot, m, n, l, r, p):
                (cross_body if L < 2 else experts_body)(L, slot, m, n, l, r, p)

            for L in range(3):
                if L == 0:
                    pe.wait_ge(stage_used, len(rounds[0]))
                    pe.wait_ge(halved, 4)
                if L == 2:
                    pe.wait_ge(stage_used, len(numbered))
                steps(pe, L, lambda slot, m, n, l, r, p, number: body(L, slot, m, n, l, r, p))
                if L == 0:
                    pe.wait_ge(later_in, 16 * len(later))
                    pe.wait_ge(cell_ready.sem, cell_ready.at(0, B - 1))
                    pe.wait_ge(v_ready.sem, v_ready.at(0, B - 1))
                    rows(work[:, 0, :], cell, w["uo_f"]).then_inc(cell_final, 1)
                if L < 2:
                    layer_end(pe, L)


def _layout(i):
    c = np.ascontiguousarray
    a = {k: np.asarray(v) for k, v in i.items()}
    z = {"x": a["x"], "ctx_t": c(a["ctx_1024"].transpose(0, 2, 1)),
         "mask0": c(a["mask_Bx1xSxS2_ik1"][:, 0]), "mask0_t": c(a["mask_Bx1xSxS2_ik1"][:, 0].transpose(0, 2, 1)),
         "mask1": a["mask_BxSxS2_ik1"], "mask1_t": c(a["mask_BxSxS2_ik1"].transpose(0, 2, 1)),
         "prob_t": c(a["fside_BxSxS2_0"].transpose(0, 2, 1)), "g_xattn": a["g_xattn"], "g_ffn": a["g_ffn"]}
    for n in "qkvo":
        z[f"w{n}0"] = c(a[f"L0_xattn_w{n}"].T)
        z[f"b{n}0"] = a[f"L0_xattn_b{n}"]
        z[f"w{n}1"] = a[f"L1_xattn_w{n}_k"]
        z[f"b{n}1"] = a[f"L1_xattn_w{n}_b"]
    for s, n in enumerate("qkv"):
        z[f"w{n}2"] = c(a["L1_ffn_W_qkv"][:, s * D:(s + 1) * D])
        z[f"b{n}2"] = c(a["L1_ffn_b_qkv"][s * D:(s + 1) * D])
    for n in "fic":
        z[f"w{n}"], z[f"u{n}"], z[f"b{n}"] = c(a[f"L0_ffn_w{n}"].T), c(a[f"L0_ffn_u{n}"].T), a[f"L0_ffn_b{n}"]
    z["wo_f"], z["uo_f"], z["bo_f"] = c(a["L0_ffn_wo"].T), c(a["L0_ffn_uo"].T), a["L0_ffn_bo"]
    z["in_c"] = a["L0_ffn_in_c"]
    z["w_gate"], z["b_gate"] = a["L1_ffn_W_gate"], a["L1_ffn_b_gate"]
    z["w_exp"], z["b_exp"] = a["L1_ffn_W_experts"], a["L1_ffn_b_experts"]
    z["ident"] = np.eye(P, dtype=np.float32)
    z["sel"] = np.zeros((P, H * P), np.float32)
    z["sel"][0:2 * H] = np.repeat(np.tile(np.eye(H, dtype=np.float32), (2, 1)), P, axis=1)
    z["earlier"] = np.tril(np.ones((E, E), np.float32), -1).reshape(-1)
    for n in ("bq0", "bk0", "bq1", "bk1", "bq2", "bk2", "bf", "bi", "bc", "in_c"):
        z[n] = z[n].reshape(KT, P).T
    return {k: c(v) for k, v in z.items()}


def kernel(**inputs):
    import concourse.bacc as _bacc
    from concourse.bass_utils import run_bass_kernel_spmd as _run

    arrays = _layout(inputs)
    batches = arrays["x"].shape[0]
    nc = _bacc.Bacc("TRN2", target_bir_lowering=False, num_devices=1)
    io = {n: nc.dram_tensor("in_" + n, a.shape, mybir.dt.from_np(a.dtype), kind="ExternalInput").ap()
          for n, a in arrays.items()}
    out = nc.dram_tensor("out_x", arrays["x"].shape, F32, kind="ExternalOutput").ap()
    flamingo_block(nc, io, out, batches)
    r = _run(nc, [{"in_" + n: a for n, a in arrays.items()}], core_ids=[0])
    return r.results[0]["out_x"]
```
